# Optimizing a Trainium2 kernel written in Bass

```python
import numpy as np
import jax
import jax.numpy as jnp

def _softmax(x, axis=-1):
    return jax.nn.softmax(x, axis=axis)

def _gelu(x):
    return jax.nn.gelu(x, approximate=True)

def _silu(x):
    return jax.nn.silu(x)

def _sigmoid(x):
    return jax.nn.sigmoid(x)

def _layernorm(x, axis=-1, eps=1e-05):
    m = jnp.mean(x, axis=axis, keepdims=True)
    v = jnp.var(x, axis=axis, keepdims=True)
    return (x - m) / jnp.sqrt(v + eps)

def _scatter_add(tgt, idx, src, axis=0):
    return tgt.at[idx].add(src)

def _segment_sum(src, seg, n):
    return jax.ops.segment_sum(src, seg, n)
kernel_name = 'mk_macaron_d1_jaxref_r8_037da5'

def setup_inputs(seed: int=0):
    np.random.seed(seed)
    _w = jnp.asarray

    def _L0_attn_setup():
        import jax, jax.numpy as jnp
        import numpy as np
        B, T = (4, 256)
        D_MODEL = 128
        QK_DIM = 128
        V_DIM = 256
        N_HEADS = 8
        SCALE_BASE = 512.0
        GN_EPS = 1e-05

        def _xpos_tables(seq_len, offset=0):
            dim_half = QK_DIM // 2
            base_scale = (jnp.arange(0, QK_DIM, 2, dtype=jnp.float32) + 0.4 * QK_DIM) / (1.4 * QK_DIM)
            pos = jnp.arange(0, seq_len + offset, dtype=jnp.float32)
            scale = base_scale[None, :] ** (pos[:, None] / SCALE_BASE)
            inv_freq = 1.0 / 10000.0 ** (jnp.arange(dim_half, dtype=jnp.float32) / dim_half)
            sinusoid = pos[:, None] * inv_freq[None, :]
            return (scale[-seq_len:], jnp.sin(sinusoid)[-seq_len:], jnp.cos(sinusoid)[-seq_len:])

        def _rotate_every_two(x):
            x1, x2 = (x[..., ::2], x[..., 1::2])
            return jnp.stack((-x2, x1), axis=-1).reshape(x.shape)

        def _apply_rotary(x, sin, cos, scale):
            sin_s = jnp.repeat(sin * scale, 2, axis=-1)
            cos_s = jnp.repeat(cos * scale, 2, axis=-1)
            return x * cos_s + _rotate_every_two(x) * sin_s

        def _reference_tuple_inner(hidden_states, W_qkv, W_g, W_proj, decay):
            b, t, _ = hidden_states.shape
            qkv = hidden_states @ W_qkv
            q, k, v = jnp.split(qkv, [QK_DIM, 2 * QK_DIM], axis=-1)
            scale, sin, cos = _xpos_tables(t)
            q = _apply_rotary(q, sin, cos, scale)
            k = _apply_rotary(k, sin, cos, 1.0 / scale)
            split = lambda x: x.reshape(b, t, N_HEADS, -1).transpose(0, 2, 1, 3)
            q, k, v = (split(q), split(k), split(v))
            dk = QK_DIM // N_HEADS
            n = jnp.arange(t)
            exponent = n[:, None] - n[None, :]
            causal = exponent >= 0
            exp_c = jnp.where(causal, exponent, 0).astype(jnp.float32)
            decay_mask = jnp.where(causal[None], decay[:, None, None] ** exp_c[None], 0.0)
            retention = jnp.einsum('bhtd,bhsd->bhts', q, k) * dk ** (-0.5)
            retention = retention * decay_mask[None]
            out = jnp.einsum('bhts,bhsv->bhtv', retention, v)
            w_last = decay_mask[:, -1, :]
            curr_kv = jnp.einsum('ht,bhtq,bhtv->bhqv', w_last, k, v)
            ret = out.transpose(0, 2, 1, 3).reshape(b, t, V_DIM)
            g = ret.reshape(b * t, N_HEADS, V_DIM // N_HEADS)
            mu = g.mean(-1, keepdims=True)
            var = ((g - mu) ** 2).mean(-1, keepdims=True)
            normed = ((g - mu) * jax.lax.rsqrt(var + GN_EPS)).reshape(b, t, V_DIM)
            gate = jax.nn.silu(hidden_states @ W_g)
            proj_out = gate * normed @ W_proj
            return (proj_out, curr_kv)
        key = jax.random.key(seed)
        k0, k1, k2, k3 = jax.random.split(key, 4)
        hidden_states = jax.random.normal(k0, (B, T, D_MODEL), dtype=jnp.float32)
        W_qkv = jax.random.normal(k1, (D_MODEL, 2 * QK_DIM + V_DIM), dtype=jnp.float32) / np.sqrt(D_MODEL)
        W_g = jax.random.normal(k2, (D_MODEL, V_DIM), dtype=jnp.float32) / np.sqrt(D_MODEL)
        W_proj = jax.random.normal(k3, (V_DIM, D_MODEL), dtype=jnp.float32) / np.sqrt(V_DIM)
        s, e = (np.log(1 / 32), np.log(1 / 64))
        decay = jnp.asarray(1.0 - np.exp(np.linspace(s, e, N_HEADS)), dtype=jnp.float32)
        return {'hidden_states': hidden_states, 'W_qkv': W_qkv, 'W_g': W_g, 'W_proj': W_proj, 'decay': decay}
    _L0_attn_in = _L0_attn_setup()

    def _L0_ffn_setup():
        import jax, jax.numpy as jnp
        import numpy as np
        D_MODEL = 128
        N_HEAD = 16
        HEAD_DIM = D_MODEL // N_HEAD
        D_FF = 512
        N_EXPERTS = 4
        EPS = 1e-05

        def _layer_norm(x, gamma, beta):
            mu = jnp.mean(x, axis=-1, keepdims=True)
            var = jnp.mean((x - mu) ** 2, axis=-1, keepdims=True)
            return (x - mu) / jnp.sqrt(var + EPS) * gamma + beta
        key = jax.random.key(seed)
        ks = jax.random.split(key, 20)
        f32 = jnp.float32
        sc = 1.0 / np.sqrt(D_MODEL)
        scf = 1.0 / np.sqrt(D_FF)
        return {'src': jax.random.normal(ks[0], (4, 64, D_MODEL), f32), 'Wq': jax.random.normal(ks[1], (D_MODEL, D_MODEL), f32) * sc, 'bq': jnp.zeros((D_MODEL,), f32), 'Wk': jax.random.normal(ks[2], (D_MODEL, D_MODEL), f32) * sc, 'bk': jnp.zeros((D_MODEL,), f32), 'Wv': jax.random.normal(ks[3], (D_MODEL, D_MODEL), f32) * sc, 'bv': jnp.zeros((D_MODEL,), f32), 'Wo': jax.random.normal(ks[4], (D_MODEL, D_MODEL), f32) * sc, 'bo': jnp.zeros((D_MODEL,), f32), 'router_w': jax.random.normal(ks[5], (D_MODEL, 1), f32) * 0.05, 'router_b': jnp.zeros((1,), f32), 'W1': jax.random.normal(ks[6], (N_EXPERTS, D_MODEL, D_FF), f32) * sc, 'b1': jnp.zeros((N_EXPERTS, D_FF), f32), 'W2': jax.random.normal(ks[7], (N_EXPERTS, D_FF, D_MODEL), f32) * scf, 'b2': jnp.zeros((N_EXPERTS, D_MODEL), f32), 'ln1_g': jnp.ones((D_MODEL,), f32), 'ln1_b': jnp.zeros((D_MODEL,), f32), 'ln2_g': jnp.ones((D_MODEL,), f32), 'ln2_b': jnp.zeros((D_MODEL,), f32)}
    _L0_ffn_in = _L0_ffn_setup()
    _d = {'L0_attn_hidden_states': _L0_attn_in['hidden_states'], 'L0_attn_W_qkv': _L0_attn_in['W_qkv'], 'L0_attn_W_g': _L0_attn_in['W_g'], 'L0_attn_W_proj': _L0_attn_in['W_proj'], 'L0_attn_decay': _L0_attn_in['decay'], 'L0_ffn_Wq': _L0_ffn_in['Wq'], 'L0_ffn_bq': _L0_ffn_in['bq'], 'L0_ffn_Wk': _L0_ffn_in['Wk'], 'L0_ffn_bk': _L0_ffn_in['bk'], 'L0_ffn_Wv': _L0_ffn_in['Wv'], 'L0_ffn_bv': _L0_ffn_in['bv'], 'L0_ffn_Wo': _L0_ffn_in['Wo'], 'L0_ffn_bo': _L0_ffn_in['bo'], 'L0_ffn_router_w': _L0_ffn_in['router_w'], 'L0_ffn_router_b': _L0_ffn_in['router_b'], 'L0_ffn_W1': _L0_ffn_in['W1'], 'L0_ffn_b1': _L0_ffn_in['b1'], 'L0_ffn_W2': _L0_ffn_in['W2'], 'L0_ffn_b2': _L0_ffn_in['b2'], 'L0_ffn_ln1_g': _L0_ffn_in['ln1_g'], 'L0_ffn_ln1_b': _L0_ffn_in['ln1_b'], 'L0_ffn_ln2_g': _L0_ffn_in['ln2_g'], 'L0_ffn_ln2_b': _L0_ffn_in['ln2_b']}
    _x0 = _d['L0_attn_hidden_states']
    _d['L0_attn_hidden_states'] = jax.random.normal(jax.random.fold_in(jax.random.key(seed), 1), (16, 256, 128), dtype=_x0.dtype)
    del _x0
    return _d

def reference(L0_attn_hidden_states, L0_attn_W_qkv, L0_attn_W_g, L0_attn_W_proj, L0_attn_decay, L0_ffn_Wq, L0_ffn_bq, L0_ffn_Wk, L0_ffn_bk, L0_ffn_Wv, L0_ffn_bv, L0_ffn_Wo, L0_ffn_bo, L0_ffn_router_w, L0_ffn_router_b, L0_ffn_W1, L0_ffn_b1, L0_ffn_W2, L0_ffn_b2, L0_ffn_ln1_g, L0_ffn_ln1_b, L0_ffn_ln2_g, L0_ffn_ln2_b):

    def _L0_attn_ref(hidden_states, W_qkv, W_g, W_proj, decay):
        import jax, jax.numpy as jnp
        import numpy as np
        B, T = (4, 256)
        D_MODEL = 128
        QK_DIM = 128
        V_DIM = 256
        N_HEADS = 8
        SCALE_BASE = 512.0
        GN_EPS = 1e-05

        def _xpos_tables(seq_len, offset=0):
            dim_half = QK_DIM // 2
            base_scale = (jnp.arange(0, QK_DIM, 2, dtype=jnp.float32) + 0.4 * QK_DIM) / (1.4 * QK_DIM)
            pos = jnp.arange(0, seq_len + offset, dtype=jnp.float32)
            scale = base_scale[None, :] ** (pos[:, None] / SCALE_BASE)
            inv_freq = 1.0 / 10000.0 ** (jnp.arange(dim_half, dtype=jnp.float32) / dim_half)
            sinusoid = pos[:, None] * inv_freq[None, :]
            return (scale[-seq_len:], jnp.sin(sinusoid)[-seq_len:], jnp.cos(sinusoid)[-seq_len:])

        def _rotate_every_two(x):
            x1, x2 = (x[..., ::2], x[..., 1::2])
            return jnp.stack((-x2, x1), axis=-1).reshape(x.shape)

        def _apply_rotary(x, sin, cos, scale):
            sin_s = jnp.repeat(sin * scale, 2, axis=-1)
            cos_s = jnp.repeat(cos * scale, 2, axis=-1)
            return x * cos_s + _rotate_every_two(x) * sin_s

        def _reference_tuple_inner(hidden_states, W_qkv, W_g, W_proj, decay):
            b, t, _ = hidden_states.shape
            qkv = hidden_states @ W_qkv
            q, k, v = jnp.split(qkv, [QK_DIM, 2 * QK_DIM], axis=-1)
            scale, sin, cos = _xpos_tables(t)
            q = _apply_rotary(q, sin, cos, scale)
            k = _apply_rotary(k, sin, cos, 1.0 / scale)
            split = lambda x: x.reshape(b, t, N_HEADS, -1).transpose(0, 2, 1, 3)
            q, k, v = (split(q), split(k), split(v))
            dk = QK_DIM // N_HEADS
            n = jnp.arange(t)
            exponent = n[:, None] - n[None, :]
            causal = exponent >= 0
            exp_c = jnp.where(causal, exponent, 0).astype(jnp.float32)
            decay_mask = jnp.where(causal[None], decay[:, None, None] ** exp_c[None], 0.0)
            retention = jnp.einsum('bhtd,bhsd->bhts', q, k) * dk ** (-0.5)
            retention = retention * decay_mask[None]
            out = jnp.einsum('bhts,bhsv->bhtv', retention, v)
            w_last = decay_mask[:, -1, :]
            curr_kv = jnp.einsum('ht,bhtq,bhtv->bhqv', w_last, k, v)
            ret = out.transpose(0, 2, 1, 3).reshape(b, t, V_DIM)
            g = ret.reshape(b * t, N_HEADS, V_DIM // N_HEADS)
            mu = g.mean(-1, keepdims=True)
            var = ((g - mu) ** 2).mean(-1, keepdims=True)
            normed = ((g - mu) * jax.lax.rsqrt(var + GN_EPS)).reshape(b, t, V_DIM)
            gate = jax.nn.silu(hidden_states @ W_g)
            proj_out = gate * normed @ W_proj
            return (proj_out, curr_kv)
        return _reference_tuple_inner(hidden_states, W_qkv, W_g, W_proj, decay)[0]

    def _L0_ffn_ref(src, Wq, bq, Wk, bk, Wv, bv, Wo, bo, router_w, router_b, W1, b1, W2, b2, ln1_g, ln1_b, ln2_g, ln2_b):
        import jax, jax.numpy as jnp
        import numpy as np
        D_MODEL = 128
        N_HEAD = 16
        HEAD_DIM = D_MODEL // N_HEAD
        D_FF = 512
        N_EXPERTS = 4
        EPS = 1e-05

        def _layer_norm(x, gamma, beta):
            mu = jnp.mean(x, axis=-1, keepdims=True)
            var = jnp.mean((x - mu) ** 2, axis=-1, keepdims=True)
            return (x - mu) / jnp.sqrt(var + EPS) * gamma + beta
        B, T, _ = src.shape
        q = (src @ Wq + bq).reshape(B, T, N_HEAD, HEAD_DIM)
        k = (src @ Wk + bk).reshape(B, T, N_HEAD, HEAD_DIM)
        v = (src @ Wv + bv).reshape(B, T, N_HEAD, HEAD_DIM)
        scale = HEAD_DIM ** (-0.5)
        scores = jnp.einsum('bqhd,bkhd->bhqk', q, k) * scale
        probs = jax.nn.softmax(scores, axis=-1)
        attn = jnp.einsum('bhqk,bkhd->bqhd', probs, v).reshape(B, T, D_MODEL)
        attn = attn @ Wo + bo
        x = _layer_norm(src + attn, ln1_g, ln1_b)
        keys = (x @ router_w + router_b)[..., 0]
        expert_idx = jnp.remainder(jnp.floor(keys).astype(jnp.int32), N_EXPERTS)
        ff_out = jnp.zeros_like(x)
        for e in range(N_EXPERTS):
            h = jax.nn.relu(x @ W1[e] + b1[e])
            y = h @ W2[e] + b2[e]
            ff_out = ff_out + jnp.where((expert_idx == e)[..., None], y, 0.0)
        return _layer_norm(x + ff_out, ln2_g, ln2_b)
    x = L0_attn_hidden_states
    x = x + 0.5 * _L0_ffn_ref(_layernorm(x, axis=-1), L0_ffn_Wq, L0_ffn_bq, L0_ffn_Wk, L0_ffn_bk, L0_ffn_Wv, L0_ffn_bv, L0_ffn_Wo, L0_ffn_bo, L0_ffn_router_w, L0_ffn_router_b, L0_ffn_W1, L0_ffn_b1, L0_ffn_W2, L0_ffn_b2, L0_ffn_ln1_g, L0_ffn_ln1_b, L0_ffn_ln2_g, L0_ffn_ln2_b)
    x = x + _L0_attn_ref(_layernorm(x, axis=-1), L0_attn_W_qkv, L0_attn_W_g, L0_attn_W_proj, L0_attn_decay)
    x = x + 0.5 * _L0_ffn_ref(_layernorm(x, axis=-1), L0_ffn_Wq, L0_ffn_bq, L0_ffn_Wk, L0_ffn_bk, L0_ffn_Wv, L0_ffn_bv, L0_ffn_Wo, L0_ffn_bo, L0_ffn_router_w, L0_ffn_router_b, L0_ffn_W1, L0_ffn_b1, L0_ffn_W2, L0_ffn_b2, L0_ffn_ln1_g, L0_ffn_ln1_b, L0_ffn_ln2_g, L0_ffn_ln2_b)
    return x

_drawn_inputs = setup_inputs


def setup_inputs(seed=0):
    import zlib

    import numpy as np

    out = dict(_drawn_inputs(seed))
    spreads = {'L0_ffn_bq': (0.0, 0.1),
     'L0_ffn_bk': (0.0, 0.1),
     'L0_ffn_bv': (0.0, 0.1),
     'L0_ffn_bo': (0.0, 0.1),
     'L0_ffn_b1': (0.0, 0.1),
     'L0_ffn_b2': (0.0, 0.1),
     'L0_ffn_ln1_g': (1.0, 0.2),
     'L0_ffn_ln1_b': (0.0, 0.1),
     'L0_ffn_ln2_g': (1.0, 0.2),
     'L0_ffn_ln2_b': (0.0, 0.1)}
    factors = {}
    for name, (base, spread) in spreads.items():
        noise = np.random.default_rng([zlib.crc32(name.encode()), seed]).standard_normal(out[name].shape)
        drawn = base * np.exp(spread * noise) if base else spread * noise
        out[name] = jnp.asarray(drawn.astype(out[name].dtype))
    for name, factor in factors.items():
        out[name] = (out[name] * factor).astype(out[name].dtype)
    return out
```

```python
import numpy as np
import concourse.bass as bass
from concourse import mybir
from contextlib import ExitStack

FP32 = mybir.dt.float32
FP32R = mybir.dt.float32r
INT32 = mybir.dt.int32
ALU = mybir.AluOpType
ACT = mybir.ActivationFunctionType
AX = mybir.AxisListType

P = 128
BATCH, SEQ, DM = 16, 256, 128
TT = SEQ // P
LN_EPS = 1e-5

NH, HD = 16, 8
GROUPS, GH = 4, 4
NE, DFF = 4, 512
CHUNKS = NE * DFF // P
CPE = DFF // P
SCALE = HD ** -0.5

RH, RK, RV, RGROUPS = 8, 16, 32, 4
QK_DIM, V_DIM, SCALE_BASE, GN_EPS = 128, 256, 512.0, 1e-5
MAGIC = 0x5F3759DF

SLOTS = 16
VROW = 17 * P


def ffn_selectors():
    sel = np.zeros((P, GROUPS, 4, P), np.float32)
    for g in range(GROUPS):
        for j in range(GH):
            for d in range(HD):
                p = (g * GH + j) * HD + d
                for kind, parts in enumerate(((0, 1), (2,), (0, 2), (1,))):
                    for part in parts:
                        sel[p, g, kind, 32 * j + HD * part + d] = 1.0
    return sel.reshape(P, -1)


def retention_selectors():
    sel = np.zeros((P, RGROUPS, 4, P), np.float32)
    for g in range(RGROUPS):
        for j in range(2):
            for d in range(RK):
                p = (2 * g + j) * RK + d
                for kind, parts in enumerate(((0, 1), (2, 3), (0, 2), (1, 3))):
                    for part in parts:
                        sel[p, g, kind, 64 * j + RK * part + d] = 1.0
    return sel.reshape(P, -1)


def rotary_tables():
    f = np.float32
    half = QK_DIM // 2
    base = (np.arange(0, QK_DIM, 2, dtype=f) + f(0.4 * QK_DIM)) / f(1.4 * QK_DIM)
    pos = np.arange(SEQ, dtype=f)
    scale = base[None, :] ** (pos[:, None] / f(SCALE_BASE))
    inv_freq = f(1.0) / f(10000.0) ** (np.arange(half, dtype=f) / f(half))
    angle = pos[:, None] * inv_freq[None, :]
    sin, cos = np.sin(angle), np.cos(angle)
    sign = np.tile(np.array([-1.0, 1.0], f), half)[:, None]
    out = []
    for s in (scale, f(1.0) / scale):
        out.append((np.repeat(cos * s, 2, 1).T, np.repeat(sin * s, 2, 1).T * sign))
    return (np.ascontiguousarray(np.concatenate([out[0][n], out[1][n]], 1), dtype=f) for n in range(2))


def constants():
    ident = np.eye(P, dtype=np.float32)
    ones_col = np.zeros((P, 1), np.float32)
    for j in range(GH):
        ones_col[32 * j + 3 * HD:32 * j + 3 * HD + 2] = 1.0
    eidx = np.tile(np.arange(NE, dtype=np.float32), TT)[None].repeat(P, 0)
    cos, sin = rotary_tables()
    return {"c_cos": cos, "c_sin": sin, "c_sel_ret": retention_selectors(), "c_ident": ident, "c_ones_col": ones_col, "c_eidx": eidx, "c_sel_ffn": ffn_selectors()}


def wait(eng, sem, value):
    if isinstance(value, int) and value <= 0:
        return
    eng.wait_ge(sem, value)


def build(nc, A):
    ctx = ExitStack()
    with ctx:
        def sb(name, shape, dt=FP32):
            return ctx.enter_context(nc.sbuf_tensor(name, shape, dt))

        def sem(name):
            return ctx.enter_context(nc.semaphore(name))

        xs = sb("xs", [P, BATCH, TT, DM])
        wide_buf = sb("wide_buf", [P, BATCH, 2, SEQ])
        resid = wide_buf[:, :, 0, :].rearrange("p b (t d) -> p b t d", t=TT)
        stage = sb("stage", [P, 4096])
        ident = sb("ident", [P, P])
        ident_r = sb("ident_r", [P, P], FP32R)
        sel_r = sb("sel_r", [P, GROUPS, 4, P], FP32R)
        ones_col = sb("ones_col", [P, 1])
        eidx = sb("eidx", [P, TT, NE])
        wq = sb("wq", [P, P]); wk = sb("wk", [P, P]); wv = sb("wv", [P, P]); wo = sb("wo", [P, P])
        w1_hi = sb("w1_hi", [P, CHUNKS, P], FP32R)
        w1_lo = sb("w1_lo", [P, CHUNKS, P], FP32R)
        w2 = sb("w2", [P, CHUNKS, P])
        dm = sb("dm", [P, RH, 384])
        dm_flat = dm[:].rearrange("p h n -> p (h n)")
        bias_rows = dm_flat[0:CHUNKS + 2, 2048:2176]
        bias_cols = sb("bias_cols", [P, CHUNKS + 2])
        vecs = sb("vecs", [P, 7, P])
        bv_b, bo_b, g1_b, b1_b, g2_b, b2_b, rw_b = (vecs[:, n, :] for n in range(7))
        rb_b = sb("rb_b", [P, 1])
        b2row = dm_flat[0:1, 2176:2688].rearrange("a (e d) -> a e d", e=NE)
        b2_r = sb("b2_r", [64, NE, P], FP32R)
        ones_r = sb("ones_r", [64, P], FP32R)
        eps_col = sb("eps_col", [P, 1])

        s_nat = sb("s_nat", [P, TT, DM])
        sT = sb("sT", [P, SEQ])
        qk = sb("qk", [P, 2, SEQ])
        qk_hi = sb("qk_hi", [P, 2, SEQ], FP32R)
        qk_lo = sb("qk_lo", [P, 2, SEQ], FP32R)
        stacks = sb("stacks", [P, 2 * GROUPS * SEQ], FP32R)
        q_st, k_st = (stacks[:, n * GROUPS * SEQ:(n + 1) * GROUPS * SEQ].rearrange("p (g t) -> p g t", g=GROUPS) for n in range(2))
        q2_st = sb("q2_st", [P, GROUPS, SEQ], FP32R)
        negmax = sb("negmax", [P, 2, TT, GH])
        mx = sb("mx", [P, TT, P], FP32R)
        probs = sb("probs", [P, 4, TT, SEQ])
        ones_wide = sb("ones_wide", [P, 8, HD])
        v_nat = sb("v_nat", [P, TT, P])
        v_st = sb("v_st", [P, TT, VROW])
        att_un = sb("att_un", [P, 2, SEQ])
        rsum = sb("rsum", [P, TT, 2, 8])
        att = sb("att", [P, TT, P])
        attT = sb("attT", [P, SEQ])
        y1 = sb("y1", [P, TT, DM])
        n1 = sb("n1", [P, TT, DM])
        x1 = sb("x1", [P, TT, DM])
        xt1 = sb("xt1", [P, TT, DM])
        x1_hi = sb("x1_hi", [P, SEQ], FP32R)
        x1_lo = sb("x1_lo", [P, SEQ], FP32R)
        rprod = sb("rprod", [P, TT, DM])
        rkey = sb("rkey", [P, 2, TT])
        rint = sb("rint", [P, 4, TT], INT32)
        masks = sb("masks", [P, BATCH, TT, NE])
        hidden = sb("hidden", [P, 4, SEQ])
        acc = sb("acc", [P, TT, DM])
        n2 = sb("n2", [P, TT, DM])
        xt2 = sb("xt2", [P, 2, TT, DM])
        ln_scratch = {}
        for s in ("prep", "ln1", "ln2"):
            ln_scratch[s] = dict(six=sb(f"six_{s}", [P, TT, 6]), mv=sb(f"mv_{s}", [P, TT, 2]),
                                 lnv=sb(f"lnv_{s}", [P, TT]), seed=sb(f"seed_{s}", [P, TT]),
                                 a=sb(f"a_{s}", [P, TT]), c=sb(f"c_{s}", [P, TT]), rstd=sb(f"rstd_{s}", [P, TT]))

        sel2_r = sb("sel2_r", [P, RGROUPS, 4, P], FP32R)
        cosT = sb("cosT", [P, 2, SEQ])
        sinT = sb("sinT", [P, 2, SEQ])
        wqkv = sb("wqkv", [P, 512])
        wqk_sw = sb("wqk_sw", [P, 256])
        wv_mean = sb("wv_mean", [P, RH])
        wv_cen = sb("wv_cen", [P, V_DIM])
        wg = sb("wg", [P, V_DIM])
        wproj = sb("wproj", [P, 2, DM])
        dec = sb("dec", [RH, 8])
        pw = sb("pw", [RH, 256])
        prow = sb("prow", [RH, 384])
        rot_a = stage[:, 0:512].rearrange("p (a t) -> p a t", a=2)
        rot_b = stage[:, 512:1024].rearrange("p (a t) -> p a t", a=2)
        r_st = stacks[:].rearrange("p (g a t) -> p g a t", g=RGROUPS, a=2)
        ret = stage[:, 1024:2176].rearrange("p (n t) -> p n t", n=3)
        v_ret = probs[:, 0:2, :, :]
        tanh_z = stage[:, 2176:2688].rearrange("p (t v) -> p t v", t=TT)
        outT = stage[:, 2688:3200].rearrange("p (a t) -> p a t", a=2)
        sq = stage[:, 3200:3712]
        ssq = sb("ssq", [P, 16])
        nrm = probs[:, 2, :, :]
        y_ret = probs[:, 3, :, :]
        yT = hidden[:, 0:2, :]
        rs = {}
        for s_, n_ in (("rln", TT), ("gn", 16)):
            rs[s_] = dict(v=sb(f"v_{s_}", [P, n_]), i=sb(f"i_{s_}", [P, n_], INT32), y=sb(f"y_{s_}", [P, n_], INT32),
                          a=sb(f"ra_{s_}", [P, n_]), c=sb(f"rc_{s_}", [P, n_]))
        six_r = sb("six_r", [P, TT, 6])
        mv_r = sb("mv_r", [P, TT, 2])
        decay_rows = nc.dram_tensor("decay_rows", (RH, P, 513), FP32, kind="Internal").ap()

        bank = [ctx.enter_context(nc.psum_tensor(f"bank{n}", [P, 512], FP32)) for n in range(8)]
        score_bank, prob_bank = bank[0:2], bank[2:4]
        pv_bank, misc, up_bank, y_bank = bank[4], bank[5], bank[6], bank[7]

        ld_x, ld_c, ld_w, ld_e, st_out = sem("ld_x"), sem("ld_c"), sem("ld_w"), sem("ld_e"), sem("st_out")
        set_dve, set_pe, set_act, set_pool = sem("set_dve"), sem("set_pe"), sem("set_act"), sem("set_pool")
        prep_ln, ln1, ln2 = sem("prep_ln"), sem("ln1"), sem("ln2")
        seed = {"prep": sem("seed_prep"), "ln1": sem("seed_ln1"), "ln2": sem("seed_ln2")}
        ln_sem = {"prep": prep_ln, "ln1": ln1, "ln2": ln2}
        sT_ps, sT_ready = sem("sT_ps"), sem("sT_ready")
        qk_ps, qk_ready, hi_ready, lo_ready = sem("qk_ps"), sem("qk_ready"), sem("hi_ready"), sem("lo_ready")
        v_ps, v_ready, va_ready, vb_ready = sem("v_ps"), sem("v_ready"), sem("va_ready"), sem("vb_ready")
        resid_ready = sem("resid_ready")
        ex_ps, ex_ready = sem("ex_ps"), sem("ex_ready")
        score_ps, max_done = sem("score_ps"), sem("max_done")
        mx_ready, m_ps, q2_ready = sem("mx_ready"), sem("m_ps"), sem("q2_ready")
        prob_ps, exp_done, pv_done = sem("prob_ps"), sem("exp_done"), sem("pv_done")
        un_ready, att_ps, att_ready = sem("un_ready"), sem("att_ps"), sem("att_ready")
        attT_ps, attT_ready, wo_ps, y1_ready = sem("attT_ps"), sem("attT_ready"), sem("wo_ps"), sem("y1_ready")
        x1_ready, x1T_ps, x1hi_ready, x1lo_ready = sem("x1_ready"), sem("x1T_ps"), sem("x1hi_ready"), sem("x1lo_ready")
        router = sem("router")
        up_ps, h_ready, down_done, y_done = sem("up_ps"), sem("h_ready"), sem("down_done"), sem("y_done")
        x_done = sem("x_done")
        ld_r, ld_d, set_prow, set_scr = sem("ld_r"), sem("ld_d"), sem("set_prow"), sem("set_scr")
        vcopy = sem("vcopy")
        rln, gn = sem("rln"), sem("gn")
        rT_ps, rT_ready = sem("rT_ps"), sem("rT_ready")
        rqk_ps, rot_ready, rqk_ready, rhi_ready, rlo_ready = sem("rqk_ps"), sem("rot_ready"), sem("rqk_ready"), sem("rhi_ready"), sem("rlo_ready")
        rv_ps, rv_ready, z_ps, th_ready, gz_ready = sem("rv_ps"), sem("rv_ready"), sem("z_ps"), sem("th_ready"), sem("gz_ready")
        rex_ps, rex_ready = sem("rex_ps"), sem("rex_ready")
        rs_ps, ret_ready, ro_ps = sem("rs_ps"), sem("ret_ready"), sem("ro_ps")
        oT_ready, on_ps, sq_ready = sem("oT_ready"), sem("on_ps"), sem("sq_ready")
        yr_ready, yT_ps, yT_ready, pr_ps, xr_done = sem("yr_ready"), sem("yT_ps"), sem("yT_ready"), sem("pr_ps"), sem("xr_done")

        block = ctx.enter_context(nc.Block())

        def live(b, base):
            return not isinstance(b, int) or base <= b < base + BATCH

        def iterations(eng, base, body):
            for i in range(base - 1, base + 4):
                body(i)
            with eng.Fori(base + 4, base + 15) as i:
                body(i)
            for i in range(base + 15, base + 19):
                body(i)

        def r_iterations(eng, body):
            for i in range(-1, 2):
                body(i)
            with eng.Fori(2, BATCH - 1) as i:
                body(i)
            for i in range(BATCH - 1, BATCH + 1):
                body(i)

        def at(b, base):
            return bass.ds(b - base, 1)

        @block.sync
        def _(sp):
            xv = A["x"].rearrange("b (t p) d -> p b t d", p=P)
            sp.dma_start(xs[:], xv).then_inc(ld_x, 16)
            sp.dma_start(stage[:, 0:2048], A["c_sel_ffn"]).then_inc(ld_c, 16)
            sp.dma_start(ident[:], A["c_ident"]).then_inc(ld_c, 16)
            sp.dma_start(ones_col[:], A["c_ones_col"]).then_inc(ld_c, 16)
            sp.dma_start(eidx[:].rearrange("p t e -> p (t e)"), A["c_eidx"]).then_inc(ld_c, 16)
            for w, name in ((wq, "Wq"), (wk, "Wk"), (wv, "Wv"), (wo, "Wo")):
                sp.dma_start(w[:], A[name]).then_inc(ld_w, 16)
            sp.dma_start(bias_rows[0:CHUNKS, :], A["b1"].rearrange("e (c p) -> (e c) p", p=P)).then_inc(ld_w, 16)
            sp.dma_start(bias_rows[CHUNKS:CHUNKS + 1, :], A["bq"].rearrange("(a n) -> a n", a=1)).then_inc(ld_w, 16)
            sp.dma_start(bias_rows[CHUNKS + 1:CHUNKS + 2, :], A["bk"].rearrange("(a n) -> a n", a=1)).then_inc(ld_w, 16)
            for n, name in enumerate(("bv", "bo", "ln1_g", "ln1_b", "ln2_g", "ln2_b")):
                sp.dma_start(vecs[:, n, :], A[name].partition_broadcast(P)).then_inc(ld_w, 16)
            sp.dma_start(vecs[:, 6, :], A["router_w"].rearrange("d o -> (d o)").partition_broadcast(P)).then_inc(ld_w, 16)
            sp.dma_start(rb_b[:], A["router_b"].partition_broadcast(P)).then_inc(ld_w, 16)
            sp.dma_start(b2row.rearrange("a e d -> a (e d)"), A["b2"].rearrange("(a e) d -> a (e d)", a=1)).then_inc(ld_w, 16)
            sp.dma_start(stage[:, 2048:4096].rearrange("p (e n) -> p e n", e=NE), A["W1"].rearrange("e d n -> d e n")).then_inc(ld_e, 16)
            sp.dma_start(w2[:].rearrange("p (e c) n -> p e c n", e=NE), A["W2"].rearrange("e (c p) n -> p e c n", p=P)).then_inc(ld_e, 16)
            sp.dma_start(dm_flat[:, 0:2048], A["c_sel_ret"]).then_inc(ld_r, 16)
            sp.dma_start(cosT[:].rearrange("p a t -> p (a t)"), A["c_cos"]).then_inc(ld_r, 16)
            sp.dma_start(sinT[:].rearrange("p a t -> p (a t)"), A["c_sin"]).then_inc(ld_r, 16)
            sp.dma_start(wqkv[:], A["W_qkv"]).then_inc(ld_r, 16)
            sp.dma_start(wg[:], A["W_g"]).then_inc(ld_r, 16)
            sp.dma_start(wproj[:], A["W_proj"].rearrange("(a p) d -> p a d", p=P)).then_inc(ld_r, 16)
            sp.dma_start(dec[:, 0:1], A["decay"].rearrange("(h a) -> h a", a=1)).then_inc(ld_r, 16)
            sp.wait_ge(set_pe, 1)
            sp.wait_ge(set_prow, 1)
            sp.dma_start(decay_rows[:, :, 0:384], prow[:].unsqueeze(1).to_broadcast([RH, P, 384])).then_inc(set_scr, 16)
            sp.wait_ge(set_scr, 16)
            for n, width in ((0, 256), (256, 128)):
                moved = bass.AP(tensor=decay_rows.tensor, offset=P, ap=[[512, P], [P * 513, RH], [1, width]])
                sp.dma_start(dm[:, :, n:n + width], moved).then_inc(ld_d, 16)
            ov = A["out"].rearrange("b (t p) d -> p b t d", p=P)
            with sp.Fori(0, BATCH) as i:
                sp.wait_ge(x_done, i * 3 + 3 * BATCH + 3)
                sp.dma_start(ov[:, bass.ds(i, 1), :, :], xs[:, bass.ds(i, 1), :, :]).then_inc(st_out, 16)
            sp.wait_ge(st_out, 16 * BATCH)

        N_LDC, N_LDW = 4 * 16, 16 * 16
        SET_DVE = 31

        @block.tensor
        def _(pe):
            turn = {}

            def take_misc(consumer, value):
                wait(pe, *turn["last"])
                turn["last"] = (consumer, value)

            pe.wait_ge(ld_w, N_LDW)
            pe.wait_ge(ld_c, N_LDC)
            pe.transpose(misc[:, 0:CHUNKS + 2], bias_rows, ident[0:CHUNKS + 2, 0:CHUNKS + 2]).then_inc(set_pe, 1)
            pe.wait_ge(set_act, 1)
            pe.wait_ge(set_dve, 7)
            pe.wait_ge(set_pool, 2)
            pe.wait_ge(ld_e, 32)

            def transposes(b):
                pe.wait_ge(prep_ln, b * 9 + 9)
                take_misc(sT_ready, b + 1)
                for t in range(TT):
                    last = pe.transpose(misc[:, t * P:(t + 1) * P], s_nat[:, t, :], ident[:])
                last.then_inc(sT_ps, 1)

            def project_qk(b):
                pe.wait_ge(sT_ready, b + 1)
                take_misc(qk_ready, b * 2 + 2)
                pe.matmul(misc[:, 0:SEQ], wq[:], sT[:], start=True, stop=True)
                pe.matmul(misc[:, SEQ:2 * SEQ], wk[:], sT[:], start=True, stop=True).then_inc(qk_ps, 1)

            def project_v(b):
                take_misc(v_ready, b + 1)
                for t in range(TT):
                    last = pe.matmul(misc[:, t * P:(t + 1) * P], sT[:, t * P:(t + 1) * P], wv[:], start=True, stop=True)
                last.then_inc(v_ps, 1)

            def expand(b, g):
                if g == 0:
                    pe.wait_ge(hi_ready, b + 1)
                    pe.wait_ge(lo_ready, b + 1)
                take_misc(ex_ready, b * 8 + 2 * g + 2)
                for n in range(2):
                    o = misc[:, n * SEQ:(n + 1) * SEQ]
                    pe.matmul(o, sel_r[:, g, 2 * n, :], qk_hi[:, n, :], start=True, stop=False)
                    last = pe.matmul(o, sel_r[:, g, 2 * n + 1, :], qk_lo[:, n, :], start=False, stop=True)
                last.then_inc(ex_ps, 1)

            def score(b, h):
                g, r = h // GH, 32 * (h % GH)
                if h % GH == 0:
                    pe.wait_ge(ex_ready, b * 8 + 2 * g + 2)
                wait(pe, max_done, b * NH + (h - 1))
                for t in range(TT):
                    last = pe.matmul(score_bank[h % 2][:, t * SEQ:(t + 1) * SEQ], q_st[r:r + 32, g, t * P:(t + 1) * P],
                                     k_st[r:r + 32, g, :], start=True, stop=True)
                last.then_inc(score_ps, 1)

            def spread_max(b, g):
                pe.wait_ge(mx_ready, b * 8 + 2 * g + 2)
                take_misc(q2_ready, b * 4 + g + 1)
                for t in range(TT):
                    last = pe.matmul(misc[:, t * P:(t + 1) * P], mx[:, t, :], ident_r[:], start=True, stop=True)
                last.then_inc(m_ps, 1)

            def shifted_score(b, h):
                g, r = h // GH, 32 * (h % GH)
                if h % GH == 0:
                    pe.wait_ge(q2_ready, b * 4 + g + 1)
                wait(pe, exp_done, b * NH + (h - 1))
                for t in range(TT):
                    last = pe.matmul(prob_bank[h % 2][:, t * SEQ:(t + 1) * SEQ], k_st[r:r + 32, g, t * P:(t + 1) * P],
                                     q2_st[r:r + 32, g, :], start=True, stop=True)
                last.then_inc(prob_ps, 1)

            def weigh_values(b, h):
                pe.wait_ge(exp_done, b * NH + h + 1)
                if h == 0:
                    pe.wait_ge(va_ready, b * 2 + 2)
                    wait(pe, un_ready, b)
                if h == NH // 2:
                    pe.wait_ge(vb_ready, b * 2 + 2)
                half, k = h // 8, h % 8
                for t in range(TT):
                    last = pe.matmul(pv_bank[:, half * SEQ:(half + 1) * SEQ], v_st[:, t, h * P:(h + 1) * P],
                                     probs[:, h % 4, t, :], start=(k == 0 and t == 0), stop=(k == 7 and t == TT - 1))
                last.then_inc(pv_done, 1)

            def att_to_tokens(b):
                pe.wait_ge(un_ready, b + 1)
                take_misc(att_ready, b * 4 + 4)
                for t in range(TT):
                    for half in range(2):
                        last = pe.transpose(misc[:, (2 * t + half) * P:(2 * t + half + 1) * P],
                                            att_un[:, half, t * P:(t + 1) * P], ident[:])
                last.then_inc(att_ps, 1)

            def att_to_dims(b):
                pe.wait_ge(att_ready, b * 4 + 4)
                take_misc(attT_ready, b + 1)
                for t in range(TT):
                    last = pe.transpose(misc[:, t * P:(t + 1) * P], att[:, t, :], ident[:])
                last.then_inc(attT_ps, 1)

            def project_out(b):
                pe.wait_ge(attT_ready, b + 1)
                take_misc(y1_ready, b + 1)
                for t in range(TT):
                    last = pe.matmul(misc[:, t * P:(t + 1) * P], attT[:, t * P:(t + 1) * P], wo[:], start=True, stop=True)
                last.then_inc(wo_ps, 1)

            def x1_to_dims(b):
                pe.wait_ge(x1_ready, b * 2 + 2)
                take_misc(x1lo_ready, b + 1)
                for t in range(TT):
                    last = pe.transpose(misc[:, t * P:(t + 1) * P], x1[:, t, :], ident[:])
                last.then_inc(x1T_ps, 1)

            def up(b, c):
                if c == 0:
                    pe.wait_ge(x1lo_ready, b + 1)
                wait(pe, h_ready, b * CHUNKS + c)
                o = up_bank[:, 0:SEQ]
                pe.matmul(o, w1_lo[:, c, :], x1_hi[:], start=True, stop=False)
                pe.matmul(o, w1_hi[:, c, :], x1_lo[:], start=False, stop=False)
                pe.matmul(o, w1_hi[:, c, :], x1_hi[:], start=False, stop=True).then_inc(up_ps, 1)

            def down(b, c):
                e, first, final = c // CPE, c % CPE == 0, c % CPE == CPE - 1
                pe.wait_ge(h_ready, b * CHUNKS + c + 1)
                if first:
                    wait(pe, y_done, b * 8 + 2 * e)
                    for t in range(TT):
                        pe.matmul(y_bank[:, t * P:(t + 1) * P], ones_r[:], b2_r[:, e, :], start=(t == 0), stop=False,
                                  skip_group_check=True)
                for t in range(TT):
                    last = pe.matmul(y_bank[:, t * P:(t + 1) * P], hidden[:, c % 4, t * P:(t + 1) * P], w2[:, c, :],
                                     start=False, stop=final, skip_group_check=True)
                last.then_inc(down_done, 1)

            def phase(base):
                turn["last"] = (set_act, 1)

                def body(i):
                    if live(i - 2, base):
                        turn["last"] = (x1lo_ready, i - 2 + 1)

                    for s in range(SLOTS):
                        h6, h8 = (s - 6) % NH, (s - 8) % NH
                        b6, b8 = (i if s >= 6 else i - 1), (i if s >= 8 else i - 1)
                        if live(i, base):
                            score(i, s)
                        if s in (1, 5, 9) and live(i, base):
                            expand(i, s // 4 + 1)
                        if s == 13 and live(i + 1, base):
                            expand(i + 1, 0)
                        bu, cu = (i - 2, s - 1) if s >= 1 else (i - 3, s + 15)
                        if live(bu, base):
                            up(bu, cu)
                        if live(b6, base):
                            shifted_score(b6, h6)
                        bd, cd = (i - 2, s - 3) if s >= 3 else (i - 3, s + 13)
                        if live(bd, base):
                            down(bd, cd)
                        if live(b8, base):
                            weigh_values(b8, h8)
                        if s == 6 and live(i + 1, base):
                            transposes(i + 1)
                        if s == 7 and live(i + 1, base):
                            project_qk(i + 1)
                        if s == 12 and live(i + 1, base):
                            project_v(i + 1)
                        if s == 8 and live(i - 1, base):
                            att_to_tokens(i - 1)
                        if s == 10 and live(i - 1, base):
                            att_to_dims(i - 1)
                        if s == 11 and live(i - 1, base):
                            project_out(i - 1)
                        if s in (4, 8, 12) and live(i, base):
                            spread_max(i, s // 4 - 1)
                        if s == 0 and live(i - 1, base):
                            spread_max(i - 1, 3)
                        if s == 15 and live(i - 1, base):
                            x1_to_dims(i - 1)

                iterations(pe, base, body)

            def retention():
                pe.wait_ge(x_done, 3 * BATCH)
                pe.wait_ge(ld_r, 7 * 16)
                pe.wait_ge(set_dve, SET_DVE)
                last7, last4 = {}, {}

                def take(which, consumer, value):
                    if "last" in which:
                        wait(pe, *which["last"])
                    which["last"] = (consumer, value)

                def body(i):
                    if live(i - 2, 0) or not isinstance(i, int):
                        last7["last"] = (xr_done, i - 1)
                        last4["last"] = (gn, (i - 1) * 15)
                    for s in range(8):
                        if live(i, 0):
                            h, r, g = s, 64 * (s % 2), s // 2
                            if h % 2 == 0:
                                pe.wait_ge(rex_ready, i * 4 + g + 1)
                            wait(pe, ret_ready, i * 8 + h - 1)
                            ps = bank[h % 2]
                            pe.matmul(ps[:, 0:256], r_st[r:r + 64, g, 1, 0:P], r_st[r:r + 64, g, 0, :], start=True, stop=True)
                            pe.matmul(ps[:, 256:384], r_st[r:r + 64, g, 1, P:2 * P], r_st[r:r + 64, g, 0, P:2 * P],
                                      start=True, stop=True).then_inc(rs_ps, 1)
                        be, ge = (i, s // 2 + 1) if s in (0, 2, 4) else (i + 1, 0)
                        if s in (0, 2, 4, 6) and live(be, 0):
                            if ge == 0:
                                pe.wait_ge(rlo_ready, be + 1)
                            wait(pe, rex_ready, be * 4 + ge)
                            for n in range(2):
                                o = bank[6][:, n * SEQ:(n + 1) * SEQ]
                                pe.matmul(o, sel2_r[:, ge, 2 * n, :], qk_hi[:, n, :], start=True, stop=False)
                                last = pe.matmul(o, sel2_r[:, ge, 2 * n + 1, :], qk_lo[:, n, :], start=False, stop=True)
                            last.then_inc(rex_ps, 1)
                        bo, ho = (i, s - 1) if s >= 1 else (i - 1, 7)
                        if live(bo, 0):
                            pe.wait_ge(ret_ready, bo * 8 + ho + 1)
                            if ho == 0:
                                pe.wait_ge(vcopy, bo + 1)
                            if ho % 4 == 0:
                                wait(pe, oT_ready, bo * 2 + ho // 4 - 1)
                            o = bank[2 + ho // 4][32 * (ho % 4):32 * (ho % 4) + 32, 0:SEQ]
                            pe.matmul(o, v_use(bo, 0, ho), ret[:, ho % 3, 0:256], start=True, stop=True)
                            pe.matmul(o[:, P:2 * P], v_use(bo, 1, ho), ret[:, ho % 3, 256:384], start=False, stop=True,
                                      skip_group_check=True).then_inc(ro_ps, 1)
                        if s == 1 and live(i + 1, 0):
                            pe.wait_ge(rln, (i + 1) * 18 + 18)
                            take(last7, rT_ready, i + 2)
                            for t in range(TT):
                                last = pe.transpose(bank[7][:, t * P:(t + 1) * P], s_nat[:, t, :], ident[:])
                            last.then_inc(rT_ps, 1)
                        if s == 2 and live(i + 1, 0):
                            pe.wait_ge(rT_ready, i + 2)
                            take(last4, rot_ready, (i + 1) * 2 + 2)
                            for n in range(2):
                                pe.matmul(bank[4][:, n * SEQ:(n + 1) * SEQ], wqkv[:, n * P:(n + 1) * P], sT[:], start=True, stop=True)
                            for n in range(2):
                                last = pe.matmul(bank[5][:, n * SEQ:(n + 1) * SEQ], wqk_sw[:, n * P:(n + 1) * P], sT[:], start=True, stop=True)
                            last.then_inc(rqk_ps, 1)
                        if s == 3 and live(i + 1, 0):
                            take(last7, rv_ready, i + 2)
                            for t in range(TT):
                                last = pe.matmul(bank[7][:, t * SEQ:(t + 1) * SEQ], sT[:, t * P:(t + 1) * P], wv_cen[:], start=True, stop=True)
                            last.then_inc(rv_ps, 1)
                        if s == 4 and live(i + 1, 0):
                            take(last7, gz_ready, i + 2)
                            for t in range(TT):
                                last = pe.matmul(bank[7][:, t * SEQ:(t + 1) * SEQ], sT[:, t * P:(t + 1) * P], wg[:], start=True, stop=True)
                            last.then_inc(z_ps, 1)
                        if s == 3 and live(i - 1, 0):
                            pe.wait_ge(oT_ready, (i - 1) * 2 + 2)
                            take(last4, gn, (i - 1) * 15 + 15)
                            for t in range(TT):
                                for half in range(2):
                                    last = pe.transpose(bank[4][:, (2 * t + half) * P:(2 * t + half + 1) * P],
                                                        outT[:, half, t * P:(t + 1) * P], ident[:])
                            last.then_inc(on_ps, 1)
                        if s == 6 and live(i - 1, 0):
                            pe.wait_ge(yr_ready, i)
                            take(last7, yT_ready, i)
                            for half in range(2):
                                for t in range(TT):
                                    last = pe.transpose(bank[7][:, (2 * half + t) * P:(2 * half + t + 1) * P],
                                                        y_ret[:, t, half * P:(half + 1) * P], ident[:])
                            last.then_inc(yT_ps, 1)
                        if s == 7 and live(i - 1, 0):
                            pe.wait_ge(yT_ready, i)
                            take(last7, xr_done, i)
                            for t in range(TT):
                                for half in range(2):
                                    last = pe.matmul(bank[7][:, t * P:(t + 1) * P], yT[:, half, t * P:(t + 1) * P], wproj[:, half, :],
                                                     start=(half == 0), stop=(half == 1))
                            last.then_inc(pr_ps, 1)

                def v_use(b, t, h):
                    return v_ret[:, 0, t, RV * h:RV * h + RV]

                r_iterations(pe, body)

            phase(0)
            retention()
            pe.wait_ge(xr_done, BATCH)
            phase(BATCH)

        @block.scalar
        def _(act):
            act.preload_act_table_set("natural_log_exp_and_others")
            act.wait_ge(set_pe, 1)
            act.activation(bias_cols[:], misc[:, 0:CHUNKS + 2], ACT.Copy).then_inc(set_act, 1)
            act.wait_ge(set_dve, 7)
            act.wait_ge(set_act, 1)

            def seeds(b, which):
                s = ln_scratch[which]
                act.wait_ge(ln_sem[which], b * 9 + 4)
                act.activation(s["lnv"][:], s["mv"][:, :, 1], ACT.Ln, bias=eps_col[:]).then_inc(seed[which], 1)
                act.wait_ge(seed[which], b * 2 + 1)
                act.activation(s["seed"][:], s["lnv"][:], ACT.Exp, scale=-0.5).then_inc(seed[which], 1)

            def out_sT(b):
                act.wait_ge(sT_ps, b + 1)
                wait(act, v_ps, b)
                act.activation(sT[:], misc[:, 0:SEQ], ACT.Copy).then_inc(sT_ready, 1)

            def out_qk(b):
                act.wait_ge(qk_ps, b + 1)
                wait(act, hi_ready, b)
                wait(act, lo_ready, b)
                for n in range(2):
                    act.activation(qk[:, n, :], misc[:, n * SEQ:(n + 1) * SEQ], ACT.Identity,
                                   bias=bias_cols[:, CHUNKS + n:CHUNKS + n + 1]).then_inc(qk_ready, 1)

            def out_expand(b, g):
                act.wait_ge(ex_ps, b * 4 + g + 1)
                wait(act, prob_ps, (b - 1) * NH + 4 * g + 4)
                act.activation(q_st[:, g, :], misc[:, 0:SEQ], ACT.Copy).then_inc(ex_ready, 1)
                act.activation(k_st[:, g, :], misc[:, SEQ:2 * SEQ], ACT.Identity, bias=ones_col[:]).then_inc(ex_ready, 1)

            def exp(b, h):
                act.wait_ge(prob_ps, b * NH + h + 1)
                wait(act, pv_done, b * NH + h - 3)
                act.activation(probs[:, h % 4, :, :], prob_bank[h % 2][:].rearrange("p (t q) -> p t q", t=TT), ACT.Exp,
                               scale=SCALE).then_inc(exp_done, 1)

            def out_pv(b):
                act.wait_ge(pv_done, b * NH + NH)
                wait(act, att_ps, b)
                act.activation(att_un[:], pv_bank[:].rearrange("p (a q) -> p a q", a=2), ACT.Copy).then_inc(un_ready, 1)

            def out_attT(b):
                act.wait_ge(attT_ps, b + 1)
                wait(act, wo_ps, b)
                act.activation(attT[:], misc[:, 0:SEQ], ACT.Copy).then_inc(attT_ready, 1)

            def round_x1(b):
                act.wait_ge(x1T_ps, b + 1)
                wait(act, up_ps, b * CHUNKS)
                act.activation(x1_hi[:], misc[:, 0:SEQ], ACT.Copy).then_inc(x1hi_ready, 1)

            def relu(b, c):
                act.wait_ge(up_ps, b * CHUNKS + c + 1)
                wait(act, down_done, b * CHUNKS + c - 3)
                act.activation(hidden[:, c % 4, :], up_bank[:, 0:SEQ], ACT.Relu, bias=bias_cols[:, c:c + 1]).then_inc(h_ready, 1)

            def phase(base):
                def body(i):
                    for s in range(SLOTS):
                        h6, b6 = (s - 6) % NH, (i if s >= 6 else i - 1)
                        if s == 0 and live(i - 2, base):
                            round_x1(i - 2)
                        if s in (1, 5, 9) and live(i, base):
                            out_expand(i, s // 4 + 1)
                        if s == 13 and live(i + 1, base):
                            out_expand(i + 1, 0)
                        bu, cu = (i - 2, s - 1) if s >= 1 else (i - 3, s + 15)
                        if live(bu, base):
                            relu(bu, cu)
                        if live(b6, base):
                            exp(b6, h6)
                        if s == 8 and live(i - 1, base):
                            out_pv(i - 1)
                        if s == 3 and live(i + 1, base):
                            seeds(i + 1, "prep")
                        if s == 12 and live(i - 1, base):
                            seeds(i - 1, "ln1")
                        if s == 4 and live(i - 3, base):
                            seeds(i - 3, "ln2")
                        if s == 6 and live(i + 1, base):
                            out_sT(i + 1)
                        if s == 7 and live(i + 1, base):
                            out_qk(i + 1)
                        if s == 10 and live(i - 1, base):
                            out_attT(i - 1)

                iterations(act, base, body)

            def retention():
                act.wait_ge(x_done, 3 * BATCH)

                def body(i):
                    for s in range(8):
                        be, ge = (i, s // 2 + 1) if s in (0, 2, 4) else (i + 1, 0)
                        if s in (0, 2, 4, 6) and live(be, 0):
                            act.wait_ge(rex_ps, be * 4 + ge + 1)
                            wait(act, rs_ps, (be - 1) * 8 + 2 * ge + 2)
                            act.activation(r_st[:, ge, :, :], bank[6][:].rearrange("p (a t) -> p a t", a=2), ACT.Copy).then_inc(rex_ready, 1)
                        if s == 1 and live(i - 1, 0):
                            act.wait_ge(ro_ps, (i - 1) * 8 + 8)
                            wait(act, on_ps, i - 1)
                            act.activation(outT[:, 1, :], bank[3][:, 0:SEQ], ACT.Copy).then_inc(oT_ready, 1)
                        if s == 5 and live(i, 0):
                            act.wait_ge(ro_ps, i * 8 + 4)
                            wait(act, on_ps, i)
                            act.activation(outT[:, 0, :], bank[2][:, 0:SEQ], ACT.Copy).then_inc(oT_ready, 1)
                        if s == 1 and live(i + 1, 0):
                            act.wait_ge(rT_ps, i + 2)
                            wait(act, z_ps, i + 1)
                            act.activation(sT[:], bank[7][:, 0:SEQ], ACT.Copy).then_inc(rT_ready, 1)
                        if s == 3 and live(i - 1, 0):
                            act.wait_ge(on_ps, i)
                            wait(act, gn, (i - 2) * 15 + 1)
                            act.activation(sq, bank[4][:], ACT.Square).then_inc(sq_ready, 1)
                        if s == 3 and live(i + 1, 0):
                            act.wait_ge(rv_ps, i + 2)
                            wait(act, vcopy, (i + 1) * 1)
                            act.activation(v_ret[:, 1, :, :], bank[7][:].rearrange("p (t v) -> p t v", t=TT), ACT.Copy).then_inc(rv_ready, 1)
                        if s == 4 and live(i + 1, 0):
                            act.wait_ge(z_ps, i + 2)
                            wait(act, gz_ready, i + 1)
                            act.activation(tanh_z, bank[7][:].rearrange("p (t v) -> p t v", t=TT), ACT.Tanh, scale=0.5).then_inc(th_ready, 1)
                        if s == 6 and live(i - 1, 0):
                            act.wait_ge(yT_ps, i)
                            wait(act, pr_ps, i - 1)
                            act.activation(yT, bank[7][:].rearrange("p (a t) -> p a t", a=2), ACT.Copy).then_inc(yT_ready, 1)

                r_iterations(act, body)

            phase(0)
            retention()
            act.wait_ge(xr_done, BATCH)
            phase(BATCH)

        @block.vector
        def _(dve):
            dve.memset(mx[:].bitcast(FP32), 0.0).then_inc(set_dve, 1)
            dve.memset(b2_r[:].bitcast(FP32), 0.0).then_inc(set_dve, 1)
            dve.memset(eps_col[:], LN_EPS).then_inc(set_dve, 1)
            dve.memset(ones_r[:].bitcast(FP32), 1.0).then_inc(set_dve, 1)
            dve.wait_ge(ld_c, N_LDC)
            dve.tensor_copy(sel_r[:].rearrange("p g k m -> p (g k m)"), stage[:, 0:2048])
            dve.tensor_copy(ident_r[:], ident[:])
            dve.wait_ge(ld_w, N_LDW)
            dve.wait_ge(set_dve, 2)
            dve.tensor_copy(b2_r[0:1, :, :], b2row)
            dve.wait_ge(ld_e, 32)
            dve.tensor_copy(w1_hi[:].rearrange("p c m -> p (c m)"), stage[:, 2048:4096]).then_inc(set_dve, 1)
            dve.wait_ge(set_dve, 5)
            dve.tensor_tensor(b2_r[32:33, :, :], b2row, b2_r[0:1, :, :].bitcast(FP32), ALU.subtract).then_inc(set_dve, 1)
            dve.tensor_tensor(w1_lo[:].rearrange("p c m -> p (c m)"), stage[:, 2048:4096],
                              w1_hi[:].rearrange("p c m -> p (c m)").bitcast(FP32), ALU.subtract).then_inc(set_dve, 1)
            dve.wait_ge(ld_x, 16)
            dve.memset(pw[:, 0:1], 1.0).then_inc(set_dve, 1)
            dve.memset(prow[:, 0:P], 0.0).then_inc(set_dve, 1)
            dve.wait_ge(ld_r, 7 * 16)
            dve.tensor_copy(sel2_r[:].rearrange("p g k m -> p (g k m)"), dm_flat[:, 0:2048]).then_inc(set_dve, 1)
            for n in range(2):
                dve.tensor_copy(wqk_sw[:].rearrange("p (c a) -> p c a", a=2)[:, :, n],
                                wqkv[:, 0:256].rearrange("p (c a) -> p c a", a=2)[:, :, 1 - n]).then_inc(set_dve, 1)
            wv_heads = wqkv[:, 256:512].rearrange("p (h v) -> p h v", h=RH)
            dve.tensor_reduce(wv_mean[:], wv_heads, AX.X, ALU.add).then_inc(set_dve, 1)
            dve.wait_ge(set_dve, 13)
            dve.tensor_scalar(wv_mean[:], wv_mean[:], -1.0 / RV, None, ALU.mult).then_inc(set_dve, 1)
            dve.wait_ge(set_dve, 14)
            dve.tensor_tensor(wv_cen[:].rearrange("p (h v) -> p h v", h=RH), wv_heads,
                              wv_mean[:].unsqueeze(2).to_broadcast([P, RH, RV]), ALU.add).then_inc(set_dve, 1)
            dve.tensor_scalar(wproj[:], wproj[:], 0.5, None, ALU.mult).then_inc(set_dve, 1)
            count = 16
            for k in range(8):
                w = 1 << k
                dve.tensor_scalar(pw[:, w:2 * w], pw[:, 0:w], dec[:, k:k + 1], None, ALU.mult).then_inc(set_dve, 1)
                if k < 7:
                    dve.tensor_tensor(dec[:, k + 1:k + 2], dec[:, k:k + 1], dec[:, k:k + 1], ALU.mult).then_inc(set_dve, 1)
                count += 2 if k < 7 else 1
                dve.wait_ge(set_dve, count)
            dve.tensor_scalar(prow[:, P:384], pw[:], RK ** -0.5, None, ALU.mult).then_inc(set_prow, 1)

            def layer_norm(b, which, src, dst):
                s, done = ln_scratch[which], ln_sem[which]
                for t in range(TT):
                    dve.bn_stats(s["six"][:, t, :], src(t)).then_inc(done, 1)

            def layer_norm_moments(b, which):
                s, done = ln_scratch[which], ln_sem[which]
                for t in range(TT):
                    dve.bn_aggr(s["mv"][:, t, :], s["six"][:, t, :]).then_inc(done, 1)

            def layer_norm_end(b, which, src, dst):
                s, done = ln_scratch[which], ln_sem[which]
                dve.wait_ge(seed[which], b * 2 + 2)
                dve.scalar_tensor_tensor(s["a"][:], s["mv"][:, :, 1], LN_EPS, s["seed"][:], ALU.add, ALU.mult).then_inc(done, 1)
                dve.wait_ge(done, b * 9 + 5)
                dve.scalar_tensor_tensor(s["c"][:], s["a"][:], -0.5, s["seed"][:], ALU.mult, ALU.mult).then_inc(done, 1)
                dve.wait_ge(done, b * 9 + 6)
                dve.scalar_tensor_tensor(s["rstd"][:], s["c"][:], 1.5, s["seed"][:], ALU.add, ALU.mult).then_inc(done, 1)
                dve.wait_ge(done, b * 9 + 7)
                for t in range(TT):
                    dve.tensor_scalar(dst(t), src(t), s["mv"][:, t, 0:1], s["rstd"][:, t:t + 1], ALU.subtract, ALU.mult)\
                       .then_inc(done, 1)

            def split_qk(b):
                dve.wait_ge(hi_ready, b + 1)
                wait(dve, ex_ps, b * 4)
                dve.tensor_tensor(qk_lo[:], qk[:], qk_hi[:].bitcast(FP32), ALU.subtract).then_inc(lo_ready, 1)

            def out_v(b):
                dve.wait_ge(v_ps, b + 1)
                wait(dve, vb_ready, b * 2)
                wait(dve, va_ready, b * 2)
                dve.tensor_tensor(v_nat[:], misc[:, 0:SEQ].rearrange("p (t d) -> p t d", t=TT),
                                  bv_b.unsqueeze(1).to_broadcast([P, TT, P]), ALU.add).then_inc(v_ready, 1)

            def maximum(b, h):
                g, j = h // GH, h % GH
                dve.wait_ge(score_ps, b * NH + h + 1)
                dve.tensor_reduce(negmax[:, g % 2, :, j], score_bank[h % 2][:].rearrange("p (t k) -> p t k", t=TT),
                                  AX.X, ALU.max, negate=True).then_inc(max_done, 1)

            def split_max(b, g):
                dve.wait_ge(max_done, b * NH + 4 * g + 4)
                wait(dve, m_ps, b * 4 + g)
                rows = mx[:].rearrange("p t (j c) -> p t j c", c=32)
                hi, lo = rows[:, :, :, 3 * HD], rows[:, :, :, 3 * HD + 1]
                dve.tensor_copy(hi, negmax[:, g % 2, :, :]).then_inc(mx_ready, 1)
                dve.wait_ge(mx_ready, b * 8 + 2 * g + 1)
                dve.tensor_tensor(lo, negmax[:, g % 2, :, :], hi.bitcast(FP32), ALU.subtract).then_inc(mx_ready, 1)

            def shift_q(b, g):
                dve.wait_ge(m_ps, b * 4 + g + 1)
                wait(dve, prob_ps, (b - 1) * NH + 4 * g + 4)
                dve.tensor_tensor(q2_st[:, g, :], misc[:, 0:SEQ], q_st[:, g, :].bitcast(FP32), ALU.add).then_inc(q2_ready, 1)

            def normalize(b):
                dve.wait_ge(att_ps, b + 1)
                wait(dve, attT_ps, b)
                m = misc[:].rearrange("p (t a h d) -> p t a h d", t=TT, a=2, h=16)
                for half in range(2):
                    sums = m[:, :, half, 8 - 8 * half:16 - 8 * half, 0]
                    dve.reciprocal(rsum[:, :, half, :], sums).then_inc(att_ready, 1)
                dve.wait_ge(att_ready, b * 4 + 2)
                for half in range(2):
                    pv = m[:, :, half, 8 * half:8 * half + 8, :]
                    dve.tensor_tensor(att[:, :, 64 * half:64 * half + 64].rearrange("p t (h d) -> p t h d", h=8), pv,
                                      rsum[:, :, half, :].unsqueeze(3).to_broadcast([P, TT, 8, HD]), ALU.mult)\
                       .then_inc(att_ready, 1)

            def add_attention(b, base):
                dve.wait_ge(wo_ps, b + 1)
                dve.wait_ge(resid_ready, b + 1)
                dve.tensor_tensor(y1[:], misc[:, 0:SEQ].rearrange("p (t d) -> p t d", t=TT),
                                  resid[:, at(b, base), :, :], ALU.add).then_inc(y1_ready, 1)
                dve.wait_ge(y1_ready, b + 1)

            def split_x1(b):
                dve.wait_ge(x1hi_ready, b + 1)
                wait(dve, up_ps, b * CHUNKS)
                dve.tensor_tensor(x1_lo[:], misc[:, 0:SEQ], x1_hi[:].bitcast(FP32), ALU.subtract).then_inc(x1lo_ready, 1)

            def route(b, base):
                n = [b * 8]

                def step(ins):
                    ins.then_inc(router, 1)
                    n.append(n[-1] + 1)
                    dve.wait_ge(router, n[-1])

                dve.wait_ge(x1_ready, b * 2 + 2)
                step(dve.tensor_tensor(rprod[:], x1[:], rw_b.unsqueeze(1).to_broadcast([P, TT, P]), ALU.mult))
                step(dve.tensor_reduce(rkey[:, 0, :], rprod[:], AX.X, ALU.add))
                step(dve.tensor_scalar(rkey[:, 1, :], rkey[:, 0, :], rb_b[:], None, ALU.add))
                step(dve.tensor_copy(rint[:, 0, :], rkey[:, 1, :]))
                step(dve.tensor_tensor(rint[:, 1, :], rint[:, 0, :], rkey[:, 1, :], ALU.is_gt))
                step(dve.tensor_tensor(rint[:, 2, :], rint[:, 0, :], rint[:, 1, :], ALU.subtract))
                step(dve.tensor_scalar(rint[:, 3, :], rint[:, 2, :], 3, None, ALU.bitwise_and))
                step(dve.tensor_tensor(masks[:, at(b, base), :, :], rint[:, 3, :].unsqueeze(2).to_broadcast([P, TT, NE]),
                                       eidx[:], ALU.is_equal))

            def add_expert(b, e, base):
                dve.wait_ge(down_done, b * CHUNKS + 4 * e + 4)
                wait(dve, y_done, b * 8 + 2 * e)
                if e == 0:
                    wait(dve, ln2, b * 9)
                for t in range(TT):
                    prior = x1 if e == 0 else acc
                    dve.scalar_tensor_tensor(acc[:, t, :], y_bank[:, t * P:(t + 1) * P], masks[:, at(b, base), t, e],
                                             prior[:, t, :], ALU.mult, ALU.add).then_inc(y_done, 1)

            def phase(base):
                def body(i):
                    def x_tile(t):
                        return xs[:, at(i + 1, base), t, :]
                    for s in range(SLOTS):
                        if s in (4, 8, 12) and live(i, base):
                            split_max(i, s // 4 - 1)
                        if s == 0 and live(i - 1, base):
                            split_max(i - 1, 3)
                        if s in (7, 11, 15) and live(i - 2, base):
                            add_expert(i - 2, (s - 7) // 4, base)
                        if s == 2 and live(i + 1, base):
                            wait(dve, sT_ps, i + 1)
                            wait(dve, resid_ready, i + 1)
                            layer_norm(i + 1, "prep", x_tile, None)
                            dve.wait_ge(prep_ln, (i + 1) * 9 + 2)
                        if s == 11 and live(i - 1, base):
                            add_attention(i - 1, base)
                            layer_norm(i - 1, "ln1", lambda t: y1[:, t, :], None)
                            dve.wait_ge(ln1, (i - 1) * 9 + 2)
                        if s == 3 and live(i - 3, base):
                            add_expert(i - 3, 3, base)
                            dve.wait_ge(y_done, (i - 3) * 8 + 8)
                            layer_norm(i - 3, "ln2", lambda t: acc[:, t, :], None)
                            dve.wait_ge(ln2, (i - 3) * 9 + 2)
                        if live(i, base):
                            maximum(i, s)
                        if s == 2 and live(i + 1, base):
                            layer_norm_moments(i + 1, "prep")
                        if s == 11 and live(i - 1, base):
                            layer_norm_moments(i - 1, "ln1")
                        if s == 3 and live(i - 3, base):
                            layer_norm_moments(i - 3, "ln2")
                        if s in (5, 9, 13) and live(i, base):
                            shift_q(i, s // 4 - 1)
                        if s == 1 and live(i - 1, base):
                            shift_q(i - 1, 3)
                        if s == 0 and live(i - 2, base):
                            split_x1(i - 2)
                        if s == 15 and live(i - 1, base):
                            route(i - 1, base)
                        if s == 4 and live(i + 1, base):
                            layer_norm_end(i + 1, "prep", x_tile, lambda t: s_nat[:, t, :])
                        if s == 10 and live(i + 1, base):
                            split_qk(i + 1)
                        if s == 12 and live(i + 1, base):
                            out_v(i + 1)
                        if s == 8 and live(i - 1, base):
                            normalize(i - 1)
                        if s == 13 and live(i - 1, base):
                            wait(dve, x1_ready, (i - 1) * 2)
                            layer_norm_end(i - 1, "ln1", lambda t: y1[:, t, :], lambda t: n1[:, t, :])
                        if s == 5 and live(i - 3, base):
                            wait(dve, x_done, (i - 3) * 3)
                            layer_norm_end(i - 3, "ln2", lambda t: acc[:, t, :], lambda t: n2[:, t, :])

                iterations(dve, base, body)

            def retention():
                dve.wait_ge(x_done, 3 * BATCH)
                dve.wait_ge(ld_d, 32)

                def rsqrt(s, src, scale, eps, done, k):
                    n = [k]

                    def step(ins):
                        ins.then_inc(done, 1)
                        n.append(n[-1] + 1)
                        dve.wait_ge(done, n[-1])

                    y = s["y"][:].bitcast(FP32)
                    step(dve.tensor_scalar(s["v"][:], src, scale, eps, ALU.mult, ALU.add))
                    step(dve.tensor_scalar(s["i"][:], s["v"][:].bitcast(INT32), 1, None, ALU.logical_shift_right))
                    step(dve.tensor_scalar(s["y"][:], s["i"][:], -1.0, float(MAGIC), ALU.mult, ALU.add))
                    for _ in range(3):
                        step(dve.scalar_tensor_tensor(s["a"][:], s["v"][:], -0.5, y, ALU.mult, ALU.mult))
                        step(dve.tensor_tensor(s["c"][:], s["a"][:], y, ALU.mult))
                        step(dve.scalar_tensor_tensor(y, s["c"][:], 1.5, y, ALU.add, ALU.mult))

                def body(i):
                    for s in range(8):
                        if s == 0 and live(i + 1, 0):
                            for t in range(TT):
                                dve.bn_stats(six_r[:, t, :], xs[:, at(i + 1, 0), t, :]).then_inc(rln, 1)
                            dve.wait_ge(rln, (i + 1) * 18 + 2)
                        if live(i, 0):
                            dve.wait_ge(rs_ps, i * 8 + s + 1)
                            wait(dve, ro_ps, i * 8 + s - 2)
                            dve.tensor_tensor(ret[:, s % 3, :], bank[s % 2][:, 0:384], dm[:, s, :], ALU.mult).then_inc(ret_ready, 1)
                        if s == 0 and live(i + 1, 0):
                            b, k = i + 1, (i + 1) * 18
                            for t in range(TT):
                                dve.bn_aggr(mv_r[:, t, :], six_r[:, t, :]).then_inc(rln, 1)
                            dve.wait_ge(rln, k + 4)
                            rsqrt(rs["rln"], mv_r[:, :, 1], 1.0, LN_EPS, rln, k + 4)
                            wait(dve, rT_ps, b)
                            for t in range(TT):
                                dve.tensor_scalar(s_nat[:, t, :], xs[:, at(b, 0), t, :], mv_r[:, t, 0:1],
                                                  rs["rln"]["y"][:, t:t + 1].bitcast(FP32), ALU.subtract, ALU.mult).then_inc(rln, 1)
                        if s == 2 and live(i + 1, 0):
                            b = i + 1
                            dve.wait_ge(rqk_ps, b + 1)
                            wait(dve, rqk_ready, b)
                            dve.tensor_tensor(rot_a, bank[4][:].rearrange("p (a t) -> p a t", a=2), cosT[:], ALU.mult).then_inc(rot_ready, 1)
                            dve.tensor_tensor(rot_b, bank[5][:].rearrange("p (a t) -> p a t", a=2), sinT[:], ALU.mult).then_inc(rot_ready, 1)
                        if s == 5 and live(i + 1, 0):
                            b = i + 1
                            dve.wait_ge(rhi_ready, b + 1)
                            wait(dve, rex_ps, b * 4)
                            dve.tensor_tensor(qk_lo[:], qk[:], qk_hi[:].bitcast(FP32), ALU.subtract).then_inc(rlo_ready, 1)
                        if s == 4 and live(i + 1, 0):
                            b = i + 1
                            dve.wait_ge(th_ready, b + 1)
                            dve.scalar_tensor_tensor(wide_buf[:, at(b, 0), :, :], tanh_z, 1.0, bank[7][:].rearrange("p (t v) -> p t v", t=TT),
                                                     ALU.add, ALU.mult).then_inc(gz_ready, 1)
                        if s == 3 and live(i - 1, 0):
                            b, k = i - 1, (i - 1) * 15
                            dve.wait_ge(sq_ready, b + 1)
                            wait(dve, gn, k)
                            dve.tensor_reduce(ssq[:], sq.rearrange("p (n v) -> p n v", v=RV), AX.X, ALU.add).then_inc(gn, 1)
                            dve.wait_ge(gn, k + 1)
                            rsqrt(rs["gn"], ssq[:], 1.0 / RV, GN_EPS, gn, k + 1)
                            wait(dve, yr_ready, b)
                            for t in range(TT):
                                dve.tensor_tensor(nrm[:, t, :].rearrange("p (n v) -> p n v", v=RV),
                                                  bank[4][:, t * SEQ:(t + 1) * SEQ].rearrange("p (n v) -> p n v", v=RV),
                                                  rs["gn"]["y"][:, 8 * t:8 * t + 8].bitcast(FP32).unsqueeze(2).to_broadcast([P, 8, RV]),
                                                  ALU.mult).then_inc(gn, 1)
                        if s == 7 and live(i - 1, 0):
                            dve.wait_ge(pr_ps, i)
                            xb = xs[:, at(i - 1, 0), :, :]
                            dve.tensor_tensor(xb, bank[7][:, 0:SEQ].rearrange("p (a t d) -> p a t d", a=1, t=TT), xb, ALU.add).then_inc(xr_done, 1)

                r_iterations(dve, body)

            phase(0)
            retention()
            dve.wait_ge(xr_done, BATCH)
            phase(BATCH)

        @block.gpsimd
        def _(pool):
            pool.memset(ones_wide[:], 1.0)
            pool.memset(v_st[:].rearrange("p t n -> p (t n)"), 0.0).then_inc(set_pool, 1)
            pool.wait_ge(set_pool, 1)
            for start in (64, 1024):
                for t in range(TT):
                    ones = v_st[:, t, start:start + 8 * 136].rearrange("p (h c) -> p h c", c=136)[:, :, 0:HD]
                    last = pool.memset(ones, 1.0)
            last.then_inc(set_pool, 1)
            pool.wait_ge(ld_w, N_LDW)
            for n in (4, 5):
                last = pool.tensor_scalar(vecs[:, n, :], vecs[:, n, :], 0.5, 0.0, ALU.mult, ALU.add)
            last.then_inc(set_pool, 1)
            pool.wait_ge(set_pool, 3)

            def wide(v):
                return v.unsqueeze(1).to_broadcast([P, TT, P])

            def round_wide(dst, src):
                pool.tensor_tensor(dst[:, :, 0:1], src[:, :, 0:1], ones_wide[:, 0:2, 0:1], ALU.mult)
                return pool.tensor_scalar(dst[:, :, 1:SEQ], src[:, :, 1:SEQ], 1.0, 0.0, ALU.mult, ALU.add)

            def add_bo(b, base):
                pool.wait_ge(prep_ln, b * 9 + 9)
                pool.tensor_tensor(resid[:, at(b, base), :, :], s_nat[:], wide(bo_b), ALU.add).then_inc(resid_ready, 1)

            def round_qk(b):
                pool.wait_ge(qk_ready, b * 2 + 2)
                wait(pool, ex_ps, b * 4)
                round_wide(qk_hi, qk[:]).then_inc(hi_ready, 1)

            def place_v(b, half):
                if half == 0:
                    pool.wait_ge(v_ready, b + 1)
                wait(pool, pv_done, (b - 1) * NH + 8 + 8 * half)
                start = 1088 * half
                for t in range(TT):
                    dst = v_st[:, t, start:start + 8 * 136].rearrange("p (h c) -> p h c", c=136)[:, :, 0:HD]
                    src = v_nat[:, t, 64 * half:64 * half + 64].rearrange("p (h d) -> p h d", h=8)
                    pool.tensor_tensor(dst, src, ones_wide[:], ALU.mult).then_inc((va_ready, vb_ready)[half], 1)

            def make_x1(b):
                pool.wait_ge(ln1, b * 9 + 9)
                wait(pool, x1_ready, b * 2)
                pool.tensor_tensor(xt1[:], n1[:], wide(g1_b), ALU.mult).then_inc(x1_ready, 1)
                pool.wait_ge(x1_ready, b * 2 + 1)
                wait(pool, x1T_ps, b)
                wait(pool, router, b * 8)
                wait(pool, y_done, (b - 1) * 8 + 2)
                pool.tensor_tensor(x1[:], xt1[:], wide(b1_b), ALU.add).then_inc(x1_ready, 1)

            def make_x(b, base):
                pool.wait_ge(ln2, b * 9 + 9)
                pool.tensor_tensor(xt2[:, 0], n2[:], wide(g2_b), ALU.mult).then_inc(x_done, 1)
                pool.wait_ge(x_done, b * 3 + 1)
                pool.tensor_tensor(xt2[:, 1], xt2[:, 0], wide(b2_b), ALU.add).then_inc(x_done, 1)
                pool.wait_ge(x_done, b * 3 + 2)
                xb = xs[:, at(b, base), :, :]
                pool.tensor_tensor(xb, xb, xt2[:, 1], ALU.add).then_inc(x_done, 1)

            def phase(base):
                def body(i):
                    if live(i, base):
                        place_v(i, 0)
                    if live(i + 1, base):
                        add_bo(i + 1, base)
                    if live(i - 3, base):
                        make_x(i - 3, base)
                    if live(i, base):
                        place_v(i, 1)
                    if live(i + 1, base):
                        round_qk(i + 1)
                    if live(i - 1, base):
                        make_x1(i - 1)

                iterations(pool, base, body)

            def retention():
                pool.wait_ge(x_done, 3 * BATCH)

                def body(i):
                    if live(i, 0):
                        pool.wait_ge(rv_ready, i + 1)
                        wait(pool, ro_ps, i * 8)
                        round_wide(v_ret[:, 0, :, :], v_ret[:, 1, :, :]).then_inc(vcopy, 1)
                    if live(i + 1, 0):
                        b = i + 1
                        pool.wait_ge(rot_ready, b * 2 + 2)
                        wait(pool, rhi_ready, b)
                        wait(pool, rlo_ready, b)
                        pool.tensor_tensor(qk[:], rot_a, rot_b, ALU.add).then_inc(rqk_ready, 1)
                        pool.wait_ge(rqk_ready, b + 1)
                        wait(pool, rex_ps, b * 4)
                        round_wide(qk_hi, qk[:]).then_inc(rhi_ready, 1)
                    if live(i - 1, 0):
                        b = i - 1
                        pool.wait_ge(gn, b * 15 + 15)
                        pool.wait_ge(gz_ready, b + 1)
                        wait(pool, yT_ps, b)
                        pool.tensor_tensor(y_ret, nrm, wide_buf[:, at(b, 0), :, :], ALU.mult).then_inc(yr_ready, 1)

                r_iterations(pool, body)

            phase(0)
            retention()
            pool.wait_ge(xr_done, BATCH)
            phase(BATCH)



INPUTS = {
    "L0_attn_hidden_states": "x", "L0_attn_W_qkv": "W_qkv", "L0_attn_W_g": "W_g", "L0_attn_W_proj": "W_proj",
    "L0_attn_decay": "decay", "L0_ffn_Wq": "Wq", "L0_ffn_bq": "bq", "L0_ffn_Wk": "Wk", "L0_ffn_bk": "bk",
    "L0_ffn_Wv": "Wv", "L0_ffn_bv": "bv", "L0_ffn_Wo": "Wo", "L0_ffn_bo": "bo", "L0_ffn_router_w": "router_w",
    "L0_ffn_router_b": "router_b", "L0_ffn_W1": "W1", "L0_ffn_b1": "b1", "L0_ffn_W2": "W2", "L0_ffn_b2": "b2",
    "L0_ffn_ln1_g": "ln1_g", "L0_ffn_ln1_b": "ln1_b", "L0_ffn_ln2_g": "ln2_g", "L0_ffn_ln2_b": "ln2_b",
}


def kernel(**inputs):
    import concourse.bacc as bacc
    from concourse.bass_utils import run_bass_kernel_spmd

    nc = bacc.Bacc("TRN2", target_bir_lowering=False, num_devices=1)
    arrays, aps = {}, {}
    given = {short: np.ascontiguousarray(inputs[name]) for name, short in INPUTS.items()}
    for name, a in {**given, **constants()}.items():
        arrays[f"in_{name}"] = a
        aps[name] = nc.dram_tensor(f"in_{name}", a.shape, mybir.dt.from_np(a.dtype), kind="ExternalInput").ap()
    aps["out"] = nc.dram_tensor("out", (BATCH, SEQ, DM), FP32, kind="ExternalOutput").ap()
    build(nc, aps)
    r = run_bass_kernel_spmd(nc, [arrays], core_ids=[0])
    return r.results[0]["out"]
```

```python
import numpy as np
import concourse.bass as bass
from concourse import mybir
from contextlib import ExitStack

FP32 = mybir.dt.float32
FP32R = mybir.dt.float32r
INT32 = mybir.dt.int32
ALU = mybir.AluOpType
ACT = mybir.ActivationFunctionType
AX = mybir.AxisListType

P = 128
BATCH, SEQ, DM = 16, 256, 128
TT = SEQ // P
LN_EPS = 1e-5

NH, HD = 16, 8
GROUPS, GH = 4, 4
NE, DFF = 4, 512
CHUNKS = NE * DFF // P
CPE = DFF // P
SCALE = HD ** -0.5

RH, RK, RV, RGROUPS = 8, 16, 32, 4
QK_DIM, V_DIM, SCALE_BASE, GN_EPS = 128, 256, 512.0, 1e-5
MAGIC = 0x5F3759DF

UP_AT, DOWN_AT = 5, 7
SLOTS = 16
LOW_ON_POOL = [0, 2, 4, 5, 6, 8, 9, 10, 12, 14, 15]
LOW_ON_DVE = [h for h in range(NH) if h not in LOW_ON_POOL]
VROW = NH * P


def ffn_selectors():
    sel = np.zeros((P, GROUPS, 4, P), np.float32)
    for g in range(GROUPS):
        for j in range(GH):
            for d in range(HD):
                p = (g * GH + j) * HD + d
                for kind, parts in enumerate(((0, 1), (2,), (0, 2), (1,))):
                    for part in parts:
                        sel[p, g, kind, 32 * j + HD * part + d] = 1.0
    return sel.reshape(P, -1)


def attention_selector():
    sel = np.zeros((P, GH * HD + GH), np.float32)
    for j in range(GH):
        for d in range(HD):
            sel[32 * j + d, HD * j + d] = sel[32 * j + HD + d, HD * j + d] = 1.0
        sel[32 * j + 2 * HD, GH * HD + j] = 1.0
    return sel


def retention_selectors():
    sel = np.zeros((P, RGROUPS, 4, P), np.float32)
    for g in range(RGROUPS):
        for j in range(2):
            for d in range(RK):
                p = (2 * g + j) * RK + d
                for kind, parts in enumerate(((0, 1), (2, 3), (0, 2), (1, 3))):
                    for part in parts:
                        sel[p, g, kind, 64 * j + RK * part + d] = 1.0
    return sel.reshape(P, -1)


def rotary_tables():
    f = np.float32
    half = QK_DIM // 2
    base = (np.arange(0, QK_DIM, 2, dtype=f) + f(0.4 * QK_DIM)) / f(1.4 * QK_DIM)
    pos = np.arange(SEQ, dtype=f)
    scale = base[None, :] ** (pos[:, None] / f(SCALE_BASE))
    inv_freq = f(1.0) / f(10000.0) ** (np.arange(half, dtype=f) / f(half))
    angle = pos[:, None] * inv_freq[None, :]
    sin, cos = np.sin(angle), np.cos(angle)
    sign = np.tile(np.array([-1.0, 1.0], f), half)[:, None]
    out = []
    for s in (scale, f(1.0) / scale):
        out.append((np.repeat(cos * s, 2, 1).T, np.repeat(sin * s, 2, 1).T * sign))
    return (np.ascontiguousarray(np.concatenate([out[0][n], out[1][n]], 1), dtype=f) for n in range(2))


def constants():
    ident = np.eye(P, dtype=np.float32)
    ones_col = np.zeros((P, 1), np.float32)
    for j in range(GH):
        ones_col[32 * j + 3 * HD:32 * j + 3 * HD + 2] = 1.0
    eidx = np.tile(np.arange(NE, dtype=np.float32), TT)[None].repeat(P, 0)
    cos, sin = rotary_tables()
    return {"c_cos": cos, "c_sin": sin, "c_sel_ret": retention_selectors(), "c_ident": ident, "c_ones_col": ones_col, "c_eidx": eidx, "c_sel_att": attention_selector(), "c_sel_ffn": ffn_selectors()}


def wait(eng, sem, value):
    if isinstance(value, int) and value <= 0:
        return
    eng.wait_ge(sem, value)


def build(nc, A):
    ctx = ExitStack()
    with ctx:
        def sb(name, shape, dt=FP32):
            return ctx.enter_context(nc.sbuf_tensor(name, shape, dt))

        def sem(name):
            return ctx.enter_context(nc.semaphore(name))

        xs = sb("xs", [P, BATCH, TT, DM])
        wide_buf = sb("wide_buf", [P, BATCH, 2, SEQ])
        resid = wide_buf[:, :, 0, :].rearrange("p b (t d) -> p b t d", t=TT)
        stage = wide_buf[:].rearrange("p b a t -> p (b a t)")[:, 0:4096]
        p_split = sb("p_split", [P, 2, 4, TT, SEQ], FP32R)
        ident = sb("ident", [P, P])
        ident_r = sb("ident_r", [P, P], FP32R)
        sel_r = sb("sel_r", [P, GROUPS, 4, P], FP32R)
        ones_col = sb("ones_col", [P, 1])
        eidx = sb("eidx", [P, TT, NE])
        wq = sb("wq", [P, P]); wk = sb("wk", [P, P]); wv = sb("wv", [P, P]); wo = sb("wo", [P, P])
        w1_hi = sb("w1_hi", [P, CHUNKS, P], FP32R)
        w1_lo = sb("w1_lo", [P, CHUNKS, P], FP32R)
        w2 = sb("w2", [P, CHUNKS, P])
        dm = sb("dm", [P, RH, 384])
        dm_flat = dm[:].rearrange("p h n -> p (h n)")
        bias_rows = dm_flat[0:CHUNKS + 2, 2048:2176]
        bias_cols = sb("bias_cols", [P, CHUNKS + 2])
        vecs = sb("vecs", [P, 7, P])
        bv_b, bo_b, g1_b, b1_b, g2_b, b2_b, rw_b = (vecs[:, n, :] for n in range(7))
        rb_b = sb("rb_b", [P, 1])
        b2row = dm_flat[0:1, 2176:2688].rearrange("a (e d) -> a e d", e=NE)
        b2_r = sb("b2_r", [64, NE, P], FP32R)
        ones_r = sb("ones_r", [64, P], FP32R)
        eps_col = sb("eps_col", [P, 1])

        s_nat = sb("s_nat", [P, TT, DM])
        sT = sb("sT", [P, SEQ])
        qk = sb("qk", [P, 2, SEQ])
        qk_hi = sb("qk_hi", [P, 2, SEQ], FP32R)
        qk_lo = sb("qk_lo", [P, 2, SEQ], FP32R)
        stacks = sb("stacks", [P, 2 * GROUPS * SEQ], FP32R)
        q_st, k_st = (stacks[:, n * GROUPS * SEQ:(n + 1) * GROUPS * SEQ].rearrange("p (g t) -> p g t", g=GROUPS) for n in range(2))
        q2_st = sb("q2_st", [P, GROUPS, SEQ], FP32R)
        negmax = sb("negmax", [P, 2, TT, GH])
        mx = sb("mx", [P, TT, P], FP32R)
        probs = sb("probs", [P, 4, TT, SEQ])
        ones_wide = sb("ones_wide", [P, 8, HD])
        v_nat = sb("v_nat", [P, TT, P])
        v_st = sb("v_st", [P, TT, VROW], FP32R)
        p_hi, p_lo = p_split[:, 0], p_split[:, 1]
        att_un = sb("att_un", [P, GROUPS, SEQ])
        sel_att = sb("sel_att", [P, GH * HD + GH])
        rsum = sb("rsum", [P, TT * GROUPS, GH])
        att_pair = sb("att_pair", [P, 2, SEQ])
        att, attT = att_pair[:, 0, :].rearrange("p (t d) -> p t d", t=TT), att_pair[:, 1, :]
        token_bufs = sb("token_bufs", [P, 9, TT, DM])
        y1, n1, x1, xt1, rprod, acc, n2 = (token_bufs[:, n] for n in range(7))
        xt2 = token_bufs[:, 7:9]
        x1_hi = sb("x1_hi", [P, SEQ], FP32R)
        x1_lo = sb("x1_lo", [P, SEQ], FP32R)
        rkey = sb("rkey", [P, 2, TT])
        rint = sb("rint", [P, 4, TT], INT32)
        masks = sb("masks", [P, BATCH, TT, NE])
        hidden = sb("hidden", [P, 4, SEQ])
        ln_scratch = {}
        for s in ("prep", "ln1", "ln2"):
            ln_scratch[s] = dict(six=sb(f"six_{s}", [P, TT, 6]), mv=sb(f"mv_{s}", [P, TT, 2]),
                                 lnv=sb(f"lnv_{s}", [P, TT]), seed=sb(f"seed_{s}", [P, TT]),
                                 a=sb(f"a_{s}", [P, TT]), c=sb(f"c_{s}", [P, TT]), rstd=sb(f"rstd_{s}", [P, TT]))

        sel2_r = sb("sel2_r", [P, RGROUPS, 4, P], FP32R)
        cosT = sb("cosT", [P, 2, SEQ])
        sinT = sb("sinT", [P, 2, SEQ])
        wqkv = sb("wqkv", [P, 512])
        wqk_sw = sb("wqk_sw", [P, 256])
        wv_mean = sb("wv_mean", [P, RH])
        wv_cen = sb("wv_cen", [P, V_DIM])
        wg = sb("wg", [P, V_DIM])
        wproj = sb("wproj", [P, 2, DM])
        dec = sb("dec", [RH, 8])
        pw = sb("pw", [RH, 256])
        prow = sb("prow", [RH, 384])
        rot_a, rot_b = att_un[:, 0:2, :], att_un[:, 2:4, :]
        token_flat = token_bufs[:].rearrange("p n t d -> p (n t d)")
        r_st = stacks[:].rearrange("p (g a t) -> p g a t", g=RGROUPS, a=2)
        ret = token_flat[:, 0:1536].rearrange("p (n t) -> p n t", n=4)
        v_ret = probs[:, 0:2, :, :]
        tanh_z = token_flat[:, 1536:2048].rearrange("p (t v) -> p t v", t=TT)
        outT = hidden[:, 2:4, :]
        sq = att_pair[:].rearrange("p a t -> p (a t)")
        ssq = sb("ssq", [P, 16])
        nrm = probs[:, 2, :, :]
        y_ret = probs[:, 3, :, :]
        yT = hidden[:, 0:2, :]
        rs = {}
        for s_, n_ in (("rln", TT), ("gn", 16)):
            rs[s_] = dict(v=sb(f"v_{s_}", [P, n_]), i=sb(f"i_{s_}", [P, n_], INT32), y=sb(f"y_{s_}", [P, n_], INT32),
                          a=sb(f"ra_{s_}", [P, n_]), c=sb(f"rc_{s_}", [P, n_]))
        six_r = sb("six_r", [P, TT, 6])
        mv_r = sb("mv_r", [P, TT, 2])
        decay_rows = nc.dram_tensor("decay_rows", (RH, P, 513), FP32, kind="Internal").ap()

        bank = [ctx.enter_context(nc.psum_tensor(f"bank{n}", [P, 512], FP32)) for n in range(8)]
        score_bank, prob_bank = bank[0:2], bank[2:4]
        pv_bank, misc, up_bank, y_bank = bank[4], bank[5], bank[6], bank[7]

        ld_x, ld_c, ld_w, ld_e, st_out = sem("ld_x"), sem("ld_c"), sem("ld_w"), sem("ld_e"), sem("st_out")
        set_dve, set_pe, set_act, set_pool = sem("set_dve"), sem("set_pe"), sem("set_act"), sem("set_pool")
        prep_ln, ln1, ln2 = sem("prep_ln"), sem("ln1"), sem("ln2")
        seed = {"prep": sem("seed_prep"), "ln1": sem("seed_ln1"), "ln2": sem("seed_ln2")}
        ln_sem = {"prep": prep_ln, "ln1": ln1, "ln2": ln2}
        sT_ps, sT_ready = sem("sT_ps"), sem("sT_ready")
        qk_ps, qk_ready, hi_ready, lo_ready = sem("qk_ps"), sem("qk_ready"), sem("hi_ready"), sem("lo_ready")
        v_ps, v_ready, va_ready, vb_ready = sem("v_ps"), sem("v_ready"), sem("va_ready"), sem("vb_ready")
        resid_ready = sem("resid_ready")
        ex_ps, ex_ready = sem("ex_ps"), sem("ex_ready")
        score_ps, max_done = sem("score_ps"), sem("max_done")
        mx_ready, m_ps, q2_ready = sem("mx_ready"), sem("m_ps"), sem("q2_ready")
        prob_ps, exp_done, pv_done = sem("prob_ps"), sem("exp_done"), sem("pv_done")
        plo_pool, plo_dve = sem("plo_pool"), sem("plo_dve")
        un_ready, att_ps, att_ready = sem("un_ready"), sem("att_ps"), sem("att_ready")
        attT_ps, attT_ready, wo_ps, y1_ready = sem("attT_ps"), sem("attT_ready"), sem("wo_ps"), sem("y1_ready")
        x1_ready, x1T_ps, x1hi_ready, x1lo_ready = sem("x1_ready"), sem("x1T_ps"), sem("x1hi_ready"), sem("x1lo_ready")
        router = sem("router")
        up_ps, h_ready, down_done, y_done = sem("up_ps"), sem("h_ready"), sem("down_done"), sem("y_done")
        x_done = sem("x_done")
        ld_r, ld_d, set_prow, set_scr = sem("ld_r"), sem("ld_d"), sem("set_prow"), sem("set_scr")
        vcopy = sem("vcopy")
        rln, gn = sem("rln"), sem("gn")
        rT_ps, rT_ready = sem("rT_ps"), sem("rT_ready")
        rqk_ps, rot_ready, rqk_ready, rhi_ready, rlo_ready = sem("rqk_ps"), sem("rot_ready"), sem("rqk_ready"), sem("rhi_ready"), sem("rlo_ready")
        rv_ps, rv_ready, z_ps, th_ready, gz_ready = sem("rv_ps"), sem("rv_ready"), sem("z_ps"), sem("th_ready"), sem("gz_ready")
        rex_ps, rex_ready = sem("rex_ps"), sem("rex_ready")
        rs_ps, ret_ready, ro_ps = sem("rs_ps"), sem("ret_ready"), sem("ro_ps")
        oT_ready, on_ps, sq_ready = sem("oT_ready"), sem("on_ps"), sem("sq_ready")
        yr_ready, yT_ps, yT_ready, pr_ps, xr_done = sem("yr_ready"), sem("yT_ps"), sem("yT_ready"), sem("pr_ps"), sem("xr_done")

        block = ctx.enter_context(nc.Block())

        def low_count(h):
            own = LOW_ON_POOL if h in LOW_ON_POOL else LOW_ON_DVE
            return (plo_pool if h in LOW_ON_POOL else plo_dve), len(own), own.index(h) + 1

        def live(b, base):
            return not isinstance(b, int) or base <= b < base + BATCH

        def iterations(eng, base, body):
            for i in range(base - 1, base + 4):
                body(i)
            with eng.Fori(base + 4, base + 15) as i:
                body(i)
            for i in range(base + 15, base + 19):
                body(i)

        def r_iterations(eng, body):
            for i in range(-2, 3):
                body(i)
            with eng.Fori(3, BATCH - 2) as i:
                body(i)
            for i in range(BATCH - 2, BATCH + 2):
                body(i)

        def at(b, base):
            return bass.ds(b - base, 1)

        @block.sync
        def _(sp):
            xv = A["x"].rearrange("b (t p) d -> p b t d", p=P)
            sp.dma_start(xs[:], xv).then_inc(ld_x, 16)
            sp.dma_start(stage[:, 0:2048], A["c_sel_ffn"]).then_inc(ld_c, 16)
            sp.dma_start(ident[:], A["c_ident"]).then_inc(ld_c, 16)
            sp.dma_start(ones_col[:], A["c_ones_col"]).then_inc(ld_c, 16)
            sp.dma_start(sel_att[:], A["c_sel_att"]).then_inc(ld_c, 16)
            sp.dma_start(eidx[:].rearrange("p t e -> p (t e)"), A["c_eidx"]).then_inc(ld_c, 16)
            for w, name in ((wq, "Wq"), (wk, "Wk"), (wv, "Wv"), (wo, "Wo")):
                sp.dma_start(w[:], A[name]).then_inc(ld_w, 16)
            sp.dma_start(bias_rows[0:CHUNKS, :], A["b1"].rearrange("e (c p) -> (e c) p", p=P)).then_inc(ld_w, 16)
            sp.dma_start(bias_rows[CHUNKS:CHUNKS + 1, :], A["bq"].rearrange("(a n) -> a n", a=1)).then_inc(ld_w, 16)
            sp.dma_start(bias_rows[CHUNKS + 1:CHUNKS + 2, :], A["bk"].rearrange("(a n) -> a n", a=1)).then_inc(ld_w, 16)
            for n, name in enumerate(("bv", "bo", "ln1_g", "ln1_b", "ln2_g", "ln2_b")):
                sp.dma_start(vecs[:, n, :], A[name].partition_broadcast(P)).then_inc(ld_w, 16)
            sp.dma_start(vecs[:, 6, :], A["router_w"].rearrange("d o -> (d o)").partition_broadcast(P)).then_inc(ld_w, 16)
            sp.dma_start(rb_b[:], A["router_b"].partition_broadcast(P)).then_inc(ld_w, 16)
            sp.dma_start(b2row.rearrange("a e d -> a (e d)"), A["b2"].rearrange("(a e) d -> a (e d)", a=1)).then_inc(ld_w, 16)
            sp.dma_start(stage[:, 2048:4096].rearrange("p (e n) -> p e n", e=NE), A["W1"].rearrange("e d n -> d e n")).then_inc(ld_e, 16)
            sp.dma_start(w2[:].rearrange("p (e c) n -> p e c n", e=NE), A["W2"].rearrange("e (c p) n -> p e c n", p=P)).then_inc(ld_e, 16)
            sp.dma_start(dm_flat[:, 0:2048], A["c_sel_ret"]).then_inc(ld_r, 16)
            sp.dma_start(cosT[:].rearrange("p a t -> p (a t)"), A["c_cos"]).then_inc(ld_r, 16)
            sp.dma_start(sinT[:].rearrange("p a t -> p (a t)"), A["c_sin"]).then_inc(ld_r, 16)
            sp.dma_start(wqkv[:], A["W_qkv"]).then_inc(ld_r, 16)
            sp.dma_start(wg[:], A["W_g"]).then_inc(ld_r, 16)
            sp.dma_start(wproj[:], A["W_proj"].rearrange("(a p) d -> p a d", p=P)).then_inc(ld_r, 16)
            sp.dma_start(dec[:, 0:1], A["decay"].rearrange("(h a) -> h a", a=1)).then_inc(ld_r, 16)
            sp.wait_ge(set_pe, 1)
            sp.wait_ge(set_prow, 1)
            sp.dma_start(decay_rows[:, :, 0:384], prow[:].unsqueeze(1).to_broadcast([RH, P, 384])).then_inc(set_scr, 16)
            sp.wait_ge(set_scr, 16)
            for n, width in ((0, 256), (256, 128)):
                moved = bass.AP(tensor=decay_rows.tensor, offset=P, ap=[[512, P], [P * 513, RH], [1, width]])
                sp.dma_start(dm[:, :, n:n + width], moved).then_inc(ld_d, 16)
            ov = A["out"].rearrange("b (t p) d -> p b t d", p=P)
            with sp.Fori(0, BATCH) as i:
                sp.wait_ge(x_done, i * 3 + 3 * BATCH + 3)
                sp.dma_start(ov[:, bass.ds(i, 1), :, :], xs[:, bass.ds(i, 1), :, :]).then_inc(st_out, 16)
            sp.wait_ge(st_out, 16 * BATCH)

        N_LDC, N_LDW = 5 * 16, 16 * 16
        SET_DVE = 31

        @block.tensor
        def _(pe):
            turn = {}

            def take_misc(consumer, value):
                wait(pe, *turn["last"])
                turn["last"] = (consumer, value)

            pe.wait_ge(ld_w, N_LDW)
            pe.wait_ge(ld_c, N_LDC)
            pe.transpose(misc[:, 0:CHUNKS + 2], bias_rows, ident[0:CHUNKS + 2, 0:CHUNKS + 2]).then_inc(set_pe, 1)
            pe.wait_ge(set_act, 1)
            pe.wait_ge(set_dve, 7)
            pe.wait_ge(set_pool, 2)
            pe.wait_ge(ld_e, 32)

            def transposes(b):
                pe.wait_ge(prep_ln, b * 9 + 9)
                take_misc(sT_ready, b + 1)
                for t in range(TT):
                    last = pe.transpose(misc[:, t * P:(t + 1) * P], s_nat[:, t, :], ident[:])
                last.then_inc(sT_ps, 1)

            def project_qk(b):
                pe.wait_ge(sT_ready, b + 1)
                take_misc(qk_ready, b * 2 + 2)
                pe.matmul(misc[:, 0:SEQ], wq[:], sT[:], start=True, stop=True)
                pe.matmul(misc[:, SEQ:2 * SEQ], wk[:], sT[:], start=True, stop=True).then_inc(qk_ps, 1)

            def project_v(b):
                take_misc(v_ready, b + 1)
                for t in range(TT):
                    last = pe.matmul(misc[:, t * P:(t + 1) * P], sT[:, t * P:(t + 1) * P], wv[:], start=True, stop=True)
                last.then_inc(v_ps, 1)

            def expand(b, g):
                if g == 0:
                    pe.wait_ge(hi_ready, b + 1)
                    pe.wait_ge(lo_ready, b + 1)
                take_misc(ex_ready, b * 8 + 2 * g + 2)
                for n in range(2):
                    o = misc[:, n * SEQ:(n + 1) * SEQ]
                    pe.matmul(o, sel_r[:, g, 2 * n, :], qk_hi[:, n, :], start=True, stop=False)
                    last = pe.matmul(o, sel_r[:, g, 2 * n + 1, :], qk_lo[:, n, :], start=False, stop=True)
                last.then_inc(ex_ps, 1)

            def score(b, h):
                g, r = h // GH, 32 * (h % GH)
                if h % GH == 0:
                    pe.wait_ge(ex_ready, b * 8 + 2 * g + 2)
                wait(pe, max_done, b * NH + (h - 1))
                for t in range(TT):
                    last = pe.matmul(score_bank[h % 2][:, t * SEQ:(t + 1) * SEQ], q_st[r:r + 32, g, t * P:(t + 1) * P],
                                     k_st[r:r + 32, g, :], start=True, stop=True)
                last.then_inc(score_ps, 1)

            def spread_max(b, g):
                pe.wait_ge(mx_ready, b * 8 + 2 * g + 2)
                take_misc(q2_ready, b * 4 + g + 1)
                for t in range(TT):
                    last = pe.matmul(misc[:, t * P:(t + 1) * P], mx[:, t, :], ident_r[:], start=True, stop=True)
                last.then_inc(m_ps, 1)

            def shifted_score(b, h):
                g, r = h // GH, 32 * (h % GH)
                if h % GH == 0:
                    pe.wait_ge(q2_ready, b * 4 + g + 1)
                wait(pe, exp_done, b * NH + (h - 1))
                for t in range(TT):
                    last = pe.matmul(prob_bank[h % 2][:, t * SEQ:(t + 1) * SEQ], k_st[r:r + 32, g, t * P:(t + 1) * P],
                                     q2_st[r:r + 32, g, :], start=True, stop=True)
                last.then_inc(prob_ps, 1)

            def weigh_values(b, h):
                pe.wait_ge(exp_done, b * NH + h + 1)
                if h == 0:
                    pe.wait_ge(va_ready, b * 2 + 2)
                    wait(pe, un_ready, b * 2)
                if h == NH // 2:
                    pe.wait_ge(vb_ready, b * 2 + 2)
                    pe.wait_ge(un_ready, b * 2 + 1)
                g, j = h // GH, h % GH
                o = pv_bank[:, (g % 2) * SEQ:(g % 2 + 1) * SEQ]
                w = h * P - 32 * j
                for t in range(TT):
                    pe.matmul(o, v_st[:, t, w:w + P], p_hi[:, h % 4, t, :], start=(j == 0 and t == 0), stop=False)
                engine, per_batch, count = low_count(h)
                pe.wait_ge(engine, b * per_batch + count)
                for t in range(TT):
                    last = pe.matmul(o, v_st[:, t, w:w + P], p_lo[:, h % 4, t, :], start=False,
                                     stop=(j == GH - 1 and t == TT - 1))
                last.then_inc(pv_done, 1)

            def att_to_tokens(b):
                pe.wait_ge(un_ready, b * 2 + 2)
                take_misc(att_ready, b * 2 + 2)
                n = GH * HD + GH
                for t in range(TT):
                    for g in range(GROUPS):
                        last = pe.matmul(misc[:, (GROUPS * t + g) * n:(GROUPS * t + g + 1) * n],
                                         att_un[:, g, t * P:(t + 1) * P], sel_att[:], start=True, stop=True)
                last.then_inc(att_ps, 1)

            def att_to_dims(b):
                pe.wait_ge(att_ready, b * 2 + 2)
                take_misc(attT_ready, b + 1)
                for t in range(TT):
                    last = pe.transpose(misc[:, t * P:(t + 1) * P], att[:, t, :], ident[:])
                last.then_inc(attT_ps, 1)

            def project_out(b):
                pe.wait_ge(attT_ready, b + 1)
                take_misc(y1_ready, b + 1)
                for t in range(TT):
                    last = pe.matmul(misc[:, t * P:(t + 1) * P], attT[:, t * P:(t + 1) * P], wo[:], start=True, stop=True)
                last.then_inc(wo_ps, 1)

            def x1_to_dims(b):
                pe.wait_ge(x1_ready, b * 2 + 2)
                take_misc(x1lo_ready, b + 1)
                for t in range(TT):
                    last = pe.transpose(misc[:, t * P:(t + 1) * P], x1[:, t, :], ident[:])
                last.then_inc(x1T_ps, 1)

            def up(b, c):
                if c == 0:
                    pe.wait_ge(x1lo_ready, b + 1)
                wait(pe, h_ready, b * CHUNKS + c)
                o = up_bank[:, 0:SEQ]
                pe.matmul(o, w1_lo[:, c, :], x1_hi[:], start=True, stop=False)
                pe.matmul(o, w1_hi[:, c, :], x1_lo[:], start=False, stop=False)
                pe.matmul(o, w1_hi[:, c, :], x1_hi[:], start=False, stop=True).then_inc(up_ps, 1)

            def down(b, c):
                e, first, final = c // CPE, c % CPE == 0, c % CPE == CPE - 1
                pe.wait_ge(h_ready, b * CHUNKS + c + 1)
                if first:
                    wait(pe, y_done, b * 8 + 2 * e)
                    for t in range(TT):
                        pe.matmul(y_bank[:, t * P:(t + 1) * P], ones_r[:], b2_r[:, e, :], start=(t == 0), stop=False,
                                  skip_group_check=True)
                for t in range(TT):
                    last = pe.matmul(y_bank[:, t * P:(t + 1) * P], hidden[:, c % 4, t * P:(t + 1) * P], w2[:, c, :],
                                     start=False, stop=final, skip_group_check=True)
                last.then_inc(down_done, 1)

            def phase(base):
                turn["last"] = (set_act, 1)

                def body(i):
                    if live(i - 2, base):
                        turn["last"] = (y1_ready, i - 2 + 1)
                    for s in range(SLOTS):
                        bu, cu = (i - 2, s - UP_AT) if s >= UP_AT else (i - 3, s + SLOTS - UP_AT)
                        bs, hs = (i, s - 6) if s >= 6 else (i - 1, s + SLOTS - 6)
                        bd, cd = (i - 2, s - DOWN_AT) if s >= DOWN_AT else (i - 3, s + SLOTS - DOWN_AT)
                        bw, hw = (i, s - 8) if s >= 8 else (i - 1, s + SLOTS - 8)
                        if live(bu, base):
                            up(bu, cu)
                        if live(i, base):
                            score(i, s)
                        if live(bs, base):
                            shifted_score(bs, hs)
                        if live(bd, base):
                            down(bd, cd)
                        if live(bw, base):
                            weigh_values(bw, hw)
                        if s == 0 and live(i - 1, base):
                            spread_max(i - 1, 3)
                        if s in (4, 8, 12) and live(i, base):
                            spread_max(i, s // 4 - 1)
                        if s in (2, 6, 10) and live(i, base):
                            expand(i, s // 4 + 1)
                        if s == 14 and live(i + 1, base):
                            expand(i + 1, 0)
                        if s == 3 and live(i - 2, base):
                            x1_to_dims(i - 2)
                        if s == 7 and live(i + 1, base):
                            transposes(i + 1)
                        if s == 9 and live(i + 1, base):
                            project_qk(i + 1)
                        if s == 1 and live(i, base):
                            project_v(i)
                        if s == 11 and live(i - 1, base):
                            att_to_tokens(i - 1)
                        if s == 13 and live(i - 1, base):
                            att_to_dims(i - 1)
                        if s == 15 and live(i - 1, base):
                            project_out(i - 1)

                iterations(pe, base, body)

            def retention():
                pe.wait_ge(x_done, 3 * BATCH)
                pe.wait_ge(ld_r, 7 * 16)
                pe.wait_ge(set_dve, SET_DVE)
                last7, last4 = {}, {}

                def take(which, consumer, value):
                    if "last" in which:
                        wait(pe, *which["last"])
                    which["last"] = (consumer, value)

                def body(i):
                    if live(i, 0):
                        last7["last"] = (gz_ready, i + 1)
                    if live(i - 2, 0):
                        last4["last"] = (gn, (i - 1) * 15)
                    for s in range(8):
                        if live(i, 0):
                            h, r, g = s, 64 * (s % 2), s // 2
                            if h % 2 == 0:
                                pe.wait_ge(rex_ready, i * 4 + g + 1)
                            wait(pe, ret_ready, i * 8 + h - 1)
                            ps = bank[h % 2]
                            pe.matmul(ps[:, 0:256], r_st[r:r + 64, g, 1, 0:P], r_st[r:r + 64, g, 0, :], start=True, stop=True)
                            pe.matmul(ps[:, 256:384], r_st[r:r + 64, g, 1, P:2 * P], r_st[r:r + 64, g, 0, P:2 * P],
                                      start=True, stop=True).then_inc(rs_ps, 1)
                        be, ge = (i, s + 1) if s in (0, 1, 2) else (i + 1, 0)
                        if s in (0, 1, 2, 6) and live(be, 0):
                            if ge == 0:
                                pe.wait_ge(rlo_ready, be + 1)
                            wait(pe, rex_ready, be * 4 + ge)
                            for n in range(2):
                                o = bank[6][:, n * SEQ:(n + 1) * SEQ]
                                pe.matmul(o, sel2_r[:, ge, 2 * n, :], qk_hi[:, n, :], start=True, stop=False)
                                last = pe.matmul(o, sel2_r[:, ge, 2 * n + 1, :], qk_lo[:, n, :], start=False, stop=True)
                            last.then_inc(rex_ps, 1)
                        bo, ho = (i, s - 2) if s >= 2 else (i - 1, s + 6)
                        if live(bo, 0):
                            pe.wait_ge(ret_ready, bo * 8 + ho + 1)
                            if ho % 4 == 0:
                                pe.wait_ge(vcopy, bo * 2 + ho // 4 + 1)
                                wait(pe, oT_ready, bo * 2 + ho // 4 - 1)
                            o = bank[2 + ho // 4][32 * (ho % 4):32 * (ho % 4) + 32, 0:SEQ]
                            pe.matmul(o, v_use(bo, 0, ho), ret[:, ho % 4, 0:256], start=True, stop=True)
                            pe.matmul(o[:, P:2 * P], v_use(bo, 1, ho), ret[:, ho % 4, 256:384], start=False, stop=True,
                                      skip_group_check=True).then_inc(ro_ps, 1)
                        if s == 0 and live(i + 1, 0):
                            pe.wait_ge(rln, (i + 1) * 18 + 18)
                            take(last7, rT_ready, i + 2)
                            for t in range(TT):
                                last = pe.transpose(bank[7][:, t * P:(t + 1) * P], s_nat[:, t, :], ident[:])
                            last.then_inc(rT_ps, 1)
                        if s == 1 and live(i + 1, 0):
                            pe.wait_ge(rT_ready, i + 2)
                            take(last4, rot_ready, (i + 1) * 2 + 2)
                            for n in range(2):
                                pe.matmul(bank[4][:, n * SEQ:(n + 1) * SEQ], wqkv[:, n * P:(n + 1) * P], sT[:], start=True, stop=True)
                            for n in range(2):
                                last = pe.matmul(bank[5][:, n * SEQ:(n + 1) * SEQ], wqk_sw[:, n * P:(n + 1) * P], sT[:], start=True, stop=True)
                            last.then_inc(rqk_ps, 1)
                        if s == 1 and live(i - 2, 0):
                            pe.wait_ge(yr_ready, i - 1)
                            take(last7, yT_ready, i - 1)
                            for half in range(2):
                                for t in range(TT):
                                    last = pe.transpose(bank[7][:, (2 * half + t) * P:(2 * half + t + 1) * P],
                                                        y_ret[:, t, half * P:(half + 1) * P], ident[:])
                            last.then_inc(yT_ps, 1)
                        if s == 2 and live(i + 1, 0):
                            take(last7, rv_ready, i + 2)
                            for t in range(TT):
                                last = pe.matmul(bank[7][:, t * SEQ:(t + 1) * SEQ], sT[:, t * P:(t + 1) * P], wv_cen[:], start=True, stop=True)
                            last.then_inc(rv_ps, 1)
                        if s == 3 and live(i - 2, 0):
                            pe.wait_ge(yT_ready, i - 1)
                            take(last7, xr_done, i - 1)
                            for t in range(TT):
                                for half in range(2):
                                    last = pe.matmul(bank[7][:, t * P:(t + 1) * P], yT[:, half, t * P:(t + 1) * P], wproj[:, half, :],
                                                     start=(half == 0), stop=(half == 1))
                            last.then_inc(pr_ps, 1)
                        if s == 3 and live(i - 1, 0):
                            pe.wait_ge(oT_ready, (i - 1) * 2 + 2)
                            take(last4, gn, (i - 1) * 15 + 15)
                            for t in range(TT):
                                for half in range(2):
                                    last = pe.transpose(bank[4][:, (2 * t + half) * P:(2 * t + half + 1) * P],
                                                        outT[:, half, t * P:(t + 1) * P], ident[:])
                            last.then_inc(on_ps, 1)
                        if s == 5 and live(i + 1, 0):
                            take(last7, gz_ready, i + 2)
                            for t in range(TT):
                                last = pe.matmul(bank[7][:, t * SEQ:(t + 1) * SEQ], sT[:, t * P:(t + 1) * P], wg[:], start=True, stop=True)
                            last.then_inc(z_ps, 1)

                def v_use(b, t, h):
                    return v_ret[:, 0, t, RV * h:RV * h + RV]

                r_iterations(pe, body)

            phase(0)
            retention()
            pe.wait_ge(xr_done, BATCH)
            phase(BATCH)

        @block.scalar
        def _(act):
            act.preload_act_table_set("natural_log_exp_and_others")
            act.wait_ge(set_pe, 1)
            act.activation(bias_cols[:], misc[:, 0:CHUNKS + 2], ACT.Copy).then_inc(set_act, 1)
            act.wait_ge(set_dve, 7)
            act.wait_ge(set_act, 1)

            def seeds(b, which):
                s = ln_scratch[which]
                act.wait_ge(ln_sem[which], b * 9 + 4)
                act.activation(s["lnv"][:], s["mv"][:, :, 1], ACT.Ln, bias=eps_col[:]).then_inc(seed[which], 1)
                act.wait_ge(seed[which], b * 2 + 1)
                act.activation(s["seed"][:], s["lnv"][:], ACT.Exp, scale=-0.5).then_inc(seed[which], 1)

            def out_sT(b):
                act.wait_ge(sT_ps, b + 1)
                wait(act, v_ps, b)
                act.activation(sT[:], misc[:, 0:SEQ], ACT.Copy).then_inc(sT_ready, 1)

            def out_qk(b):
                act.wait_ge(qk_ps, b + 1)
                wait(act, hi_ready, b)
                wait(act, lo_ready, b)
                for n in range(2):
                    act.activation(qk[:, n, :], misc[:, n * SEQ:(n + 1) * SEQ], ACT.Identity,
                                   bias=bias_cols[:, CHUNKS + n:CHUNKS + n + 1]).then_inc(qk_ready, 1)

            def out_expand(b, g):
                act.wait_ge(ex_ps, b * 4 + g + 1)
                wait(act, prob_ps, (b - 1) * NH + 4 * g + 4)
                act.activation(q_st[:, g, :], misc[:, 0:SEQ], ACT.Copy).then_inc(ex_ready, 1)
                act.activation(k_st[:, g, :], misc[:, SEQ:2 * SEQ], ACT.Identity, bias=ones_col[:]).then_inc(ex_ready, 1)

            def exp(b, h):
                act.wait_ge(prob_ps, b * NH + h + 1)
                wait(act, pv_done, b * NH + h - 3)
                shifted = prob_bank[h % 2][:].rearrange("p (t q) -> p t q", t=TT)
                act.activation(probs[:, h % 4, :, :], shifted, ACT.Exp, scale=SCALE)
                act.activation(p_hi[:, h % 4, :, :], shifted, ACT.Exp, scale=SCALE).then_inc(exp_done, 1)

            def out_pv(b, half):
                act.wait_ge(pv_done, b * NH + 8 * half + 8)
                if half == 0:
                    wait(act, att_ps, b)
                act.activation(att_un[:, 2 * half:2 * half + 2, :], pv_bank[:].rearrange("p (a q) -> p a q", a=2),
                               ACT.Copy).then_inc(un_ready, 1)

            def out_attT(b):
                act.wait_ge(attT_ps, b + 1)
                wait(act, wo_ps, b)
                act.activation(attT[:], misc[:, 0:SEQ], ACT.Copy).then_inc(attT_ready, 1)

            def round_x1(b):
                act.wait_ge(x1T_ps, b + 1)
                wait(act, up_ps, b * CHUNKS)
                act.activation(x1_hi[:], misc[:, 0:SEQ], ACT.Copy).then_inc(x1hi_ready, 1)

            def relu(b, c):
                act.wait_ge(up_ps, b * CHUNKS + c + 1)
                wait(act, down_done, b * CHUNKS + c - 3)
                act.activation(hidden[:, c % 4, :], up_bank[:, 0:SEQ], ACT.Relu, bias=bias_cols[:, c:c + 1]).then_inc(h_ready, 1)

            def phase(base):
                def body(i):
                    for s in range(SLOTS):
                        bu, cu = (i - 2, s - UP_AT) if s >= UP_AT else (i - 3, s + SLOTS - UP_AT)
                        bs, hs = (i, s - 6) if s >= 6 else (i - 1, s + SLOTS - 6)
                        if s == 8 and live(i - 1, base):
                            out_pv(i - 1, 1)
                        if s == 0 and live(i - 1, base):
                            out_pv(i - 1, 0)
                        if s in (3, 7, 11) and live(i, base):
                            out_expand(i, s // 4 + 1)
                        if s == 15 and live(i + 1, base):
                            out_expand(i + 1, 0)
                        if s == 8 and live(i + 1, base):
                            out_sT(i + 1)
                        if s == 4 and live(i - 2, base):
                            round_x1(i - 2)
                        if s == 10 and live(i + 1, base):
                            out_qk(i + 1)
                        if s == 14 and live(i - 1, base):
                            out_attT(i - 1)
                        if live(bu, base):
                            relu(bu, cu)
                        if live(bs, base):
                            exp(bs, hs)
                        if s == 1 and live(i - 2, base):
                            seeds(i - 2, "ln1")
                        if s == 2 and live(i + 1, base):
                            seeds(i + 1, "prep")
                        if s == 8 and live(i - 3, base):
                            seeds(i - 3, "ln2")

                iterations(act, base, body)

            def retention():
                act.wait_ge(x_done, 3 * BATCH)

                def body(i):
                    for s in range(8):
                        be, ge = (i, s + 1) if s in (0, 1, 2) else (i + 1, 0)
                        if s == 1 and live(i + 1, 0):
                            act.wait_ge(rT_ps, i + 2)
                            wait(act, z_ps, i + 1)
                            act.activation(sT[:], bank[7][:, 0:SEQ], ACT.Copy).then_inc(rT_ready, 1)
                        if s == 2 and live(i - 2, 0):
                            act.wait_ge(yT_ps, i - 1)
                            wait(act, pr_ps, i - 2)
                            act.activation(yT, bank[7][:].rearrange("p (a t) -> p a t", a=2), ACT.Copy).then_inc(yT_ready, 1)
                        if s in (0, 1, 2, 6) and live(be, 0):
                            act.wait_ge(rex_ps, be * 4 + ge + 1)
                            wait(act, rs_ps, (be - 1) * 8 + 2 * ge + 2)
                            act.activation(r_st[:, ge, :, :], bank[6][:].rearrange("p (a t) -> p a t", a=2), ACT.Copy).then_inc(rex_ready, 1)
                        if s == 2 and live(i - 1, 0):
                            act.wait_ge(ro_ps, (i - 1) * 8 + 8)
                            wait(act, on_ps, i - 1)
                            act.activation(outT[:, 1, :], bank[3][:, 0:SEQ], ACT.Copy).then_inc(oT_ready, 1)
                        if s == 6 and live(i, 0):
                            act.wait_ge(ro_ps, i * 8 + 4)
                            wait(act, on_ps, i)
                            act.activation(outT[:, 0, :], bank[2][:, 0:SEQ], ACT.Copy).then_inc(oT_ready, 1)
                        if s == 3 and live(i + 1, 0):
                            act.wait_ge(rv_ps, i + 2)
                            wait(act, vcopy, (i + 1) * 2)
                            act.activation(v_ret[:, 1, :, :], bank[7][:].rearrange("p (t v) -> p t v", t=TT), ACT.Copy).then_inc(rv_ready, 1)
                        if s == 4 and live(i - 1, 0):
                            act.wait_ge(on_ps, i)
                            wait(act, gn, (i - 2) * 15 + 1)
                            act.activation(sq, bank[4][:], ACT.Square).then_inc(sq_ready, 1)
                        if s == 6 and live(i + 1, 0):
                            act.wait_ge(z_ps, i + 2)
                            wait(act, gz_ready, i + 1)
                            act.activation(tanh_z, bank[7][:].rearrange("p (t v) -> p t v", t=TT), ACT.Tanh, scale=0.5).then_inc(th_ready, 1)

                r_iterations(act, body)

            phase(0)
            retention()
            act.wait_ge(xr_done, BATCH)
            act.preload_act_table_set("natural_log_exp_and_others")
            phase(BATCH)

        @block.vector
        def _(dve):
            dve.memset(mx[:].bitcast(FP32), 0.0).then_inc(set_dve, 1)
            dve.memset(b2_r[:].bitcast(FP32), 0.0).then_inc(set_dve, 1)
            dve.memset(eps_col[:], LN_EPS).then_inc(set_dve, 1)
            dve.memset(ones_r[:].bitcast(FP32), 1.0).then_inc(set_dve, 1)
            dve.wait_ge(ld_c, N_LDC)
            dve.tensor_copy(sel_r[:].rearrange("p g k m -> p (g k m)"), stage[:, 0:2048])
            dve.tensor_copy(ident_r[:], ident[:])
            dve.wait_ge(ld_w, N_LDW)
            dve.wait_ge(set_dve, 2)
            dve.tensor_copy(b2_r[0:1, :, :], b2row)
            dve.wait_ge(ld_e, 32)
            dve.tensor_copy(w1_hi[:].rearrange("p c m -> p (c m)"), stage[:, 2048:4096]).then_inc(set_dve, 1)
            dve.wait_ge(set_dve, 5)
            dve.tensor_tensor(b2_r[32:33, :, :], b2row, b2_r[0:1, :, :].bitcast(FP32), ALU.subtract).then_inc(set_dve, 1)
            dve.tensor_tensor(w1_lo[:].rearrange("p c m -> p (c m)"), stage[:, 2048:4096],
                              w1_hi[:].rearrange("p c m -> p (c m)").bitcast(FP32), ALU.subtract).then_inc(set_dve, 1)
            dve.wait_ge(ld_x, 16)
            dve.memset(pw[:, 0:1], 1.0).then_inc(set_dve, 1)
            dve.memset(prow[:, 0:P], 0.0).then_inc(set_dve, 1)
            dve.wait_ge(ld_r, 7 * 16)
            dve.tensor_copy(sel2_r[:].rearrange("p g k m -> p (g k m)"), dm_flat[:, 0:2048]).then_inc(set_dve, 1)
            for n in range(2):
                dve.tensor_copy(wqk_sw[:].rearrange("p (c a) -> p c a", a=2)[:, :, n],
                                wqkv[:, 0:256].rearrange("p (c a) -> p c a", a=2)[:, :, 1 - n]).then_inc(set_dve, 1)
            wv_heads = wqkv[:, 256:512].rearrange("p (h v) -> p h v", h=RH)
            dve.tensor_reduce(wv_mean[:], wv_heads, AX.X, ALU.add).then_inc(set_dve, 1)
            dve.wait_ge(set_dve, 13)
            dve.tensor_scalar(wv_mean[:], wv_mean[:], -1.0 / RV, None, ALU.mult).then_inc(set_dve, 1)
            dve.wait_ge(set_dve, 14)
            dve.tensor_tensor(wv_cen[:].rearrange("p (h v) -> p h v", h=RH), wv_heads,
                              wv_mean[:].unsqueeze(2).to_broadcast([P, RH, RV]), ALU.add).then_inc(set_dve, 1)
            dve.tensor_scalar(wproj[:], wproj[:], 0.5, None, ALU.mult).then_inc(set_dve, 1)
            count = 16
            for k in range(8):
                w = 1 << k
                dve.tensor_scalar(pw[:, w:2 * w], pw[:, 0:w], dec[:, k:k + 1], None, ALU.mult).then_inc(set_dve, 1)
                if k < 7:
                    dve.tensor_tensor(dec[:, k + 1:k + 2], dec[:, k:k + 1], dec[:, k:k + 1], ALU.mult).then_inc(set_dve, 1)
                count += 2 if k < 7 else 1
                dve.wait_ge(set_dve, count)
            dve.tensor_scalar(prow[:, P:384], pw[:], RK ** -0.5, None, ALU.mult).then_inc(set_prow, 1)

            def layer_norm(b, which, src, dst):
                s, done = ln_scratch[which], ln_sem[which]
                for t in range(TT):
                    dve.bn_stats(s["six"][:, t, :], src(t)).then_inc(done, 1)

            def layer_norm_moments(b, which):
                s, done = ln_scratch[which], ln_sem[which]
                for t in range(TT):
                    dve.bn_aggr(s["mv"][:, t, :], s["six"][:, t, :]).then_inc(done, 1)

            def layer_norm_end(b, which, part, src=None, dst=None):
                s, done = ln_scratch[which], ln_sem[which]
                if part == 0:
                    dve.wait_ge(seed[which], b * 2 + 2)
                    dve.scalar_tensor_tensor(s["a"][:], s["mv"][:, :, 1], LN_EPS, s["seed"][:], ALU.add, ALU.mult).then_inc(done, 1)
                    return
                dve.wait_ge(done, b * 9 + 4 + part)
                if part == 1:
                    dve.scalar_tensor_tensor(s["c"][:], s["a"][:], -0.5, s["seed"][:], ALU.mult, ALU.mult).then_inc(done, 1)
                elif part == 2:
                    dve.scalar_tensor_tensor(s["rstd"][:], s["c"][:], 1.5, s["seed"][:], ALU.add, ALU.mult).then_inc(done, 1)
                else:
                    for t in range(TT):
                        dve.tensor_scalar(dst(t), src(t), s["mv"][:, t, 0:1], s["rstd"][:, t:t + 1], ALU.subtract, ALU.mult)\
                           .then_inc(done, 1)

            def split_qk(b):
                dve.wait_ge(hi_ready, b + 1)
                wait(dve, ex_ps, b * 4)
                dve.tensor_tensor(qk_lo[:], qk[:], qk_hi[:].bitcast(FP32), ALU.subtract).then_inc(lo_ready, 1)

            def out_v(b):
                dve.wait_ge(v_ps, b + 1)
                wait(dve, vb_ready, b * 2)
                wait(dve, va_ready, b * 2)
                dve.tensor_tensor(v_nat[:], misc[:, 0:SEQ].rearrange("p (t d) -> p t d", t=TT),
                                  bv_b.unsqueeze(1).to_broadcast([P, TT, P]), ALU.add).then_inc(v_ready, 1)

            def maximum(b, h):
                g, j = h // GH, h % GH
                dve.wait_ge(score_ps, b * NH + h + 1)
                dve.tensor_reduce(negmax[:, g % 2, :, j], score_bank[h % 2][:].rearrange("p (t k) -> p t k", t=TT),
                                  AX.X, ALU.max, negate=True).then_inc(max_done, 1)

            def split_max(b, g):
                dve.wait_ge(max_done, b * NH + 4 * g + 4)
                wait(dve, m_ps, b * 4 + g)
                rows = mx[:].rearrange("p t (j c) -> p t j c", c=32)
                hi, lo = rows[:, :, :, 3 * HD], rows[:, :, :, 3 * HD + 1]
                dve.tensor_copy(hi, negmax[:, g % 2, :, :]).then_inc(mx_ready, 1)
                dve.wait_ge(mx_ready, b * 8 + 2 * g + 1)
                dve.tensor_tensor(lo, negmax[:, g % 2, :, :], hi.bitcast(FP32), ALU.subtract).then_inc(mx_ready, 1)

            def shift_q(b, g):
                dve.wait_ge(m_ps, b * 4 + g + 1)
                wait(dve, prob_ps, (b - 1) * NH + 4 * g + 4)
                dve.tensor_tensor(q2_st[:, g, :], misc[:, 0:SEQ], q_st[:, g, :].bitcast(FP32), ALU.add).then_inc(q2_ready, 1)

            def normalize(b):
                dve.wait_ge(att_ps, b + 1)
                wait(dve, attT_ps, b)
                m = misc[:, 0:TT * GROUPS * (GH * HD + GH)].rearrange("p (n c) -> p n c", n=TT * GROUPS)
                dve.reciprocal(rsum[:], m[:, :, GH * HD:]).then_inc(att_ready, 1)
                dve.wait_ge(att_ready, b * 2 + 1)
                dve.tensor_tensor(att[:].rearrange("p t (g j d) -> p (t g) j d", g=GROUPS, j=GH),
                                  m[:, :, 0:GH * HD].rearrange("p n (j d) -> p n j d", j=GH),
                                  rsum[:].unsqueeze(3).to_broadcast([P, TT * GROUPS, GH, HD]), ALU.mult).then_inc(att_ready, 1)

            def add_attention(b, base):
                dve.wait_ge(wo_ps, b + 1)
                dve.wait_ge(resid_ready, b + 1)
                dve.tensor_tensor(y1[:], misc[:, 0:SEQ].rearrange("p (t d) -> p t d", t=TT),
                                  resid[:, at(b, base), :, :], ALU.add).then_inc(y1_ready, 1)
                dve.wait_ge(y1_ready, b + 1)

            def split_x1(b):
                dve.wait_ge(x1hi_ready, b + 1)
                wait(dve, up_ps, b * CHUNKS)
                dve.tensor_tensor(x1_lo[:], misc[:, 0:SEQ], x1_hi[:].bitcast(FP32), ALU.subtract).then_inc(x1lo_ready, 1)

            def route(b, base, n):
                if n == 0:
                    dve.wait_ge(x1_ready, b * 2 + 2)
                else:
                    dve.wait_ge(router, b * 8 + n)
                if n == 0:
                    step = dve.tensor_tensor(rprod[:], x1[:], rw_b.unsqueeze(1).to_broadcast([P, TT, P]), ALU.mult)
                elif n == 1:
                    step = dve.tensor_reduce(rkey[:, 0, :], rprod[:], AX.X, ALU.add)
                elif n == 2:
                    step = dve.tensor_scalar(rkey[:, 1, :], rkey[:, 0, :], rb_b[:], None, ALU.add)
                elif n == 3:
                    step = dve.tensor_copy(rint[:, 0, :], rkey[:, 1, :])
                elif n == 4:
                    step = dve.tensor_tensor(rint[:, 1, :], rint[:, 0, :], rkey[:, 1, :], ALU.is_gt)
                elif n == 5:
                    step = dve.tensor_tensor(rint[:, 2, :], rint[:, 0, :], rint[:, 1, :], ALU.subtract)
                elif n == 6:
                    step = dve.tensor_scalar(rint[:, 3, :], rint[:, 2, :], 3, None, ALU.bitwise_and)
                else:
                    step = dve.tensor_tensor(masks[:, at(b, base), :, :],
                                             rint[:, 3, :].unsqueeze(2).to_broadcast([P, TT, NE]), eidx[:], ALU.is_equal)
                step.then_inc(router, 1)

            def add_expert(b, e, base):
                dve.wait_ge(down_done, b * CHUNKS + 4 * e + 4)
                wait(dve, y_done, b * 8 + 2 * e)
                if e == 0:
                    dve.wait_ge(router, b * 8 + 8)
                    wait(dve, ln2, b * 9)
                for t in range(TT):
                    prior = x1 if e == 0 else acc
                    dve.scalar_tensor_tensor(acc[:, t, :], y_bank[:, t * P:(t + 1) * P], masks[:, at(b, base), t, e],
                                             prior[:, t, :], ALU.mult, ALU.add).then_inc(y_done, 1)

            def low_part(b, h):
                dve.wait_ge(exp_done, b * NH + h + 1)
                dve.tensor_tensor(p_lo[:, h % 4, :, :], probs[:, h % 4, :, :], p_hi[:, h % 4, :, :].bitcast(FP32),
                                  ALU.subtract).then_inc(plo_dve, 1)

            def phase(base):
                def body(i):
                    def x_tile(t):
                        return xs[:, at(i + 1, base), t, :]
                    for s in range(SLOTS):
                        if s == 0 and live(i - 1, base):
                            split_max(i - 1, 3)
                        if s in (4, 8, 12) and live(i, base):
                            split_max(i, s // 4 - 1)
                        if s == 1 and live(i - 1, base):
                            shift_q(i - 1, 3)
                        if s in (5, 9, 13) and live(i, base):
                            shift_q(i, s // 4 - 1)
                        if s == 2 and live(i, base):
                            out_v(i)
                        if s in (11, 15) and live(i - 2, base):
                            add_expert(i - 2, (s - 11) // 4, base)
                        if s in (3, 7) and live(i - 3, base):
                            add_expert(i - 3, (s + 5) // 4, base)
                        if s == 4 and live(i - 2, base):
                            split_x1(i - 2)
                        if s == 12 and live(i - 1, base):
                            normalize(i - 1)
                        if s == 0 and live(i - 2, base):
                            add_attention(i - 2, base)
                            layer_norm(i - 2, "ln1", lambda t: y1[:, t, :], None)
                            dve.wait_ge(ln1, (i - 2) * 9 + 2)
                        if s == 1 and live(i + 1, base):
                            wait(dve, sT_ps, i + 1)
                            wait(dve, resid_ready, i + 1)
                            layer_norm(i + 1, "prep", x_tile, None)
                            dve.wait_ge(prep_ln, (i + 1) * 9 + 2)
                        if s == 7 and live(i - 3, base):
                            dve.wait_ge(y_done, (i - 3) * 8 + 8)
                            layer_norm(i - 3, "ln2", lambda t: acc[:, t, :], None)
                            dve.wait_ge(ln2, (i - 3) * 9 + 2)
                        if s == 2 and live(i - 2, base):
                            layer_norm_end(i - 2, "ln1", 0)
                        if s in (5, 6) and live(i + 1, base):
                            layer_norm_end(i + 1, "prep", 2 * s - 10)
                        if s in (9, 10) and live(i - 3, base):
                            layer_norm_end(i - 3, "ln2", 2 * s - 18)
                        if s in (6, 7, 8, 9) and live(i - 2, base):
                            route(i - 2, base, 2 * s - 12)
                        if live(i, base):
                            maximum(i, s)
                        if s == 2 and live(i - 2, base):
                            layer_norm_end(i - 2, "ln1", 1)
                        if s == 5 and live(i + 1, base):
                            layer_norm_end(i + 1, "prep", 1)
                        if s == 9 and live(i - 3, base):
                            layer_norm_end(i - 3, "ln2", 1)
                        if s in (6, 7, 8, 9) and live(i - 2, base):
                            route(i - 2, base, 2 * s - 11)
                        bl, hl = (i, s - 7) if s >= 7 else (i - 1, s + SLOTS - 7)
                        if hl in LOW_ON_DVE and live(bl, base):
                            low_part(bl, hl)
                        if s == 0 and live(i - 2, base):
                            layer_norm_moments(i - 2, "ln1")
                        if s == 1 and live(i + 1, base):
                            layer_norm_moments(i + 1, "prep")
                        if s == 7 and live(i - 3, base):
                            layer_norm_moments(i - 3, "ln2")
                        if s == 2 and live(i - 2, base):
                            layer_norm_end(i - 2, "ln1", 2)
                            wait(dve, x1_ready, (i - 2) * 2)
                            layer_norm_end(i - 2, "ln1", 3, lambda t: y1[:, t, :], lambda t: n1[:, t, :])
                        if s == 6 and live(i + 1, base):
                            layer_norm_end(i + 1, "prep", 3, x_tile, lambda t: s_nat[:, t, :])
                        if s == 10 and live(i - 3, base):
                            wait(dve, x_done, (i - 3) * 3)
                            layer_norm_end(i - 3, "ln2", 3, lambda t: acc[:, t, :], lambda t: n2[:, t, :])
                        if s == 13 and live(i + 1, base):
                            split_qk(i + 1)

                iterations(dve, base, body)

            def retention():
                dve.wait_ge(x_done, 3 * BATCH)
                dve.wait_ge(ld_d, 32)

                def rsqrt_start(s, src, scale, eps, done, k):
                    dve.tensor_scalar(s["v"][:], src, scale, eps, ALU.mult, ALU.add).then_inc(done, 1)
                    dve.wait_ge(done, k + 1)
                    dve.tensor_scalar(s["i"][:], s["v"][:].bitcast(INT32), 1, None, ALU.logical_shift_right).then_inc(done, 1)
                    dve.wait_ge(done, k + 2)
                    dve.tensor_scalar(s["y"][:], s["i"][:], -1.0, float(MAGIC), ALU.mult, ALU.add).then_inc(done, 1)

                def newton(s, done, k):
                    y = s["y"][:].bitcast(FP32)
                    dve.wait_ge(done, k)
                    dve.scalar_tensor_tensor(s["a"][:], s["v"][:], -0.5, y, ALU.mult, ALU.mult).then_inc(done, 1)
                    dve.wait_ge(done, k + 1)
                    dve.tensor_tensor(s["c"][:], s["a"][:], y, ALU.mult).then_inc(done, 1)
                    dve.wait_ge(done, k + 2)
                    dve.scalar_tensor_tensor(y, s["c"][:], 1.5, y, ALU.add, ALU.mult).then_inc(done, 1)

                def body(i):
                    bn, kn = i + 2, (i + 2) * 18
                    bg, kg = i - 1, (i - 1) * 15
                    for s in range(8):
                        if s == 0 and live(bn, 0):
                            for t in range(TT):
                                dve.bn_stats(six_r[:, t, :], xs[:, at(bn, 0), t, :]).then_inc(rln, 1)
                            dve.wait_ge(rln, kn + 2)
                        if live(i, 0):
                            dve.wait_ge(rs_ps, i * 8 + s + 1)
                            wait(dve, ro_ps, i * 8 + s - 3)
                            dve.tensor_tensor(ret[:, s % 4, :], bank[s % 2][:, 0:384], dm[:, s, :], ALU.mult).then_inc(ret_ready, 1)
                        if s == 0 and live(bn, 0):
                            for t in range(TT):
                                dve.bn_aggr(mv_r[:, t, :], six_r[:, t, :]).then_inc(rln, 1)
                            dve.wait_ge(rln, kn + 4)
                            rsqrt_start(rs["rln"], mv_r[:, :, 1], 1.0, LN_EPS, rln, kn + 4)
                        if s == 1 and live(bn, 0):
                            newton(rs["rln"], rln, kn + 7)
                            newton(rs["rln"], rln, kn + 10)
                        if s == 2 and live(i + 1, 0):
                            b = i + 1
                            dve.wait_ge(rqk_ps, b + 1)
                            wait(dve, rqk_ready, b)
                            dve.tensor_tensor(rot_a, bank[4][:].rearrange("p (a t) -> p a t", a=2), cosT[:], ALU.mult).then_inc(rot_ready, 1)
                            dve.tensor_tensor(rot_b, bank[5][:].rearrange("p (a t) -> p a t", a=2), sinT[:], ALU.mult).then_inc(rot_ready, 1)
                        if s == 3 and live(bn, 0):
                            newton(rs["rln"], rln, kn + 13)
                            dve.wait_ge(rln, kn + 16)
                            wait(dve, rT_ps, bn)
                            for t in range(TT):
                                dve.tensor_scalar(s_nat[:, t, :], xs[:, at(bn, 0), t, :], mv_r[:, t, 0:1],
                                                  rs["rln"]["y"][:, t:t + 1].bitcast(FP32), ALU.subtract, ALU.mult).then_inc(rln, 1)
                        if s == 4 and live(i - 2, 0):
                            dve.wait_ge(pr_ps, i - 1)
                            xb = xs[:, at(i - 2, 0), :, :]
                            dve.tensor_tensor(xb, bank[7][:, 0:SEQ].rearrange("p (a t d) -> p a t d", a=1, t=TT), xb, ALU.add).then_inc(xr_done, 1)
                        if s == 4 and live(i + 1, 0):
                            b = i + 1
                            dve.wait_ge(rhi_ready, b + 1)
                            wait(dve, rex_ps, b * 4)
                            dve.tensor_tensor(qk_lo[:], qk[:], qk_hi[:].bitcast(FP32), ALU.subtract).then_inc(rlo_ready, 1)
                        if s == 5 and live(bg, 0):
                            dve.wait_ge(sq_ready, bg + 1)
                            wait(dve, gn, kg)
                            dve.tensor_reduce(ssq[:], sq.rearrange("p (n v) -> p n v", v=RV), AX.X, ALU.add).then_inc(gn, 1)
                            dve.wait_ge(gn, kg + 1)
                            rsqrt_start(rs["gn"], ssq[:], 1.0 / RV, GN_EPS, gn, kg + 1)
                        if s == 5 and live(bg, 0):
                            newton(rs["gn"], gn, kg + 4)
                        if s == 6 and live(i + 1, 0):
                            b = i + 1
                            dve.wait_ge(th_ready, b + 1)
                            dve.scalar_tensor_tensor(wide_buf[:, at(b, 0), :, :], tanh_z, 1.0, bank[7][:].rearrange("p (t v) -> p t v", t=TT),
                                                     ALU.add, ALU.mult).then_inc(gz_ready, 1)
                        if s == 6 and live(bg, 0):
                            newton(rs["gn"], gn, kg + 7)
                        if s == 7 and live(bg, 0):
                            newton(rs["gn"], gn, kg + 10)
                            dve.wait_ge(gn, kg + 13)
                            wait(dve, yr_ready, bg)
                            for t in range(TT):
                                dve.tensor_tensor(nrm[:, t, :].rearrange("p (n v) -> p n v", v=RV),
                                                  bank[4][:, t * SEQ:(t + 1) * SEQ].rearrange("p (n v) -> p n v", v=RV),
                                                  rs["gn"]["y"][:, 8 * t:8 * t + 8].bitcast(FP32).unsqueeze(2).to_broadcast([P, 8, RV]),
                                                  ALU.mult).then_inc(gn, 1)

                r_iterations(dve, body)

            phase(0)
            retention()
            dve.wait_ge(xr_done, BATCH)
            phase(BATCH)

        @block.gpsimd
        def _(pool):
            pool.memset(ones_wide[:], 1.0)
            pool.memset(v_st[:].rearrange("p t n -> p (t n)").bitcast(FP32), 0.0).then_inc(set_pool, 1)
            pool.wait_ge(set_pool, 1)
            blocks = v_st[:].rearrange("p t (h c) -> p t h c", h=NH)
            for t in range(TT):
                last = pool.memset(blocks[:, t, :, 2 * HD:3 * HD].bitcast(FP32), 1.0)
            last.then_inc(set_pool, 1)
            pool.wait_ge(ld_w, N_LDW)
            for n in (4, 5):
                last = pool.tensor_scalar(vecs[:, n, :], vecs[:, n, :], 0.5, 0.0, ALU.mult, ALU.add)
            last.then_inc(set_pool, 1)
            pool.wait_ge(set_pool, 3)

            def wide(v):
                return v.unsqueeze(1).to_broadcast([P, TT, P])

            def round_wide(dst, src):
                width = src.shape[-1]
                pool.tensor_tensor(dst[:, :, 0:1], src[:, :, 0:1], ones_wide[:, 0:2, 0:1], ALU.mult)
                return pool.tensor_scalar(dst[:, :, 1:width], src[:, :, 1:width], 1.0, 0.0, ALU.mult, ALU.add)

            def add_bo(b, base):
                pool.wait_ge(prep_ln, b * 9 + 9)
                pool.tensor_tensor(resid[:, at(b, base), :, :], s_nat[:], wide(bo_b), ALU.add).then_inc(resid_ready, 1)

            def round_qk(b):
                pool.wait_ge(qk_ready, b * 2 + 2)
                wait(pool, ex_ps, b * 4)
                round_wide(qk_hi, qk[:]).then_inc(hi_ready, 1)

            def place_v(b, half):
                if half == 0:
                    pool.wait_ge(v_ready, b + 1)
                wait(pool, pv_done, (b - 1) * NH + 8 + 8 * half)
                done = (va_ready, vb_ready)[half]
                heads = slice(8 * half, 8 * half + 8)
                src = v_nat[:, :, 64 * half:64 * half + 64].rearrange("p t (h d) -> p t h d", h=8)
                hi, lo = blocks[:, :, heads, 0:HD], blocks[:, :, heads, HD:2 * HD]
                pool.tensor_tensor(hi, src, ones_wide[:].unsqueeze(1).to_broadcast([P, TT, 8, HD]), ALU.mult).then_inc(done, 1)
                pool.wait_ge(done, b * 2 + 1)
                pool.tensor_tensor(lo, src, hi.bitcast(FP32), ALU.subtract).then_inc(done, 1)

            def low_part(b, h):
                pool.wait_ge(exp_done, b * NH + h + 1)
                pool.tensor_tensor(p_lo[:, h % 4, :, :], probs[:, h % 4, :, :], p_hi[:, h % 4, :, :].bitcast(FP32),
                                   ALU.subtract).then_inc(plo_pool, 1)

            def make_x1(b):
                pool.wait_ge(ln1, b * 9 + 9)
                wait(pool, x1_ready, b * 2)
                pool.tensor_tensor(xt1[:], n1[:], wide(g1_b), ALU.mult).then_inc(x1_ready, 1)
                pool.wait_ge(x1_ready, b * 2 + 1)
                wait(pool, x1T_ps, b)
                wait(pool, router, b * 8)
                wait(pool, y_done, (b - 1) * 8 + 2)
                pool.tensor_tensor(x1[:], xt1[:], wide(b1_b), ALU.add).then_inc(x1_ready, 1)

            def make_x(b, base):
                pool.wait_ge(ln2, b * 9 + 9)
                pool.tensor_tensor(xt2[:, 0], n2[:], wide(g2_b), ALU.mult).then_inc(x_done, 1)
                pool.wait_ge(x_done, b * 3 + 1)
                pool.tensor_tensor(xt2[:, 1], xt2[:, 0], wide(b2_b), ALU.add).then_inc(x_done, 1)
                pool.wait_ge(x_done, b * 3 + 2)
                xb = xs[:, at(b, base), :, :]
                pool.tensor_tensor(xb, xb, xt2[:, 1], ALU.add).then_inc(x_done, 1)

            def phase(base):
                def body(i):
                    for s in range(SLOTS):
                        bl, hl = (i, s - 7) if s >= 7 else (i - 1, s + SLOTS - 7)
                        if hl in LOW_ON_POOL and live(bl, base):
                            low_part(bl, hl)
                        if s == 3 and live(i, base):
                            place_v(i, 0)
                        if s == 2 and live(i - 2, base):
                            make_x1(i - 2)
                        if s == 6 and live(i + 1, base):
                            add_bo(i + 1, base)
                        if s == 8 and live(i, base):
                            place_v(i, 1)
                        if s == 11 and live(i + 1, base):
                            round_qk(i + 1)
                        if s == 14 and live(i - 3, base):
                            make_x(i - 3, base)

                iterations(pool, base, body)

            def retention():
                pool.wait_ge(x_done, 3 * BATCH)

                def use_values(half):
                    cols = slice(half * P, (half + 1) * P)
                    round_wide(v_ret[:, 0, :, cols], v_ret[:, 1, :, cols]).then_inc(vcopy, 1)

                def body(i):
                    if live(i - 2, 0):
                        b = i - 2
                        pool.wait_ge(gn, b * 15 + 15)
                        pool.wait_ge(gz_ready, b + 1)
                        wait(pool, yT_ps, b)
                        pool.tensor_tensor(y_ret, nrm, wide_buf[:, at(b, 0), :, :], ALU.mult).then_inc(yr_ready, 1)
                    if live(i, 0):
                        wait(pool, ro_ps, i * 8)
                        use_values(1)
                    if live(i + 1, 0):
                        b = i + 1
                        pool.wait_ge(rot_ready, b * 2 + 2)
                        wait(pool, rhi_ready, b)
                        wait(pool, rlo_ready, b)
                        pool.tensor_tensor(qk[:], rot_a, rot_b, ALU.add).then_inc(rqk_ready, 1)
                        pool.wait_ge(rqk_ready, b + 1)
                        wait(pool, rex_ps, b * 4)
                        round_wide(qk_hi, qk[:]).then_inc(rhi_ready, 1)
                        pool.wait_ge(rv_ready, b + 1)
                        wait(pool, ro_ps, i * 8 + 4)
                        use_values(0)

                r_iterations(pool, body)

            phase(0)
            retention()
            pool.wait_ge(xr_done, BATCH)
            phase(BATCH)



INPUTS = {
    "L0_attn_hidden_states": "x", "L0_attn_W_qkv": "W_qkv", "L0_attn_W_g": "W_g", "L0_attn_W_proj": "W_proj",
    "L0_attn_decay": "decay", "L0_ffn_Wq": "Wq", "L0_ffn_bq": "bq", "L0_ffn_Wk": "Wk", "L0_ffn_bk": "bk",
    "L0_ffn_Wv": "Wv", "L0_ffn_bv": "bv", "L0_ffn_Wo": "Wo", "L0_ffn_bo": "bo", "L0_ffn_router_w": "router_w",
    "L0_ffn_router_b": "router_b", "L0_ffn_W1": "W1", "L0_ffn_b1": "b1", "L0_ffn_W2": "W2", "L0_ffn_b2": "b2",
    "L0_ffn_ln1_g": "ln1_g", "L0_ffn_ln1_b": "ln1_b", "L0_ffn_ln2_g": "ln2_g", "L0_ffn_ln2_b": "ln2_b",
}


def kernel(**inputs):
    import concourse.bacc as bacc
    from concourse.bass_utils import run_bass_kernel_spmd

    nc = bacc.Bacc("TRN2", target_bir_lowering=False, num_devices=1)
    arrays, aps = {}, {}
    given = {short: np.ascontiguousarray(inputs[name]) for name, short in INPUTS.items()}
    for name, a in {**given, **constants()}.items():
        arrays[f"in_{name}"] = a
        aps[name] = nc.dram_tensor(f"in_{name}", a.shape, mybir.dt.from_np(a.dtype), kind="ExternalInput").ap()
    aps["out"] = nc.dram_tensor("out", (BATCH, SEQ, DM), FP32, kind="ExternalOutput").ap()
    build(nc, aps)
    r = run_bass_kernel_spmd(nc, [arrays], core_ids=[0])
    return r.results[0]["out"]
```

```python
import numpy as np
import concourse.bass as bass
from concourse import mybir
from contextlib import ExitStack

FP32 = mybir.dt.float32
FP32R = mybir.dt.float32r
INT32 = mybir.dt.int32
ALU = mybir.AluOpType
ACT = mybir.ActivationFunctionType
AX = mybir.AxisListType

P = 128
BATCH, SEQ, DM = 16, 256, 128
TT = SEQ // P
LN_EPS = 1e-5

NH, HD = 16, 8
GROUPS, GH = 4, 4
NE, DFF = 4, 512
CHUNKS = NE * DFF // P
CPE = DFF // P
SCALE = HD ** -0.5

RH, RK, RV, RGROUPS = 8, 16, 32, 4
QK_DIM, V_DIM, SCALE_BASE, GN_EPS = 128, 256, 512.0, 1e-5
MAGIC = 0x5F3759DF

UP_AT, DOWN_AT = 5, 7
SLOTS = 16
LOW_ON_POOL = [0, 2, 3, 5, 6, 8, 9, 10, 12, 14, 15]
LOW_ON_DVE = [h for h in range(NH) if h not in LOW_ON_POOL]
VROW = NH * P


def ffn_selectors():
    sel = np.zeros((P, GROUPS, 4, P), np.float32)
    for g in range(GROUPS):
        for j in range(GH):
            for d in range(HD):
                p = (g * GH + j) * HD + d
                for kind, parts in enumerate(((0, 1), (2,), (0, 2), (1,))):
                    for part in parts:
                        sel[p, g, kind, 32 * j + HD * part + d] = 1.0
    return sel.reshape(P, -1)


def attention_selector():
    sel = np.zeros((P, GH * HD + GH), np.float32)
    for j in range(GH):
        for d in range(HD):
            sel[32 * j + d, HD * j + d] = sel[32 * j + HD + d, HD * j + d] = 1.0
        sel[32 * j + 2 * HD, GH * HD + j] = 1.0
    return sel


def retention_selectors():
    sel = np.zeros((P, RGROUPS, 4, P), np.float32)
    for g in range(RGROUPS):
        for j in range(2):
            for d in range(RK):
                p = (2 * g + j) * RK + d
                for kind, parts in enumerate(((0, 1), (2, 3), (0, 2), (1, 3))):
                    for part in parts:
                        sel[p, g, kind, 64 * j + RK * part + d] = 1.0
    return sel.reshape(P, -1)


def rotary_tables():
    f = np.float32
    half = QK_DIM // 2
    base = (np.arange(0, QK_DIM, 2, dtype=f) + f(0.4 * QK_DIM)) / f(1.4 * QK_DIM)
    pos = np.arange(SEQ, dtype=f)
    scale = base[None, :] ** (pos[:, None] / f(SCALE_BASE))
    inv_freq = f(1.0) / f(10000.0) ** (np.arange(half, dtype=f) / f(half))
    angle = pos[:, None] * inv_freq[None, :]
    sin, cos = np.sin(angle), np.cos(angle)
    sign = np.tile(np.array([-1.0, 1.0], f), half)[:, None]
    out = []
    for s in (scale, f(1.0) / scale):
        out.append((np.repeat(cos * s, 2, 1).T, np.repeat(sin * s, 2, 1).T * sign))
    return (np.ascontiguousarray(np.concatenate([out[0][n], out[1][n]], 1), dtype=f) for n in range(2))


def constants():
    ident = np.eye(P, dtype=np.float32)
    ones_col = np.zeros((P, 1), np.float32)
    for j in range(GH):
        ones_col[32 * j + 3 * HD:32 * j + 3 * HD + 2] = 1.0
    eidx = np.tile(np.arange(NE, dtype=np.float32), TT)[None].repeat(P, 0)
    cos, sin = rotary_tables()
    small = np.concatenate([ident, ones_col, attention_selector(), eidx], 1)
    return {"c_cos": cos, "c_sin": sin, "c_sel_ret": retention_selectors(), "c_small": small, "c_sel_ffn": ffn_selectors()}


def packed(A):
    A = dict(A)
    A["w_att"] = np.concatenate([A.pop(n) for n in ("Wq", "Wk", "Wv", "Wo")], 1)
    A["bias_rows"] = np.concatenate([A.pop("b1").reshape(CHUNKS, P), A.pop("bq")[None], A.pop("bk")[None]], 0)
    A["vecs"] = np.concatenate([A.pop(n).reshape(-1) for n in ("bv", "bo", "ln1_g", "ln1_b", "ln2_g", "ln2_b", "router_w", "router_b")])
    return A


def wait(eng, sem, value):
    if isinstance(value, int) and value <= 0:
        return
    eng.wait_ge(sem, value)


def build(nc, A):
    ctx = ExitStack()
    with ctx:
        def sb(name, shape, dt=FP32):
            return ctx.enter_context(nc.sbuf_tensor(name, shape, dt))

        def sem(name):
            return ctx.enter_context(nc.semaphore(name))

        xs = sb("xs", [P, BATCH, TT, DM])
        wide_buf = sb("wide_buf", [P, BATCH, 2, SEQ])
        resid = wide_buf[:, :, 0, :].rearrange("p b (t d) -> p b t d", t=TT)
        stage = wide_buf[:].rearrange("p b a t -> p (b a t)")[:, 0:4096]
        p_split = sb("p_split", [P, 2, 4, TT, SEQ], FP32R)
        small = sb("small", [P, P + 1 + GH * HD + GH + TT * NE])
        ident, ones_col = small[:, 0:P], small[:, P:P + 1]
        sel_att = small[:, P + 1:P + 1 + GH * HD + GH]
        eidx = small[:, P + 1 + GH * HD + GH:].rearrange("p (t e) -> p t e", t=TT)
        ident_r = sb("ident_r", [P, P], FP32R)
        sel_r = sb("sel_r", [P, GROUPS, 4, P], FP32R)
        w_att = sb("w_att_sb", [P, 4, P])
        wq, wk, wv, wo = (w_att[:, n, :] for n in range(4))
        w1_hi = sb("w1_hi", [P, CHUNKS, P], FP32R)
        w1_lo = sb("w1_lo", [P, CHUNKS, P], FP32R)
        w2 = sb("w2", [P, CHUNKS, P])
        dm = sb("dm", [P, RH, 384])
        dm_flat = dm[:].rearrange("p h n -> p (h n)")
        bias_rows = dm_flat[0:CHUNKS + 2, 2048:2176]
        bias_cols = sb("bias_cols", [P, CHUNKS + 2])
        vecs = sb("vecs_sb", [P, 7 * P + 1])
        bv_b, bo_b, g1_b, b1_b, g2_b, b2_b, rw_b = (vecs[:, n * P:(n + 1) * P] for n in range(7))
        rb_b = vecs[:, 7 * P:7 * P + 1]
        b2row = dm_flat[0:1, 2176:2688].rearrange("a (e d) -> a e d", e=NE)
        b2_r = sb("b2_r", [64, NE, P], FP32R)
        ones_r = sb("ones_r", [64, P], FP32R)
        eps_col = sb("eps_col", [P, 1])

        s_nat = sb("s_nat", [P, TT, DM])
        sT = sb("sT", [P, SEQ])
        qk = sb("qk", [P, 2, SEQ])
        qk_hi = sb("qk_hi", [P, 2, SEQ], FP32R)
        qk_lo = sb("qk_lo", [P, 2, SEQ], FP32R)
        stacks = sb("stacks", [P, 2 * GROUPS * SEQ], FP32R)
        q_st, k_st = (stacks[:, n * GROUPS * SEQ:(n + 1) * GROUPS * SEQ].rearrange("p (g t) -> p g t", g=GROUPS) for n in range(2))
        q2_st = sb("q2_st", [P, GROUPS, SEQ], FP32R)
        negmax = sb("negmax", [P, 2, TT, GH])
        mx = sb("mx", [P, TT, P], FP32R)
        probs = sb("probs", [P, 4, TT, SEQ])
        ones_wide = sb("ones_wide", [P, 8, HD])
        v_nat = sb("v_nat", [P, TT, P])
        v_st = sb("v_st", [P, TT, VROW], FP32R)
        p_hi, p_lo = p_split[:, 0], p_split[:, 1]
        att_un = sb("att_un", [P, GROUPS, SEQ])
        rsum = sb("rsum", [P, TT * GROUPS, GH])
        att_pair = sb("att_pair", [P, 2, SEQ])
        att, attT = att_pair[:, 0, :].rearrange("p (t d) -> p t d", t=TT), att_pair[:, 1, :]
        token_bufs = sb("token_bufs", [P, 9, TT, DM])
        y1, n1, x1, xt1, rprod, acc, n2 = (token_bufs[:, n] for n in range(7))
        xt2 = token_bufs[:, 7:9]
        x1_hi = sb("x1_hi", [P, SEQ], FP32R)
        x1_lo = sb("x1_lo", [P, SEQ], FP32R)
        rkey = sb("rkey", [P, 2, TT])
        rint = sb("rint", [P, 4, TT], INT32)
        masks = sb("masks", [P, BATCH, TT, NE])
        hidden = sb("hidden", [P, 4, SEQ])
        ln_scratch = {}
        for s in ("prep", "ln1", "ln2"):
            ln_scratch[s] = dict(six=sb(f"six_{s}", [P, TT, 6]), mv=sb(f"mv_{s}", [P, TT, 2]),
                                 lnv=sb(f"lnv_{s}", [P, TT]), seed=sb(f"seed_{s}", [P, TT]),
                                 a=sb(f"a_{s}", [P, TT]), c=sb(f"c_{s}", [P, TT]), rstd=sb(f"rstd_{s}", [P, TT]))

        sel2_r = sb("sel2_r", [P, RGROUPS, 4, P], FP32R)
        cosT = sb("cosT", [P, 2, SEQ])
        sinT = sb("sinT", [P, 2, SEQ])
        wqkv = sb("wqkv", [P, 512])
        wqk_sw = sb("wqk_sw", [P, 256])
        wv_mean = sb("wv_mean", [P, RH])
        wv_cen = sb("wv_cen", [P, V_DIM])
        wg = sb("wg", [P, V_DIM])
        wproj = sb("wproj", [P, 2, DM])
        dec = sb("dec", [RH, 8])
        pw = sb("pw", [RH, 256])
        prow = sb("prow", [RH, 384])
        rot_a, rot_b = att_un[:, 0:2, :], att_un[:, 2:4, :]
        token_flat = token_bufs[:].rearrange("p n t d -> p (n t d)")
        r_st = stacks[:].rearrange("p (g a t) -> p g a t", g=RGROUPS, a=2)
        ret = token_flat[:, 0:1536].rearrange("p (n t) -> p n t", n=4)
        v_ret = probs[:, 0:2, :, :]
        tanh_z = token_flat[:, 1536:2048].rearrange("p (t v) -> p t v", t=TT)
        outT = hidden[:, 2:4, :]
        sq = att_pair[:].rearrange("p a t -> p (a t)")
        ssq = sb("ssq", [P, 16])
        nrm = probs[:, 2, :, :]
        y_ret = probs[:, 3, :, :]
        yT = hidden[:, 0:2, :]
        rs = {}
        for s_, n_ in (("rln", TT), ("gn", 16)):
            rs[s_] = dict(v=sb(f"v_{s_}", [P, n_]), i=sb(f"i_{s_}", [P, n_], INT32), y=sb(f"y_{s_}", [P, n_], INT32),
                          a=sb(f"ra_{s_}", [P, n_]), c=sb(f"rc_{s_}", [P, n_]))
        six_r = sb("six_r", [P, TT, 6])
        mv_r = sb("mv_r", [P, TT, 2])
        decay_rows = nc.dram_tensor("decay_rows", (RH, P, 513), FP32, kind="Internal").ap()

        bank = [ctx.enter_context(nc.psum_tensor(f"bank{n}", [P, 512], FP32)) for n in range(8)]
        score_bank, prob_bank = bank[0:2], bank[2:4]
        pv_bank, misc, up_bank, y_bank = bank[4], bank[5], bank[6], bank[7]

        ld_x, ld_c, ld_w, ld_e, ld_r, ld_d = sem("ld_x"), sem("ld_c"), sem("ld_w"), sem("ld_e"), sem("ld_r"), sem("ld_d")
        set_dve, set_pe, set_act, set_pool, set_prow, set_scr = sem("set_dve"), sem("set_pe"), sem("set_act"), sem("set_pool"), sem("set_prow"), sem("set_scr")
        st_out = sem("st_out")
        prep_ln, ln1, ln2 = sem("prep_ln"), sem("ln1"), sem("ln2")
        seed = {"prep": sem("seed_prep"), "ln1": sem("seed_ln1"), "ln2": sem("seed_ln2")}
        ln_sem = {"prep": prep_ln, "ln1": ln1, "ln2": ln2}
        sT_ps, sT_ready = sem("sT_ps"), sem("sT_ready")
        qk_ps, qk_ready, hi_ready, lo_ready = sem("qk_ps"), sem("qk_ready"), sem("hi_ready"), sem("lo_ready")
        v_ps, v_ready, va_ready, vb_ready = sem("v_ps"), sem("v_ready"), sem("va_ready"), sem("vb_ready")
        resid_ready = sem("resid_ready")
        ex_ps, ex_ready = sem("ex_ps"), sem("ex_ready")
        score_ps, max_done, mx_ready, m_ps, q2_ready = sem("score_ps"), sem("max_done"), sem("mx_ready"), sem("m_ps"), sem("q2_ready")
        prob_ps, exp_done, plo_pool, plo_dve, pv_done = sem("prob_ps"), sem("exp_done"), sem("plo_pool"), sem("plo_dve"), sem("pv_done")
        un_ready, att_ps, att_ready = sem("un_ready"), sem("att_ps"), sem("att_ready")
        attT_ps, attT_ready, wo_ps, y1_ready = sem("attT_ps"), sem("attT_ready"), sem("wo_ps"), sem("y1_ready")
        x1_ready, x1T_ps, x1hi_ready, x1lo_ready, router = sem("x1_ready"), sem("x1T_ps"), sem("x1hi_ready"), sem("x1lo_ready"), sem("router")
        up_ps, h_ready, down_done, y_done, x_done = sem("up_ps"), sem("h_ready"), sem("down_done"), sem("y_done"), sem("x_done")
        rln, gn = sem("rln"), sem("gn")
        rT_ps, rT_ready = sem("rT_ps"), sem("rT_ready")
        rqk_ps, rot_ready, rqk_ready, rhi_ready, rlo_ready = sem("rqk_ps"), sem("rot_ready"), sem("rqk_ready"), sem("rhi_ready"), sem("rlo_ready")
        rv_ps, rv_ready, vcopy, z_ps, th_ready, gz_ready = sem("rv_ps"), sem("rv_ready"), sem("vcopy"), sem("z_ps"), sem("th_ready"), sem("gz_ready")
        rex_ps, rex_ready, rs_ps, ret_ready, ro_ps = sem("rex_ps"), sem("rex_ready"), sem("rs_ps"), sem("ret_ready"), sem("ro_ps")
        oT_ready, on_ps, sq_ready, on_ready = sem("oT_ready"), sem("on_ps"), sem("sq_ready"), sem("on_ready")
        yr_ready, yT_ps, yT_ready, pr_ps, xr_done = sem("yr_ready"), sem("yT_ps"), sem("yT_ready"), sem("pr_ps"), sem("xr_done")

        block = ctx.enter_context(nc.Block())

        def low_count(h):
            own = LOW_ON_POOL if h in LOW_ON_POOL else LOW_ON_DVE
            return (plo_pool if h in LOW_ON_POOL else plo_dve), len(own), own.index(h) + 1

        def live(b, base):
            return not isinstance(b, int) or base <= b < base + BATCH

        def iterations(eng, base, body):
            for i in range(base - 1, base + 4):
                body(i)
            with eng.Fori(base + 4, base + 15) as i:
                body(i)
            for i in range(base + 15, base + 19):
                body(i)

        def r_iterations(eng, body):
            for i in range(-2, 3):
                body(i)
            with eng.Fori(3, BATCH - 2) as i:
                body(i)
            for i in range(BATCH - 2, BATCH + 2):
                body(i)

        def at(b, base):
            return bass.ds(b - base, 1)

        @block.sync
        def _(sp):
            xv = A["x"].rearrange("b (t p) d -> p b t d", p=P)
            sp.dma_start(xs[:, 0:2], xv[:, 0:2]).then_inc(ld_x, 16)
            sp.dma_start(bias_rows, A["bias_rows"]).then_inc(ld_c, 16)
            sp.dma_start(small[:], A["c_small"]).then_inc(ld_c, 16)
            sp.dma_start(w_att[:].rearrange("p n d -> p (n d)"), A["w_att"]).then_inc(ld_w, 16)
            sp.dma_start(stage[:, 0:2048], A["c_sel_ffn"]).then_inc(ld_c, 16)
            sp.dma_start(vecs[:], A["vecs"].partition_broadcast(P)).then_inc(ld_w, 16)
            sp.dma_start(b2row.rearrange("a e d -> a (e d)"), A["b2"].rearrange("(a e) d -> a (e d)", a=1)).then_inc(ld_e, 16)
            sp.dma_start(stage[:, 2048:4096].rearrange("p (e n) -> p e n", e=NE), A["W1"].rearrange("e d n -> d e n")).then_inc(ld_e, 16)
            sp.dma_start(w2[:].rearrange("p (e c) n -> p e c n", e=NE), A["W2"].rearrange("e (c p) n -> p e c n", p=P)).then_inc(ld_e, 16)
            sp.dma_start(xs[:, 2:BATCH], xv[:, 2:BATCH]).then_inc(ld_x, 16)
            sp.dma_start(dm_flat[:, 0:2048], A["c_sel_ret"]).then_inc(ld_r, 16)
            sp.dma_start(cosT[:].rearrange("p a t -> p (a t)"), A["c_cos"]).then_inc(ld_r, 16)
            sp.dma_start(sinT[:].rearrange("p a t -> p (a t)"), A["c_sin"]).then_inc(ld_r, 16)
            sp.dma_start(wqkv[:], A["W_qkv"]).then_inc(ld_r, 16)
            sp.dma_start(wg[:], A["W_g"]).then_inc(ld_r, 16)
            sp.dma_start(wproj[:], A["W_proj"].rearrange("(a p) d -> p a d", p=P)).then_inc(ld_r, 16)
            sp.dma_start(dec[:, 0:1], A["decay"].rearrange("(h a) -> h a", a=1)).then_inc(ld_r, 16)
            sp.wait_ge(set_pe, 1)
            sp.wait_ge(set_prow, 1)
            sp.dma_start(decay_rows[:, :, 0:384], prow[:].unsqueeze(1).to_broadcast([RH, P, 384])).then_inc(set_scr, 16)
            sp.wait_ge(set_scr, 16)
            for n, width in ((0, 256), (256, 128)):
                moved = bass.AP(tensor=decay_rows.tensor, offset=P, ap=[[512, P], [P * 513, RH], [1, width]])
                sp.dma_start(dm[:, :, n:n + width], moved).then_inc(ld_d, 16)
            ov = A["out"].rearrange("b (t p) d -> p b t d", p=P)
            with sp.Fori(0, BATCH) as i:
                sp.wait_ge(x_done, i * 3 + 3 * BATCH + 3)
                sp.dma_start(ov[:, bass.ds(i, 1), :, :], xs[:, bass.ds(i, 1), :, :]).then_inc(st_out, 16)
            sp.wait_ge(st_out, 16 * BATCH)

        N_LDC, N_LDW, N_LDE = 3 * 16, 2 * 16, 3 * 16
        SET_ATT, SET_EXPERTS, SET_DVE = 5, 8, 32

        @block.tensor
        def _(pe):
            turn = {}

            def take_misc(consumer, value):
                wait(pe, *turn["last"])
                turn["last"] = (consumer, value)

            pe.wait_ge(ld_c, N_LDC)
            pe.transpose(misc[:, 0:CHUNKS + 2], bias_rows, ident[0:CHUNKS + 2, 0:CHUNKS + 2]).then_inc(set_pe, 1)
            pe.wait_ge(set_act, 1)
            pe.wait_ge(set_dve, SET_ATT)
            pe.wait_ge(set_pool, 2)
            pe.wait_ge(ld_w, N_LDW)

            def transposes(b):
                pe.wait_ge(prep_ln, b * 9 + 9)
                take_misc(sT_ready, b + 1)
                for t in range(TT):
                    last = pe.transpose(misc[:, t * P:(t + 1) * P], s_nat[:, t, :], ident[:])
                last.then_inc(sT_ps, 1)

            def project_qk(b):
                pe.wait_ge(sT_ready, b + 1)
                take_misc(qk_ready, b * 2 + 2)
                pe.matmul(misc[:, 0:SEQ], wq[:], sT[:], start=True, stop=True)
                pe.matmul(misc[:, SEQ:2 * SEQ], wk[:], sT[:], start=True, stop=True).then_inc(qk_ps, 1)

            def project_v(b):
                take_misc(v_ready, b + 1)
                for t in range(TT):
                    last = pe.matmul(misc[:, t * P:(t + 1) * P], sT[:, t * P:(t + 1) * P], wv[:], start=True, stop=True)
                last.then_inc(v_ps, 1)

            def expand(b, g):
                if g == 0:
                    pe.wait_ge(hi_ready, b + 1)
                    pe.wait_ge(lo_ready, b + 1)
                take_misc(ex_ready, b * 8 + 2 * g + 2)
                for n in range(2):
                    o = misc[:, n * SEQ:(n + 1) * SEQ]
                    pe.matmul(o, sel_r[:, g, 2 * n, :], qk_hi[:, n, :], start=True, stop=False)
                    last = pe.matmul(o, sel_r[:, g, 2 * n + 1, :], qk_lo[:, n, :], start=False, stop=True)
                last.then_inc(ex_ps, 1)

            def score(b, h):
                g, r = h // GH, 32 * (h % GH)
                if h % GH == 0:
                    pe.wait_ge(ex_ready, b * 8 + 2 * g + 2)
                wait(pe, max_done, b * NH + (h - 1))
                for t in range(TT):
                    last = pe.matmul(score_bank[h % 2][:, t * SEQ:(t + 1) * SEQ], q_st[r:r + 32, g, t * P:(t + 1) * P],
                                     k_st[r:r + 32, g, :], start=True, stop=True)
                last.then_inc(score_ps, 1)

            def spread_max(b, g):
                pe.wait_ge(mx_ready, b * 8 + 2 * g + 2)
                take_misc(q2_ready, b * 4 + g + 1)
                for t in range(TT):
                    last = pe.matmul(misc[:, t * P:(t + 1) * P], mx[:, t, :], ident_r[:], start=True, stop=True)
                last.then_inc(m_ps, 1)

            def shifted_score(b, h):
                g, r = h // GH, 32 * (h % GH)
                if h % GH == 0:
                    pe.wait_ge(q2_ready, b * 4 + g + 1)
                wait(pe, exp_done, b * NH + (h - 1))
                for t in range(TT):
                    last = pe.matmul(prob_bank[h % 2][:, t * SEQ:(t + 1) * SEQ], k_st[r:r + 32, g, t * P:(t + 1) * P],
                                     q2_st[r:r + 32, g, :], start=True, stop=True)
                last.then_inc(prob_ps, 1)

            def weigh_values(b, h):
                pe.wait_ge(exp_done, b * NH + h + 1)
                if h == 0:
                    pe.wait_ge(va_ready, b * 2 + 2)
                    wait(pe, un_ready, b * 2)
                if h == NH // 2:
                    pe.wait_ge(vb_ready, b * 2 + 2)
                    pe.wait_ge(un_ready, b * 2 + 1)
                g, j = h // GH, h % GH
                o = pv_bank[:, (g % 2) * SEQ:(g % 2 + 1) * SEQ]
                w = h * P - 32 * j
                for t in range(TT):
                    pe.matmul(o, v_st[:, t, w:w + P], p_hi[:, h % 4, t, :], start=(j == 0 and t == 0), stop=False)
                engine, per_batch, count = low_count(h)
                pe.wait_ge(engine, b * per_batch + count)
                for t in range(TT):
                    last = pe.matmul(o, v_st[:, t, w:w + P], p_lo[:, h % 4, t, :], start=False,
                                     stop=(j == GH - 1 and t == TT - 1))
                last.then_inc(pv_done, 1)

            def att_to_tokens(b):
                pe.wait_ge(un_ready, b * 2 + 2)
                take_misc(att_ready, b * 2 + 2)
                n = GH * HD + GH
                for t in range(TT):
                    for g in range(GROUPS):
                        last = pe.matmul(misc[:, (GROUPS * t + g) * n:(GROUPS * t + g + 1) * n],
                                         att_un[:, g, t * P:(t + 1) * P], sel_att[:], start=True, stop=True)
                last.then_inc(att_ps, 1)

            def att_to_dims(b):
                pe.wait_ge(att_ready, b * 2 + 2)
                take_misc(attT_ready, b + 1)
                for t in range(TT):
                    last = pe.transpose(misc[:, t * P:(t + 1) * P], att[:, t, :], ident[:])
                last.then_inc(attT_ps, 1)

            def project_out(b):
                pe.wait_ge(attT_ready, b + 1)
                take_misc(y1_ready, b + 1)
                for t in range(TT):
                    last = pe.matmul(misc[:, t * P:(t + 1) * P], attT[:, t * P:(t + 1) * P], wo[:], start=True, stop=True)
                last.then_inc(wo_ps, 1)

            def x1_to_dims(b):
                pe.wait_ge(x1_ready, b * 2 + 2)
                take_misc(x1lo_ready, b + 1)
                for t in range(TT):
                    last = pe.transpose(misc[:, t * P:(t + 1) * P], x1[:, t, :], ident[:])
                last.then_inc(x1T_ps, 1)

            def up(b, c):
                if isinstance(b, int) and b == 0 and c == 0:
                    pe.wait_ge(set_dve, SET_EXPERTS)
                    pe.wait_ge(ld_e, N_LDE)
                if c == 0:
                    pe.wait_ge(x1lo_ready, b + 1)
                wait(pe, h_ready, b * CHUNKS + c)
                o = up_bank[:, 0:SEQ]
                pe.matmul(o, w1_lo[:, c, :], x1_hi[:], start=True, stop=False)
                pe.matmul(o, w1_hi[:, c, :], x1_lo[:], start=False, stop=False)
                pe.matmul(o, w1_hi[:, c, :], x1_hi[:], start=False, stop=True).then_inc(up_ps, 1)

            def down(b, c):
                e, first, final = c // CPE, c % CPE == 0, c % CPE == CPE - 1
                pe.wait_ge(h_ready, b * CHUNKS + c + 1)
                if first:
                    wait(pe, y_done, b * 8 + 2 * e)
                    pe.matmul(y_bank[:, 0:SEQ], ones_r[:], b2_r[:, e, :].unsqueeze(1).to_broadcast([64, TT, P]),
                              start=True, stop=False, skip_group_check=True)
                for t in range(TT):
                    last = pe.matmul(y_bank[:, t * P:(t + 1) * P], hidden[:, c % 4, t * P:(t + 1) * P], w2[:, c, :],
                                     start=False, stop=final, skip_group_check=True)
                last.then_inc(down_done, 1)

            def phase(base):
                turn["last"] = (set_act, 1)

                def body(i):
                    if live(i - 2, base):
                        turn["last"] = (y1_ready, i - 2 + 1)
                    for s in range(SLOTS):
                        bu, cu = (i - 2, s - UP_AT) if s >= UP_AT else (i - 3, s + SLOTS - UP_AT)
                        bs, hs = (i, s - 6) if s >= 6 else (i - 1, s + SLOTS - 6)
                        bd, cd = (i - 2, s - DOWN_AT) if s >= DOWN_AT else (i - 3, s + SLOTS - DOWN_AT)
                        bw, hw = (i, s - 8) if s >= 8 else (i - 1, s + SLOTS - 8)
                        if live(bu, base):
                            up(bu, cu)
                        if live(i, base):
                            score(i, s)
                        if live(bs, base):
                            shifted_score(bs, hs)
                        if cd % CPE != 0 and live(bd, base):
                            down(bd, cd)
                        if live(bw, base):
                            weigh_values(bw, hw)
                        if cd % CPE == 0 and live(bd, base):
                            down(bd, cd)
                        if s == 0 and live(i - 1, base):
                            spread_max(i - 1, 3)
                        if s in (4, 8, 12) and live(i, base):
                            spread_max(i, s // 4 - 1)
                        if s in (2, 6, 10) and live(i, base):
                            expand(i, s // 4 + 1)
                        if s == 14 and live(i + 1, base):
                            expand(i + 1, 0)
                        if s == 3 and live(i - 2, base):
                            x1_to_dims(i - 2)
                        if s == 7 and live(i + 1, base):
                            transposes(i + 1)
                        if s == 9 and live(i + 1, base):
                            project_qk(i + 1)
                        if s == 1 and live(i, base):
                            project_v(i)
                        if s == 11 and live(i - 1, base):
                            att_to_tokens(i - 1)
                        if s == 13 and live(i - 1, base):
                            att_to_dims(i - 1)
                        if s == 15 and live(i - 1, base):
                            project_out(i - 1)

                iterations(pe, base, body)

            def retention():
                pe.wait_ge(x_done, 3 * BATCH)
                pe.wait_ge(ld_r, 7 * 16)
                pe.wait_ge(set_dve, SET_DVE)
                last7, last4 = {}, {}

                def take(which, consumer, value):
                    if "last" in which:
                        wait(pe, *which["last"])
                    which["last"] = (consumer, value)

                def body(i):
                    if live(i, 0):
                        last7["last"] = (gz_ready, i + 1)
                    if live(i - 2, 0):
                        last4["last"] = (on_ready, i - 1)
                    for s in range(8):
                        if live(i, 0):
                            h, r, g = s, 64 * (s % 2), s // 2
                            if h % 2 == 0:
                                pe.wait_ge(rex_ready, i * 4 + g + 1)
                            wait(pe, ret_ready, i * 8 + h - 1)
                            ps = bank[h % 2]
                            pe.matmul(ps[:, 0:256], r_st[r:r + 64, g, 1, 0:P], r_st[r:r + 64, g, 0, :], start=True, stop=True)
                            pe.matmul(ps[:, 256:384], r_st[r:r + 64, g, 1, P:2 * P], r_st[r:r + 64, g, 0, P:2 * P],
                                      start=True, stop=True).then_inc(rs_ps, 1)
                        be, ge = (i, s + 1) if s in (0, 1, 2) else (i + 1, 0)
                        if s in (0, 1, 2, 6) and live(be, 0):
                            if ge == 0:
                                pe.wait_ge(rlo_ready, be + 1)
                            wait(pe, rex_ready, be * 4 + ge)
                            for n in range(2):
                                o = bank[6][:, n * SEQ:(n + 1) * SEQ]
                                pe.matmul(o, sel2_r[:, ge, 2 * n, :], qk_hi[:, n, :], start=True, stop=False)
                                last = pe.matmul(o, sel2_r[:, ge, 2 * n + 1, :], qk_lo[:, n, :], start=False, stop=True)
                            last.then_inc(rex_ps, 1)
                        bo, ho = (i, s - 2) if s >= 2 else (i - 1, s + 6)
                        if live(bo, 0):
                            pe.wait_ge(ret_ready, bo * 8 + ho + 1)
                            if ho % 4 == 0:
                                pe.wait_ge(vcopy, bo * 2 + ho // 4 + 1)
                                wait(pe, oT_ready, bo * 2 + ho // 4 - 1)
                            o = bank[2 + ho // 4][32 * (ho % 4):32 * (ho % 4) + 32, 0:SEQ]
                            pe.matmul(o, v_use(bo, 0, ho), ret[:, ho % 4, 0:256], start=True, stop=True)
                            pe.matmul(o[:, P:2 * P], v_use(bo, 1, ho), ret[:, ho % 4, 256:384], start=False, stop=True,
                                      skip_group_check=True).then_inc(ro_ps, 1)
                        if s == 0 and live(i + 1, 0):
                            pe.wait_ge(rln, (i + 1) * 18 + 18)
                            take(last7, rT_ready, i + 2)
                            for t in range(TT):
                                last = pe.transpose(bank[7][:, t * P:(t + 1) * P], s_nat[:, t, :], ident[:])
                            last.then_inc(rT_ps, 1)
                        if s == 1 and live(i + 1, 0):
                            pe.wait_ge(rT_ready, i + 2)
                            take(last4, rot_ready, (i + 1) * 2 + 2)
                            for n in range(2):
                                pe.matmul(bank[4][:, n * SEQ:(n + 1) * SEQ], wqkv[:, n * P:(n + 1) * P], sT[:], start=True, stop=True)
                            for n in range(2):
                                last = pe.matmul(bank[5][:, n * SEQ:(n + 1) * SEQ], wqk_sw[:, n * P:(n + 1) * P], sT[:], start=True, stop=True)
                            last.then_inc(rqk_ps, 1)
                        if s == 1 and live(i - 2, 0):
                            pe.wait_ge(yr_ready, i - 1)
                            take(last7, yT_ready, i - 1)
                            for half in range(2):
                                for t in range(TT):
                                    last = pe.transpose(bank[7][:, (2 * half + t) * P:(2 * half + t + 1) * P],
                                                        y_ret[:, t, half * P:(half + 1) * P], ident[:])
                            last.then_inc(yT_ps, 1)
                        if s == 2 and live(i + 1, 0):
                            take(last7, rv_ready, i + 2)
                            for t in range(TT):
                                last = pe.matmul(bank[7][:, t * SEQ:(t + 1) * SEQ], sT[:, t * P:(t + 1) * P], wv_cen[:], start=True, stop=True)
                            last.then_inc(rv_ps, 1)
                        if s == 4 and live(i - 2, 0):
                            pe.wait_ge(yT_ready, i - 1)
                            take(last7, xr_done, i - 1)
                            for t in range(TT):
                                for half in range(2):
                                    last = pe.matmul(bank[7][:, t * P:(t + 1) * P], yT[:, half, t * P:(t + 1) * P], wproj[:, half, :],
                                                     start=(half == 0), stop=(half == 1))
                            last.then_inc(pr_ps, 1)
                        if s == 3 and live(i - 1, 0):
                            pe.wait_ge(oT_ready, (i - 1) * 2 + 2)
                            take(last4, on_ready, i)
                            for t in range(TT):
                                for half in range(2):
                                    last = pe.transpose(bank[4][:, (2 * t + half) * P:(2 * t + half + 1) * P],
                                                        outT[:, half, t * P:(t + 1) * P], ident[:])
                            last.then_inc(on_ps, 1)
                        if s == 5 and live(i + 1, 0):
                            take(last7, gz_ready, i + 2)
                            for t in range(TT):
                                last = pe.matmul(bank[7][:, t * SEQ:(t + 1) * SEQ], sT[:, t * P:(t + 1) * P], wg[:], start=True, stop=True)
                            last.then_inc(z_ps, 1)

                def v_use(b, t, h):
                    return v_ret[:, 0, t, RV * h:RV * h + RV]

                r_iterations(pe, body)

            phase(0)
            retention()
            pe.wait_ge(xr_done, BATCH)
            phase(BATCH)

        @block.scalar
        def _(act):
            act.preload_act_table_set("natural_log_exp_and_others")
            act.wait_ge(set_pe, 1)
            act.activation(bias_cols[:], misc[:, 0:CHUNKS + 2], ACT.Copy).then_inc(set_act, 1)
            act.wait_ge(set_dve, SET_ATT)
            act.wait_ge(set_act, 1)

            def seeds(b, which):
                s = ln_scratch[which]
                act.wait_ge(ln_sem[which], b * 9 + 4)
                act.activation(s["lnv"][:], s["mv"][:, :, 1], ACT.Ln, bias=eps_col[:]).then_inc(seed[which], 1)
                act.wait_ge(seed[which], b * 2 + 1)
                act.activation(s["seed"][:], s["lnv"][:], ACT.Exp, scale=-0.5).then_inc(seed[which], 1)

            def out_sT(b):
                act.wait_ge(sT_ps, b + 1)
                wait(act, v_ps, b)
                act.activation(sT[:], misc[:, 0:SEQ], ACT.Copy).then_inc(sT_ready, 1)

            def out_qk(b):
                act.wait_ge(qk_ps, b + 1)
                wait(act, hi_ready, b)
                wait(act, lo_ready, b)
                for n in range(2):
                    act.activation(qk[:, n, :], misc[:, n * SEQ:(n + 1) * SEQ], ACT.Identity,
                                   bias=bias_cols[:, CHUNKS + n:CHUNKS + n + 1]).then_inc(qk_ready, 1)

            def out_expand(b, g):
                act.wait_ge(ex_ps, b * 4 + g + 1)
                wait(act, prob_ps, (b - 1) * NH + 4 * g + 4)
                act.activation(q_st[:, g, :], misc[:, 0:SEQ], ACT.Copy).then_inc(ex_ready, 1)
                act.activation(k_st[:, g, :], misc[:, SEQ:2 * SEQ], ACT.Identity, bias=ones_col[:]).then_inc(ex_ready, 1)

            def exp(b, h):
                act.wait_ge(prob_ps, b * NH + h + 1)
                wait(act, pv_done, b * NH + h - 3)
                shifted = prob_bank[h % 2][:].rearrange("p (t q) -> p t q", t=TT)
                act.activation(probs[:, h % 4, :, :], shifted, ACT.Exp, scale=SCALE)
                act.activation(p_hi[:, h % 4, :, :], shifted, ACT.Exp, scale=SCALE).then_inc(exp_done, 1)

            def out_pv(b, half):
                act.wait_ge(pv_done, b * NH + 8 * half + 8)
                if half == 0:
                    wait(act, att_ps, b)
                act.activation(att_un[:, 2 * half:2 * half + 2, :], pv_bank[:].rearrange("p (a q) -> p a q", a=2),
                               ACT.Copy).then_inc(un_ready, 1)

            def out_attT(b):
                act.wait_ge(attT_ps, b + 1)
                wait(act, wo_ps, b)
                act.activation(attT[:], misc[:, 0:SEQ], ACT.Copy).then_inc(attT_ready, 1)

            def round_x1(b):
                act.wait_ge(x1T_ps, b + 1)
                wait(act, up_ps, b * CHUNKS)
                act.activation(x1_hi[:], misc[:, 0:SEQ], ACT.Copy).then_inc(x1hi_ready, 1)

            def relu(b, c):
                act.wait_ge(up_ps, b * CHUNKS + c + 1)
                wait(act, down_done, b * CHUNKS + c - 3)
                act.activation(hidden[:, c % 4, :], up_bank[:, 0:SEQ], ACT.Relu, bias=bias_cols[:, c:c + 1]).then_inc(h_ready, 1)

            def phase(base):
                def body(i):
                    for s in range(SLOTS):
                        bu, cu = (i - 2, s - UP_AT) if s >= UP_AT else (i - 3, s + SLOTS - UP_AT)
                        bs, hs = (i, s - 6) if s >= 6 else (i - 1, s + SLOTS - 6)
                        if s == 8 and live(i - 1, base):
                            out_pv(i - 1, 1)
                        if s == 0 and live(i - 1, base):
                            out_pv(i - 1, 0)
                        if s in (3, 7, 11) and live(i, base):
                            out_expand(i, s // 4 + 1)
                        if s == 15 and live(i + 1, base):
                            out_expand(i + 1, 0)
                        if s == 8 and live(i + 1, base):
                            out_sT(i + 1)
                        if s == 4 and live(i - 2, base):
                            round_x1(i - 2)
                        if s == 10 and live(i + 1, base):
                            out_qk(i + 1)
                        if s == 14 and live(i - 1, base):
                            out_attT(i - 1)
                        if s == 1 and live(i - 2, base):
                            seeds(i - 2, "ln1")
                        if live(bu, base):
                            relu(bu, cu)
                        if live(bs, base):
                            exp(bs, hs)
                        if s == 2 and live(i + 1, base):
                            seeds(i + 1, "prep")
                        if s == 8 and live(i - 3, base):
                            seeds(i - 3, "ln2")

                iterations(act, base, body)

            def retention():
                act.wait_ge(x_done, 3 * BATCH)

                def body(i):
                    for s in range(8):
                        be, ge = (i, s + 1) if s in (0, 1, 2) else (i + 1, 0)
                        if s == 1 and live(i + 1, 0):
                            act.wait_ge(rT_ps, i + 2)
                            wait(act, z_ps, i + 1)
                            act.activation(sT[:], bank[7][:, 0:SEQ], ACT.Copy).then_inc(rT_ready, 1)
                        if s == 2 and live(i - 2, 0):
                            act.wait_ge(yT_ps, i - 1)
                            wait(act, pr_ps, i - 2)
                            act.activation(yT, bank[7][:].rearrange("p (a t) -> p a t", a=2), ACT.Copy).then_inc(yT_ready, 1)
                        if s == 6 and live(i + 1, 0):
                            act.wait_ge(z_ps, i + 2)
                            wait(act, gz_ready, i + 1)
                            act.activation(tanh_z, bank[7][:].rearrange("p (t v) -> p t v", t=TT), ACT.Tanh, scale=0.5).then_inc(th_ready, 1)
                        if s in (0, 1, 2, 6) and live(be, 0):
                            act.wait_ge(rex_ps, be * 4 + ge + 1)
                            wait(act, rs_ps, (be - 1) * 8 + 2 * ge + 2)
                            act.activation(r_st[:, ge, :, :], bank[6][:].rearrange("p (a t) -> p a t", a=2), ACT.Copy).then_inc(rex_ready, 1)
                        if s == 2 and live(i - 1, 0):
                            act.wait_ge(ro_ps, (i - 1) * 8 + 8)
                            wait(act, on_ps, i - 1)
                            act.activation(outT[:, 1, :], bank[3][:, 0:SEQ], ACT.Copy).then_inc(oT_ready, 1)
                        if s == 6 and live(i, 0):
                            act.wait_ge(ro_ps, i * 8 + 4)
                            wait(act, on_ps, i)
                            act.activation(outT[:, 0, :], bank[2][:, 0:SEQ], ACT.Copy).then_inc(oT_ready, 1)
                        if s == 3 and live(i + 1, 0):
                            act.wait_ge(rv_ps, i + 2)
                            wait(act, vcopy, (i + 1) * 2)
                            act.activation(v_ret[:, 1, :, :], bank[7][:].rearrange("p (t v) -> p t v", t=TT), ACT.Copy).then_inc(rv_ready, 1)
                        if s == 4 and live(i - 1, 0):
                            act.wait_ge(on_ps, i)
                            wait(act, gn, (i - 2) * 15 + 1)
                            act.activation(sq, bank[4][:], ACT.Square).then_inc(sq_ready, 1)
                            wait(act, yr_ready, i - 1)
                            act.activation(nrm, bank[4][:].rearrange("p (t v) -> p t v", t=TT), ACT.Copy).then_inc(on_ready, 1)

                r_iterations(act, body)

            phase(0)
            retention()
            act.wait_ge(xr_done, BATCH)
            act.preload_act_table_set("natural_log_exp_and_others")
            phase(BATCH)

        @block.vector
        def _(dve):
            dve.memset(mx[:].bitcast(FP32), 0.0).then_inc(set_dve, 1)
            dve.memset(b2_r[:].bitcast(FP32), 0.0).then_inc(set_dve, 1)
            dve.memset(eps_col[:], LN_EPS).then_inc(set_dve, 1)
            dve.memset(ones_r[:].bitcast(FP32), 1.0).then_inc(set_dve, 1)
            dve.wait_ge(ld_c, N_LDC)
            dve.tensor_copy(sel_r[:].rearrange("p g k m -> p (g k m)"), stage[:, 0:2048])
            dve.tensor_copy(ident_r[:], ident[:]).then_inc(set_dve, 1)
            dve.wait_ge(ld_w, N_LDW)
            dve.wait_ge(ld_x, 16)

            def later_setup(part):
                if part == 0:
                    dve.wait_ge(ld_e, N_LDE)
                    dve.wait_ge(set_dve, 2)
                    dve.tensor_copy(b2_r[0:1, :, :], b2row)
                    dve.tensor_copy(w1_hi[:].rearrange("p c m -> p (c m)"), stage[:, 2048:4096]).then_inc(set_dve, 1)
                elif part == 1:
                    dve.wait_ge(set_dve, 6)
                    dve.tensor_tensor(b2_r[32:33, :, :], b2row, b2_r[0:1, :, :].bitcast(FP32), ALU.subtract).then_inc(set_dve, 1)
                    for n in range(2):
                        half = slice(n * CHUNKS // 2, (n + 1) * CHUNKS // 2)
                        last = dve.tensor_tensor(w1_lo[:, half, :], stage[:, 2048 + n * 1024:3072 + n * 1024].rearrange("p (c m) -> p c m", m=P),
                                                 w1_hi[:, half, :].bitcast(FP32), ALU.subtract)
                    last.then_inc(set_dve, 1)
                elif part == 2:
                    dve.memset(pw[:, 0:1], 1.0).then_inc(set_dve, 1)
                    dve.memset(prow[:, 0:P], 0.0).then_inc(set_dve, 1)
                    dve.wait_ge(ld_r, 7 * 16)
                    dve.tensor_copy(sel2_r[:].rearrange("p g k m -> p (g k m)"), dm_flat[:, 0:2048]).then_inc(set_dve, 1)
                elif part == 3:
                    for n in range(2):
                        dve.tensor_copy(wqk_sw[:].rearrange("p (c a) -> p c a", a=2)[:, :, n],
                                        wqkv[:, 0:256].rearrange("p (c a) -> p c a", a=2)[:, :, 1 - n]).then_inc(set_dve, 1)
                    dve.tensor_reduce(wv_mean[:], wv_heads, AX.X, ALU.add).then_inc(set_dve, 1)
                elif part == 4:
                    dve.wait_ge(set_dve, 14)
                    dve.tensor_scalar(wv_mean[:], wv_mean[:], -1.0 / RV, None, ALU.mult).then_inc(set_dve, 1)
                    dve.wait_ge(set_dve, 15)
                    dve.tensor_tensor(wv_cen[:].rearrange("p (h v) -> p h v", h=RH), wv_heads,
                                      wv_mean[:].unsqueeze(2).to_broadcast([P, RH, RV]), ALU.add).then_inc(set_dve, 1)
                    dve.tensor_scalar(wproj[:], wproj[:], 0.5, None, ALU.mult).then_inc(set_dve, 1)
                elif part < 13:
                    k = part - 5
                    w = 1 << k
                    dve.wait_ge(set_dve, 17 + 2 * k)
                    dve.tensor_scalar(pw[:, w:2 * w], pw[:, 0:w], dec[:, k:k + 1], None, ALU.mult).then_inc(set_dve, 1)
                    if k < 7:
                        dve.tensor_tensor(dec[:, k + 1:k + 2], dec[:, k:k + 1], dec[:, k:k + 1], ALU.mult).then_inc(set_dve, 1)
                else:
                    dve.wait_ge(set_dve, SET_DVE)
                    dve.tensor_scalar(prow[:, P:384], pw[:], RK ** -0.5, None, ALU.mult).then_inc(set_prow, 1)

            wv_heads = wqkv[:, 256:512].rearrange("p (h v) -> p h v", h=RH)
            LATER_PARTS = 14

            def layer_norm(b, which, src, dst):
                s, done = ln_scratch[which], ln_sem[which]
                for t in range(TT):
                    dve.bn_stats(s["six"][:, t, :], src(t)).then_inc(done, 1)

            def layer_norm_moments(b, which):
                s, done = ln_scratch[which], ln_sem[which]
                for t in range(TT):
                    dve.bn_aggr(s["mv"][:, t, :], s["six"][:, t, :]).then_inc(done, 1)

            def layer_norm_end(b, which, part, src=None, dst=None):
                s, done = ln_scratch[which], ln_sem[which]
                if part == 0:
                    dve.wait_ge(seed[which], b * 2 + 2)
                    dve.scalar_tensor_tensor(s["a"][:], s["mv"][:, :, 1], LN_EPS, s["seed"][:], ALU.add, ALU.mult).then_inc(done, 1)
                    return
                dve.wait_ge(done, b * 9 + 4 + part)
                if part == 1:
                    dve.scalar_tensor_tensor(s["c"][:], s["a"][:], -0.5, s["seed"][:], ALU.mult, ALU.mult).then_inc(done, 1)
                elif part == 2:
                    dve.scalar_tensor_tensor(s["rstd"][:], s["c"][:], 1.5, s["seed"][:], ALU.add, ALU.mult).then_inc(done, 1)
                else:
                    for t in range(TT):
                        dve.tensor_scalar(dst(t), src(t), s["mv"][:, t, 0:1], s["rstd"][:, t:t + 1], ALU.subtract, ALU.mult)\
                           .then_inc(done, 1)

            def split_qk(b):
                dve.wait_ge(hi_ready, b + 1)
                wait(dve, ex_ps, b * 4)
                dve.tensor_tensor(qk_lo[:], qk[:], qk_hi[:].bitcast(FP32), ALU.subtract).then_inc(lo_ready, 1)

            def out_v(b):
                dve.wait_ge(v_ps, b + 1)
                wait(dve, vb_ready, b * 2)
                wait(dve, va_ready, b * 2)
                dve.tensor_tensor(v_nat[:], misc[:, 0:SEQ].rearrange("p (t d) -> p t d", t=TT),
                                  bv_b.unsqueeze(1).to_broadcast([P, TT, P]), ALU.add).then_inc(v_ready, 1)

            def maximum(b, h):
                g, j = h // GH, h % GH
                dve.wait_ge(score_ps, b * NH + h + 1)
                dve.tensor_reduce(negmax[:, g % 2, :, j], score_bank[h % 2][:].rearrange("p (t k) -> p t k", t=TT),
                                  AX.X, ALU.max, negate=True).then_inc(max_done, 1)

            def split_max(b, g):
                dve.wait_ge(max_done, b * NH + 4 * g + 4)
                wait(dve, m_ps, b * 4 + g)
                rows = mx[:].rearrange("p t (j c) -> p t j c", c=32)
                hi, lo = rows[:, :, :, 3 * HD], rows[:, :, :, 3 * HD + 1]
                dve.tensor_copy(hi, negmax[:, g % 2, :, :]).then_inc(mx_ready, 1)
                dve.wait_ge(mx_ready, b * 8 + 2 * g + 1)
                dve.tensor_tensor(lo, negmax[:, g % 2, :, :], hi.bitcast(FP32), ALU.subtract).then_inc(mx_ready, 1)

            def shift_q(b, g):
                dve.wait_ge(m_ps, b * 4 + g + 1)
                wait(dve, prob_ps, (b - 1) * NH + 4 * g + 4)
                dve.tensor_tensor(q2_st[:, g, :], misc[:, 0:SEQ], q_st[:, g, :].bitcast(FP32), ALU.add).then_inc(q2_ready, 1)

            def normalize(b):
                dve.wait_ge(att_ps, b + 1)
                wait(dve, attT_ps, b)
                m = misc[:, 0:TT * GROUPS * (GH * HD + GH)].rearrange("p (n c) -> p n c", n=TT * GROUPS)
                dve.reciprocal(rsum[:], m[:, :, GH * HD:]).then_inc(att_ready, 1)
                dve.wait_ge(att_ready, b * 2 + 1)
                dve.tensor_tensor(att[:].rearrange("p t (g j d) -> p (t g) j d", g=GROUPS, j=GH),
                                  m[:, :, 0:GH * HD].rearrange("p n (j d) -> p n j d", j=GH),
                                  rsum[:].unsqueeze(3).to_broadcast([P, TT * GROUPS, GH, HD]), ALU.mult).then_inc(att_ready, 1)

            def add_attention(b, base):
                dve.wait_ge(wo_ps, b + 1)
                dve.wait_ge(resid_ready, b + 1)
                dve.tensor_tensor(y1[:], misc[:, 0:SEQ].rearrange("p (t d) -> p t d", t=TT),
                                  resid[:, at(b, base), :, :], ALU.add).then_inc(y1_ready, 1)
                dve.wait_ge(y1_ready, b + 1)

            def split_x1(b):
                dve.wait_ge(x1hi_ready, b + 1)
                wait(dve, up_ps, b * CHUNKS)
                dve.tensor_tensor(x1_lo[:], misc[:, 0:SEQ], x1_hi[:].bitcast(FP32), ALU.subtract).then_inc(x1lo_ready, 1)

            def route(b, base, n):
                if n == 0:
                    dve.wait_ge(x1_ready, b * 2 + 2)
                else:
                    dve.wait_ge(router, b * 8 + n)
                if n == 0:
                    step = dve.tensor_tensor(rprod[:], x1[:], rw_b.unsqueeze(1).to_broadcast([P, TT, P]), ALU.mult)
                elif n == 1:
                    step = dve.tensor_reduce(rkey[:, 0, :], rprod[:], AX.X, ALU.add)
                elif n == 2:
                    step = dve.tensor_scalar(rkey[:, 1, :], rkey[:, 0, :], rb_b[:], None, ALU.add)
                elif n == 3:
                    step = dve.tensor_copy(rint[:, 0, :], rkey[:, 1, :])
                elif n == 4:
                    step = dve.tensor_tensor(rint[:, 1, :], rint[:, 0, :], rkey[:, 1, :], ALU.is_gt)
                elif n == 5:
                    step = dve.tensor_tensor(rint[:, 2, :], rint[:, 0, :], rint[:, 1, :], ALU.subtract)
                elif n == 6:
                    step = dve.tensor_scalar(rint[:, 3, :], rint[:, 2, :], 3, None, ALU.bitwise_and)
                else:
                    step = dve.tensor_tensor(masks[:, at(b, base), :, :],
                                             rint[:, 3, :].unsqueeze(2).to_broadcast([P, TT, NE]), eidx[:], ALU.is_equal)
                step.then_inc(router, 1)

            def add_expert(b, e, base):
                dve.wait_ge(down_done, b * CHUNKS + 4 * e + 4)
                wait(dve, y_done, b * 8 + 2 * e)
                if e == 0:
                    dve.wait_ge(router, b * 8 + 8)
                    wait(dve, ln2, b * 9)
                for t in range(TT):
                    prior = x1 if e == 0 else acc
                    dve.scalar_tensor_tensor(acc[:, t, :], y_bank[:, t * P:(t + 1) * P], masks[:, at(b, base), t, e],
                                             prior[:, t, :], ALU.mult, ALU.add).then_inc(y_done, 1)

            def low_part(b, h):
                dve.wait_ge(exp_done, b * NH + h + 1)
                dve.tensor_tensor(p_lo[:, h % 4, :, :], probs[:, h % 4, :, :], p_hi[:, h % 4, :, :].bitcast(FP32),
                                  ALU.subtract).then_inc(plo_dve, 1)

            def phase(base):
                def body(i):
                    def x_tile(t):
                        return xs[:, at(i + 1, base), t, :]
                    if isinstance(i, int) and i == 1:
                        dve.wait_ge(ld_x, 32)
                    for s in range(SLOTS):
                        if isinstance(i, int) and i == 0 and 2 <= s < 2 + LATER_PARTS:
                            later_setup(s - 2)
                        if s == 0 and live(i - 1, base):
                            split_max(i - 1, 3)
                        if s in (4, 8, 12) and live(i, base):
                            split_max(i, s // 4 - 1)
                        if s == 1 and live(i - 1, base):
                            shift_q(i - 1, 3)
                        if s in (5, 9, 13) and live(i, base):
                            shift_q(i, s // 4 - 1)
                        if s == 2 and live(i, base):
                            out_v(i)
                        if s in (11, 15) and live(i - 2, base):
                            add_expert(i - 2, (s - 11) // 4, base)
                        if s in (3, 7) and live(i - 3, base):
                            add_expert(i - 3, (s + 5) // 4, base)
                        if s == 4 and live(i - 2, base):
                            split_x1(i - 2)
                        if s == 12 and live(i - 1, base):
                            normalize(i - 1)
                        if s == 0 and live(i - 2, base):
                            add_attention(i - 2, base)
                            layer_norm(i - 2, "ln1", lambda t: y1[:, t, :], None)
                            dve.wait_ge(ln1, (i - 2) * 9 + 2)
                        if s == 1 and live(i + 1, base):
                            wait(dve, sT_ps, i + 1)
                            wait(dve, resid_ready, i + 1)
                            layer_norm(i + 1, "prep", x_tile, None)
                            dve.wait_ge(prep_ln, (i + 1) * 9 + 2)
                        if s == 7 and live(i - 3, base):
                            dve.wait_ge(y_done, (i - 3) * 8 + 8)
                            layer_norm(i - 3, "ln2", lambda t: acc[:, t, :], None)
                            dve.wait_ge(ln2, (i - 3) * 9 + 2)
                        if s == 2 and live(i - 2, base):
                            layer_norm_end(i - 2, "ln1", 1)
                        if s in (5, 6) and live(i + 1, base):
                            layer_norm_end(i + 1, "prep", 2 * s - 10)
                        if s in (9, 10) and live(i - 3, base):
                            layer_norm_end(i - 3, "ln2", 2 * s - 18)
                        if s in (6, 7, 8, 9) and live(i - 2, base):
                            route(i - 2, base, 2 * s - 12)
                        if live(i, base):
                            maximum(i, s)
                        if s == 2 and live(i - 2, base):
                            layer_norm_end(i - 2, "ln1", 2)
                            wait(dve, x1_ready, (i - 2) * 2)
                            layer_norm_end(i - 2, "ln1", 3, lambda t: y1[:, t, :], lambda t: n1[:, t, :])
                        if s == 5 and live(i + 1, base):
                            layer_norm_end(i + 1, "prep", 1)
                        if s == 9 and live(i - 3, base):
                            layer_norm_end(i - 3, "ln2", 1)
                        if s in (6, 7, 8, 9) and live(i - 2, base):
                            route(i - 2, base, 2 * s - 11)
                        bl, hl = (i, s - 7) if s >= 7 else (i - 1, s + SLOTS - 7)
                        if hl in LOW_ON_DVE and live(bl, base):
                            low_part(bl, hl)
                        if s == 0 and live(i - 2, base):
                            layer_norm_moments(i - 2, "ln1")
                        if s == 1 and live(i + 1, base):
                            layer_norm_moments(i + 1, "prep")
                        if s == 7 and live(i - 3, base):
                            layer_norm_moments(i - 3, "ln2")
                        if s == 1 and live(i - 2, base):
                            layer_norm_end(i - 2, "ln1", 0)
                        if s == 6 and live(i + 1, base):
                            layer_norm_end(i + 1, "prep", 3, x_tile, lambda t: s_nat[:, t, :])
                        if s == 10 and live(i - 3, base):
                            wait(dve, x_done, (i - 3) * 3)
                            layer_norm_end(i - 3, "ln2", 3, lambda t: acc[:, t, :], lambda t: n2[:, t, :])
                        if s == 13 and live(i + 1, base):
                            split_qk(i + 1)

                iterations(dve, base, body)

            def retention():
                dve.wait_ge(x_done, 3 * BATCH)
                dve.wait_ge(ld_d, 32)

                def rsqrt(which, b, k):
                    s = rs[which]
                    done, start, src, scale, eps = {"rln": (rln, b * 18 + 4, mv_r[:, :, 1], 1.0, LN_EPS),
                                                    "gn": (gn, b * 15 + 1, ssq[:], 1.0 / RV, GN_EPS)}[which]
                    y = s["y"][:].bitcast(FP32)
                    dve.wait_ge(done, start + k)
                    if k == 0:
                        step = dve.tensor_scalar(s["v"][:], src, scale, eps, ALU.mult, ALU.add)
                    elif k == 1:
                        step = dve.tensor_scalar(s["i"][:], s["v"][:].bitcast(INT32), 1, None, ALU.logical_shift_right)
                    elif k == 2:
                        step = dve.tensor_scalar(s["y"][:], s["i"][:], -1.0, float(MAGIC), ALU.mult, ALU.add)
                    elif k % 3 == 0:
                        step = dve.scalar_tensor_tensor(s["a"][:], s["v"][:], -0.5, y, ALU.mult, ALU.mult)
                    elif k % 3 == 1:
                        step = dve.tensor_tensor(s["c"][:], s["a"][:], y, ALU.mult)
                    else:
                        step = dve.scalar_tensor_tensor(y, s["c"][:], 1.5, y, ALU.add, ALU.mult)
                    step.then_inc(done, 1)

                def mask_scores(b, h):
                    dve.wait_ge(rs_ps, b * 8 + h + 1)
                    wait(dve, ro_ps, b * 8 + h - 3)
                    dve.tensor_tensor(ret[:, h % 4, :], bank[h % 2][:, 0:384], dm[:, h, :], ALU.mult).then_inc(ret_ready, 1)

                def normalized(b, t):
                    dve.wait_ge(rln, b * 18 + 16)
                    if t == 0:
                        wait(dve, rT_ps, b)
                    dve.tensor_scalar(s_nat[:, t, :], xs[:, at(b, 0), t, :], mv_r[:, t, 0:1],
                                      rs["rln"]["y"][:, t:t + 1].bitcast(FP32), ALU.subtract, ALU.mult).then_inc(rln, 1)

                def rotate(b, n):
                    if n == 0:
                        dve.wait_ge(rqk_ps, b + 1)
                        wait(dve, rqk_ready, b)
                    dve.tensor_tensor((rot_a, rot_b)[n], bank[4 + n][:].rearrange("p (a t) -> p a t", a=2),
                                      (cosT, sinT)[n][:], ALU.mult).then_inc(rot_ready, 1)

                def gate(b):
                    dve.wait_ge(th_ready, b + 1)
                    dve.scalar_tensor_tensor(wide_buf[:, at(b, 0), :, :], tanh_z, 1.0, bank[7][:].rearrange("p (t v) -> p t v", t=TT),
                                             ALU.add, ALU.mult).then_inc(gz_ready, 1)

                def sum_squares(b):
                    dve.wait_ge(sq_ready, b + 1)
                    wait(dve, gn, b * 15)
                    dve.tensor_reduce(ssq[:], sq.rearrange("p (n v) -> p n v", v=RV), AX.X, ALU.add).then_inc(gn, 1)

                def group_normalized(b):
                    dve.wait_ge(gn, b * 15 + 13)
                    dve.wait_ge(on_ready, b + 1)
                    for t in range(TT):
                        heads = nrm[:, t, :].rearrange("p (n v) -> p n v", v=RV)
                        dve.tensor_tensor(heads, heads,
                                          rs["gn"]["y"][:, 8 * t:8 * t + 8].bitcast(FP32).unsqueeze(2).to_broadcast([P, 8, RV]),
                                          ALU.mult).then_inc(gn, 1)

                def add_output(b):
                    dve.wait_ge(pr_ps, b + 1)
                    xb = xs[:, at(b, 0), :, :]
                    dve.tensor_tensor(xb, bank[7][:, 0:SEQ].rearrange("p (a t d) -> p a t d", a=1, t=TT), xb, ALU.add).then_inc(xr_done, 1)

                LN_BEFORE, LN_AFTER = {1: 0, 2: 2, 3: 6, 4: 8, 5: 10}, {1: 1, 2: 3, 3: 7, 4: 9, 5: 11}
                GN_BEFORE, GN_AFTER = {5: 2, 6: 5, 7: 8}, {4: 1, 5: 3, 6: 6, 7: 9}

                def body(i):
                    for s in range(8):
                        if s == 0 and live(i + 2, 0):
                            for t in range(TT):
                                dve.bn_stats(six_r[:, t, :], xs[:, at(i + 2, 0), t, :]).then_inc(rln, 1)
                            dve.wait_ge(rln, (i + 2) * 18 + 2)
                        if s == 7 and live(i + 1, 0):
                            gate(i + 1)
                        if s in LN_BEFORE and live(i + 2, 0):
                            rsqrt("rln", i + 2, LN_BEFORE[s])
                        if s in GN_BEFORE and live(i - 1, 0):
                            rsqrt("gn", i - 1, GN_BEFORE[s])
                        if live(i, 0):
                            mask_scores(i, s)
                        if s == 0 and live(i + 2, 0):
                            for t in range(TT):
                                dve.bn_aggr(mv_r[:, t, :], six_r[:, t, :]).then_inc(rln, 1)
                        if s == 4 and live(i - 1, 0):
                            sum_squares(i - 1)
                        if s == 4 and live(i - 2, 0):
                            add_output(i - 2)
                        if s == 4 and live(i - 1, 0):
                            rsqrt("gn", i - 1, 0)
                        if s in LN_AFTER and live(i + 2, 0):
                            rsqrt("rln", i + 2, LN_AFTER[s])
                        if s == 6 and live(i + 2, 0):
                            normalized(i + 2, 0)
                        if s in GN_AFTER and live(i - 1, 0):
                            rsqrt("gn", i - 1, GN_AFTER[s])
                        if s == 6 and live(i + 2, 0):
                            normalized(i + 2, 1)
                        if s in (5, 6, 7) and live(i - 1, 0):
                            rsqrt("gn", i - 1, GN_AFTER[s] + 1)
                        if s == 2:
                            for n in range(2):
                                if live(i + 1, 0):
                                    rotate(i + 1, n)
                                if live(i + 2, 0):
                                    rsqrt("rln", i + 2, 4 + n)
                        if s == 7 and live(i - 1, 0):
                            rsqrt("gn", i - 1, 11)
                            group_normalized(i - 1)

                r_iterations(dve, body)

            phase(0)
            retention()
            dve.wait_ge(xr_done, BATCH)
            phase(BATCH)

        @block.gpsimd
        def _(pool):
            pool.memset(ones_wide[:], 1.0)
            pool.memset(v_st[:].rearrange("p t n -> p (t n)").bitcast(FP32), 0.0).then_inc(set_pool, 1)
            pool.wait_ge(set_pool, 1)
            blocks = v_st[:].rearrange("p t (h c) -> p t h c", h=NH)
            for t in range(TT):
                last = pool.memset(blocks[:, t, :, 2 * HD:3 * HD].bitcast(FP32), 1.0)
            last.then_inc(set_pool, 1)
            pool.wait_ge(ld_w, N_LDW)
            pool.tensor_scalar(vecs[:, 4 * P:6 * P], vecs[:, 4 * P:6 * P], 0.5, 0.0, ALU.mult, ALU.add).then_inc(set_pool, 1)
            pool.wait_ge(set_pool, 3)

            def wide(v):
                return v.unsqueeze(1).to_broadcast([P, TT, P])

            def round_wide(dst, src):
                width = src.shape[-1]
                pool.tensor_tensor(dst[:, :, 0:1], src[:, :, 0:1], ones_wide[:, 0:2, 0:1], ALU.mult)
                return pool.tensor_scalar(dst[:, :, 1:width], src[:, :, 1:width], 1.0, 0.0, ALU.mult, ALU.add)

            def add_bo(b, base):
                pool.wait_ge(prep_ln, b * 9 + 9)
                pool.tensor_tensor(resid[:, at(b, base), :, :], s_nat[:], wide(bo_b), ALU.add).then_inc(resid_ready, 1)

            def round_qk(b):
                pool.wait_ge(qk_ready, b * 2 + 2)
                wait(pool, ex_ps, b * 4)
                round_wide(qk_hi, qk[:]).then_inc(hi_ready, 1)

            def place_v(b, half):
                if half == 0:
                    pool.wait_ge(v_ready, b + 1)
                wait(pool, pv_done, (b - 1) * NH + 8 + 8 * half)
                done = (va_ready, vb_ready)[half]
                heads = slice(8 * half, 8 * half + 8)
                src = v_nat[:, :, 64 * half:64 * half + 64].rearrange("p t (h d) -> p t h d", h=8)
                hi, lo = blocks[:, :, heads, 0:HD], blocks[:, :, heads, HD:2 * HD]
                pool.tensor_tensor(hi, src, ones_wide[:].unsqueeze(1).to_broadcast([P, TT, 8, HD]), ALU.mult).then_inc(done, 1)
                pool.wait_ge(done, b * 2 + 1)
                pool.tensor_tensor(lo, src, hi.bitcast(FP32), ALU.subtract).then_inc(done, 1)

            def low_part(b, h):
                pool.wait_ge(exp_done, b * NH + h + 1)
                pool.tensor_tensor(p_lo[:, h % 4, :, :], probs[:, h % 4, :, :], p_hi[:, h % 4, :, :].bitcast(FP32),
                                   ALU.subtract).then_inc(plo_pool, 1)

            def make_x1(b):
                pool.wait_ge(ln1, b * 9 + 9)
                wait(pool, x1_ready, b * 2)
                pool.tensor_tensor(xt1[:], n1[:], wide(g1_b), ALU.mult).then_inc(x1_ready, 1)
                pool.wait_ge(x1_ready, b * 2 + 1)
                wait(pool, x1T_ps, b)
                wait(pool, router, b * 8)
                wait(pool, y_done, (b - 1) * 8 + 2)
                pool.tensor_tensor(x1[:], xt1[:], wide(b1_b), ALU.add).then_inc(x1_ready, 1)

            def make_x(b, base):
                pool.wait_ge(ln2, b * 9 + 9)
                pool.tensor_tensor(xt2[:, 0], n2[:], wide(g2_b), ALU.mult).then_inc(x_done, 1)
                pool.wait_ge(x_done, b * 3 + 1)
                pool.tensor_tensor(xt2[:, 1], xt2[:, 0], wide(b2_b), ALU.add).then_inc(x_done, 1)
                pool.wait_ge(x_done, b * 3 + 2)
                xb = xs[:, at(b, base), :, :]
                pool.tensor_tensor(xb, xb, xt2[:, 1], ALU.add).then_inc(x_done, 1)

            def phase(base):
                def body(i):
                    for s in range(SLOTS):
                        bl, hl = (i, s - 7) if s >= 7 else (i - 1, s + SLOTS - 7)
                        if hl in LOW_ON_POOL and live(bl, base):
                            low_part(bl, hl)
                        if s == 3 and live(i, base):
                            place_v(i, 0)
                        if s == 2 and live(i - 2, base):
                            make_x1(i - 2)
                        if s == 6 and live(i + 1, base):
                            add_bo(i + 1, base)
                        if s == 8 and live(i, base):
                            place_v(i, 1)
                        if s == 11 and live(i + 1, base):
                            round_qk(i + 1)
                        if s == 14 and live(i - 3, base):
                            make_x(i - 3, base)

                iterations(pool, base, body)

            def retention():
                pool.wait_ge(x_done, 3 * BATCH)

                def use_values(half):
                    cols = slice(half * P, (half + 1) * P)
                    round_wide(v_ret[:, 0, :, cols], v_ret[:, 1, :, cols]).then_inc(vcopy, 1)

                def body(i):
                    if live(i - 2, 0):
                        b = i - 2
                        pool.wait_ge(gn, b * 15 + 15)
                        pool.wait_ge(gz_ready, b + 1)
                        wait(pool, yT_ps, b)
                        pool.tensor_tensor(y_ret, nrm, wide_buf[:, at(b, 0), :, :], ALU.mult).then_inc(yr_ready, 1)
                    if live(i, 0):
                        wait(pool, ro_ps, i * 8)
                        use_values(1)
                    if live(i + 1, 0):
                        b = i + 1
                        pool.wait_ge(rot_ready, b * 2 + 2)
                        wait(pool, rhi_ready, b)
                        wait(pool, rlo_ready, b)
                        pool.tensor_tensor(qk[:], rot_a, rot_b, ALU.add).then_inc(rqk_ready, 1)
                        pool.wait_ge(rqk_ready, b + 1)
                        wait(pool, rex_ps, b * 4)
                        round_wide(qk_hi, qk[:]).then_inc(rhi_ready, 1)
                        pool.wait_ge(rhi_ready, b + 1)
                        pool.tensor_tensor(qk_lo[:], qk[:], qk_hi[:].bitcast(FP32), ALU.subtract).then_inc(rlo_ready, 1)
                        pool.wait_ge(rv_ready, b + 1)
                        wait(pool, ro_ps, i * 8 + 4)
                        use_values(0)

                r_iterations(pool, body)

            phase(0)
            retention()
            pool.wait_ge(xr_done, BATCH)
            phase(BATCH)




INPUTS = {
    "L0_attn_hidden_states": "x", "L0_attn_W_qkv": "W_qkv", "L0_attn_W_g": "W_g", "L0_attn_W_proj": "W_proj",
    "L0_attn_decay": "decay", "L0_ffn_Wq": "Wq", "L0_ffn_bq": "bq", "L0_ffn_Wk": "Wk", "L0_ffn_bk": "bk",
    "L0_ffn_Wv": "Wv", "L0_ffn_bv": "bv", "L0_ffn_Wo": "Wo", "L0_ffn_bo": "bo", "L0_ffn_router_w": "router_w",
    "L0_ffn_router_b": "router_b", "L0_ffn_W1": "W1", "L0_ffn_b1": "b1", "L0_ffn_W2": "W2", "L0_ffn_b2": "b2",
    "L0_ffn_ln1_g": "ln1_g", "L0_ffn_ln1_b": "ln1_b", "L0_ffn_ln2_g": "ln2_g", "L0_ffn_ln2_b": "ln2_b",
}


def kernel(**inputs):
    import concourse.bacc as bacc
    from concourse.bass_utils import run_bass_kernel_spmd

    nc = bacc.Bacc("TRN2", target_bir_lowering=False, num_devices=1)
    arrays, aps = {}, {}
    given = {short: np.ascontiguousarray(inputs[name]) for name, short in INPUTS.items()}
    for name, a in {**packed(given), **constants()}.items():
        arrays[f"in_{name}"] = a
        aps[name] = nc.dram_tensor(f"in_{name}", a.shape, mybir.dt.from_np(a.dtype), kind="ExternalInput").ap()
    aps["out"] = nc.dram_tensor("out", (BATCH, SEQ, DM), FP32, kind="ExternalOutput").ap()
    build(nc, aps)
    r = run_bass_kernel_spmd(nc, [arrays], core_ids=[0])
    return r.results[0]["out"]
```
